# Optimizing a Trainium2 kernel written in Bass

```python
import numpy as np
import jax
import jax.numpy as jnp

def _softmax(x, axis=-1):
    return jax.nn.softmax(x, axis=axis)

def _gelu(x):
    return jax.nn.gelu(x, approximate=True)

def _silu(x):
    return jax.nn.silu(x)

def _sigmoid(x):
    return jax.nn.sigmoid(x)

def _layernorm(x, axis=-1, eps=1e-05):
    m = jnp.mean(x, axis=axis, keepdims=True)
    v = jnp.var(x, axis=axis, keepdims=True)
    return (x - m) / jnp.sqrt(v + eps)

def _scatter_add(tgt, idx, src, axis=0):
    return tgt.at[idx].add(src)

def _segment_sum(src, seg, n):
    return jax.ops.segment_sum(src, seg, n)
kernel_name = 'mk_gnn_resnorm_d4_gnn_r32_bab2e6'

def setup_inputs(seed: int=0):
    np.random.seed(seed)
    _w = jnp.asarray

    def _rec_inputs():
        import jax
        import jax.numpy as jnp
        _gk = jax.random.key(seed)
        x = -0.000202 + 1 * jax.random.normal(jax.random.fold_in(_gk, 1), (50000, 128), jnp.float32)
        src = jax.random.randint(jax.random.fold_in(_gk, 2), (25000,), 0, 50000, jnp.int32)
        dst = jnp.minimum((50000 * jax.random.uniform(jax.random.fold_in(_gk, 3), (25000,)) ** 2.0).astype(jnp.int32), 49999)
        _o = jnp.argsort(dst, stable=True)
        src = src[_o]
        dst = dst[_o]
        edge_attr_128 = 2.93046e-05 + 1.00006 * jax.random.normal(jax.random.fold_in(_gk, 11), (25000, 128), jnp.float32)
        edge_type_3 = jax.random.randint(jax.random.fold_in(_gk, 13), (25000,), 0, 3, jnp.int32)
        return (x, src, dst, edge_attr_128, edge_type_3)
    x, src, dst, edge_attr_128, edge_type_3 = _rec_inputs()

    def _L0_gnn_setup():
        import jax, jax.numpy as jnp
        import numpy as np
        N_NODES = 50000
        N_EDGES = 25000
        IN_DIM = 128
        OUT_DIM = 128
        NUM_HEADS = 8
        HEAD_DIM = OUT_DIM // NUM_HEADS
        LN_EPS = 1e-05
        key = jax.random.key(seed)
        ks = jax.random.split(key, 8)

        def xavier(k, shape, fan_in, fan_out):
            a = float(np.sqrt(6.0 / (fan_in + fan_out)))
            return jax.random.uniform(k, shape, jnp.float32, -a, a)
        x = jax.random.normal(ks[0], (N_NODES, IN_DIM), jnp.float32)
        edge_index = jax.random.randint(ks[1], (2, N_EDGES), 0, N_NODES, jnp.int32)
        W_src = xavier(ks[2], (IN_DIM, OUT_DIM), IN_DIM, OUT_DIM)
        W_dst = xavier(ks[3], (IN_DIM, OUT_DIM), IN_DIM, OUT_DIM)
        attn = xavier(ks[4], (NUM_HEADS, HEAD_DIM), HEAD_DIM, NUM_HEADS)
        W_out = xavier(ks[5], (OUT_DIM, OUT_DIM), OUT_DIM, OUT_DIM)
        b_out = jnp.zeros((OUT_DIM,), jnp.float32)
        gamma = jnp.ones((OUT_DIM,), jnp.float32)
        beta = jnp.zeros((OUT_DIM,), jnp.float32)
        return {'x': x, 'edge_index': edge_index, 'W_src': W_src, 'W_dst': W_dst, 'attn': attn, 'W_out': W_out, 'b_out': b_out, 'gamma': gamma, 'beta': beta}
    _L0_gnn_all = _L0_gnn_setup()
    _L0_gnn_in = {k: v for k, v in _L0_gnn_all.items() if k in ('W_src', 'W_dst', 'attn', 'W_out', 'b_out', 'gamma', 'beta')}
    del _L0_gnn_all

    def _L1_gnn_setup():
        import jax, jax.numpy as jnp
        import numpy as np
        N_NODES = 10000
        D = 128
        N_EDGES = 20000
        key = jax.random.key(seed)
        ks = jax.random.split(key, 14)
        x = jax.random.normal(ks[0], (N_NODES, D), dtype=jnp.float32)
        edge_index = jax.random.randint(ks[1], (2, N_EDGES), 0, N_NODES, dtype=jnp.int64)
        edge_attr = jax.random.normal(ks[2], (N_EDGES, D), dtype=jnp.float32)
        s = 1.0 / np.sqrt(D)

        def lin(kw, kb):
            W = jax.random.uniform(kw, (D, D), dtype=jnp.float32, minval=-s, maxval=s)
            b = jax.random.uniform(kb, (D,), dtype=jnp.float32, minval=-s, maxval=s)
            return (W, b)
        WA, bA = lin(ks[3], ks[4])
        WB, bB = lin(ks[5], ks[6])
        WC, bC = lin(ks[7], ks[8])
        WE, bE = lin(ks[9], ks[10])
        Wres, bres = lin(ks[11], ks[12])
        return {'x': x, 'edge_index': edge_index, 'edge_attr': edge_attr, 'WA': WA, 'bA': bA, 'WB': WB, 'bB': bB, 'WC': WC, 'bC': bC, 'WE': WE, 'bE': bE, 'Wres': Wres, 'bres': bres}
    _L1_gnn_all = _L1_gnn_setup()
    _L1_gnn_in = {k: v for k, v in _L1_gnn_all.items() if k in ('WA', 'bA', 'WB', 'bB', 'WC', 'bC', 'WE', 'bE', 'Wres', 'bres')}
    del _L1_gnn_all

    def _L2_gnn_setup():
        import jax, jax.numpy as jnp
        import numpy as np
        import math
        N = 50000
        E = 25000
        HID = 128
        HEADS = 8
        DK = HID // HEADS
        EPS_LN = 1e-05

        def _layer_norm(x, g, b):
            mu = jnp.mean(x, axis=-1, keepdims=True)
            var = jnp.mean(jnp.square(x - mu), axis=-1, keepdims=True)
            return (x - mu) * jax.lax.rsqrt(var + EPS_LN) * g + b
        key = jax.random.key(seed)
        ks = jax.random.split(key, 20)
        s = 1.0 / math.sqrt(HID)
        inp = {'x': jax.random.normal(ks[0], (N, HID), jnp.float32), 'Wq': jax.random.normal(ks[1], (HID, HID), jnp.float32) * s, 'bq': jnp.zeros((HID,), jnp.float32), 'Wk': jax.random.normal(ks[2], (HID, HID), jnp.float32) * s, 'bk': jnp.zeros((HID,), jnp.float32), 'Wv': jax.random.normal(ks[3], (HID, HID), jnp.float32) * s, 'bv': jnp.zeros((HID,), jnp.float32), 'Wo': jax.random.normal(ks[4], (HID, HID), jnp.float32) * s, 'bo': jnp.zeros((HID,), jnp.float32), 'ln1_g': jnp.ones((HID,), jnp.float32), 'ln1_b': jnp.zeros((HID,), jnp.float32), 'W1': jax.random.normal(ks[5], (HID, 4 * HID), jnp.float32) * s, 'b1': jnp.zeros((4 * HID,), jnp.float32), 'W2': jax.random.normal(ks[6], (4 * HID, HID), jnp.float32) * (0.5 * s), 'b2': jnp.zeros((HID,), jnp.float32), 'ln2_g': jnp.ones((HID,), jnp.float32), 'ln2_b': jnp.zeros((HID,), jnp.float32), 'edge_index': jax.random.randint(ks[7], (2, E), 0, N, jnp.int64 if jax.config.jax_enable_x64 else jnp.int32)}
        return inp
    _L2_gnn_all = _L2_gnn_setup()
    _L2_gnn_in = {k: v for k, v in _L2_gnn_all.items() if k in ('Wq', 'bq', 'Wk', 'bk', 'Wv', 'bv', 'Wo', 'bo', 'ln1_g', 'ln1_b', 'W1', 'b1', 'W2', 'b2', 'ln2_g', 'ln2_b')}
    del _L2_gnn_all

    def _L3_gnn_setup():
        import jax, jax.numpy as jnp
        import numpy as np
        N_NODES = 50000
        N_EDGES = 50000
        IN_DIM = 128
        HEADS = 4
        HEAD_DIM = 32
        N_REL = 3
        NEG_SLOPE = 0.2
        key = jax.random.key(seed)
        ks = jax.random.split(key, 8)
        x = jax.random.normal(ks[0], (N_NODES, IN_DIM), dtype=jnp.float32)
        edge_index = jax.random.randint(ks[1], (2, N_EDGES), 0, N_NODES, dtype=jnp.int64)
        edge_type = jax.random.randint(ks[2], (N_EDGES,), 0, N_REL, dtype=jnp.int64)
        s = 1.0 / np.sqrt(IN_DIM)
        W = jax.random.normal(ks[3], (N_REL, IN_DIM, HEADS * HEAD_DIM), dtype=jnp.float32) * s
        att_src = jax.random.normal(ks[4], (N_REL, HEADS, HEAD_DIM), dtype=jnp.float32) * s
        att_dst = jax.random.normal(ks[5], (N_REL, HEADS, HEAD_DIM), dtype=jnp.float32) * s
        bias = jnp.zeros((N_REL, HEADS * HEAD_DIM), dtype=jnp.float32)
        rel_w = jnp.ones((N_REL,), dtype=jnp.float32)
        return {'x': x, 'W': W, 'att_src': att_src, 'att_dst': att_dst, 'bias': bias, 'rel_w': rel_w, 'edge_index': edge_index, 'edge_type': edge_type}
    _L3_gnn_all = _L3_gnn_setup()
    _L3_gnn_in = {k: v for k, v in _L3_gnn_all.items() if k in ('W', 'att_src', 'att_dst', 'bias', 'rel_w')}
    del _L3_gnn_all
    return {'x': x, 'src': src, 'dst': dst, 'edge_attr_128': edge_attr_128, 'edge_type_3': edge_type_3, 'L0_gnn_W_src': _L0_gnn_in['W_src'], 'L0_gnn_W_dst': _L0_gnn_in['W_dst'], 'L0_gnn_attn': _L0_gnn_in['attn'], 'L0_gnn_W_out': _L0_gnn_in['W_out'], 'L0_gnn_b_out': _L0_gnn_in['b_out'], 'L0_gnn_gamma': _L0_gnn_in['gamma'], 'L0_gnn_beta': _L0_gnn_in['beta'], 'L1_gnn_WA': _L1_gnn_in['WA'], 'L1_gnn_bA': _L1_gnn_in['bA'], 'L1_gnn_WB': _L1_gnn_in['WB'], 'L1_gnn_bB': _L1_gnn_in['bB'], 'L1_gnn_WC': _L1_gnn_in['WC'], 'L1_gnn_bC': _L1_gnn_in['bC'], 'L1_gnn_WE': _L1_gnn_in['WE'], 'L1_gnn_bE': _L1_gnn_in['bE'], 'L1_gnn_Wres': _L1_gnn_in['Wres'], 'L1_gnn_bres': _L1_gnn_in['bres'], 'L2_gnn_Wq': _L2_gnn_in['Wq'], 'L2_gnn_bq': _L2_gnn_in['bq'], 'L2_gnn_Wk': _L2_gnn_in['Wk'], 'L2_gnn_bk': _L2_gnn_in['bk'], 'L2_gnn_Wv': _L2_gnn_in['Wv'], 'L2_gnn_bv': _L2_gnn_in['bv'], 'L2_gnn_Wo': _L2_gnn_in['Wo'], 'L2_gnn_bo': _L2_gnn_in['bo'], 'L2_gnn_ln1_g': _L2_gnn_in['ln1_g'], 'L2_gnn_ln1_b': _L2_gnn_in['ln1_b'], 'L2_gnn_W1': _L2_gnn_in['W1'], 'L2_gnn_b1': _L2_gnn_in['b1'], 'L2_gnn_W2': _L2_gnn_in['W2'], 'L2_gnn_b2': _L2_gnn_in['b2'], 'L2_gnn_ln2_g': _L2_gnn_in['ln2_g'], 'L2_gnn_ln2_b': _L2_gnn_in['ln2_b'], 'L3_gnn_W': _L3_gnn_in['W'], 'L3_gnn_att_src': _L3_gnn_in['att_src'], 'L3_gnn_att_dst': _L3_gnn_in['att_dst'], 'L3_gnn_bias': _L3_gnn_in['bias'], 'L3_gnn_rel_w': _L3_gnn_in['rel_w']}

def reference(x, src, dst, edge_attr_128, edge_type_3, L0_gnn_W_src, L0_gnn_W_dst, L0_gnn_attn, L0_gnn_W_out, L0_gnn_b_out, L0_gnn_gamma, L0_gnn_beta, L1_gnn_WA, L1_gnn_bA, L1_gnn_WB, L1_gnn_bB, L1_gnn_WC, L1_gnn_bC, L1_gnn_WE, L1_gnn_bE, L1_gnn_Wres, L1_gnn_bres, L2_gnn_Wq, L2_gnn_bq, L2_gnn_Wk, L2_gnn_bk, L2_gnn_Wv, L2_gnn_bv, L2_gnn_Wo, L2_gnn_bo, L2_gnn_ln1_g, L2_gnn_ln1_b, L2_gnn_W1, L2_gnn_b1, L2_gnn_W2, L2_gnn_b2, L2_gnn_ln2_g, L2_gnn_ln2_b, L3_gnn_W, L3_gnn_att_src, L3_gnn_att_dst, L3_gnn_bias, L3_gnn_rel_w):
    import jax
    import jax.numpy as jnp

    def _L0_gnn_ref(x, edge_index, W_src, W_dst, attn, W_out, b_out, gamma, beta):
        import jax, jax.numpy as jnp
        import numpy as np
        N_NODES = 50000
        N_EDGES = 25000
        IN_DIM = 128
        OUT_DIM = 128
        NUM_HEADS = 8
        HEAD_DIM = OUT_DIM // NUM_HEADS
        LN_EPS = 1e-05
        N = x.shape[0]
        H, D = attn.shape
        src, dst = (edge_index[0], edge_index[1])
        h_src = (x @ W_src).reshape(N, H, D)
        h_dst = (x @ W_dst).reshape(N, H, D)
        h_src_e = h_src[src]
        e = jax.nn.leaky_relu(h_src_e + h_dst[dst], 0.2)
        s = jnp.einsum('ehd,hd->eh', e, attn)
        m = jax.ops.segment_max(s, dst, num_segments=N)
        exp = jnp.exp(s - m[dst])
        denom = jax.ops.segment_sum(exp, dst, num_segments=N)
        alpha = exp / (denom[dst] + 1e-08)
        msg = (h_src_e * alpha[..., None]).reshape(-1, H * D)
        out = jax.ops.segment_sum(msg, dst, num_segments=N)
        out = out @ W_out + b_out
        out = out + x
        mu = jnp.mean(out, axis=-1, keepdims=True)
        var = jnp.var(out, axis=-1, keepdims=True)
        out = (out - mu) * jax.lax.rsqrt(var + LN_EPS) * gamma + beta
        return out

    def _L1_gnn_ref(x, edge_index, edge_attr, WA, bA, WB, bB, WC, bC, WE, bE, Wres, bres):
        import jax, jax.numpy as jnp
        import numpy as np
        N_NODES = 10000
        D = 128
        N_EDGES = 20000
        row, col = (edge_index[0], edge_index[1])
        Bx = x @ WB + bB
        Cx = x @ WC + bC
        Ax = x @ WA + bA
        m = Bx[row] + Cx[col] + (edge_attr @ WE + bE)
        m = jax.nn.sigmoid(m) * Ax[row]
        agg = jax.ops.segment_sum(m, col, num_segments=x.shape[0])
        return jax.nn.relu(agg + (x @ Wres + bres))

    def _L2_gnn_ref(x, Wq, bq, Wk, bk, Wv, bv, Wo, bo, ln1_g, ln1_b, W1, b1, W2, b2, ln2_g, ln2_b, edge_index):
        import jax, jax.numpy as jnp
        import numpy as np
        import math
        N = 50000
        E = 25000
        HID = 128
        HEADS = 8
        DK = HID // HEADS
        EPS_LN = 1e-05

        def _layer_norm(x, g, b):
            mu = jnp.mean(x, axis=-1, keepdims=True)
            var = jnp.mean(jnp.square(x - mu), axis=-1, keepdims=True)
            return (x - mu) * jax.lax.rsqrt(var + EPS_LN) * g + b
        n = x.shape[0]
        src, tgt = (edge_index[0], edge_index[1])
        Q = (x @ Wq + bq).reshape(n, HEADS, DK)
        K = (x @ Wk + bk).reshape(n, HEADS, DK)
        V = (x @ Wv + bv).reshape(n, HEADS, DK)
        scores = jnp.sum(Q[tgt] * K[src], axis=-1) / math.sqrt(DK)
        smax = jax.ops.segment_max(scores, tgt, num_segments=n)
        sexp = jnp.exp(scores - smax[tgt])
        ssum = jax.ops.segment_sum(sexp, tgt, num_segments=n)
        alpha = sexp / (ssum[tgt] + 1e-16)
        messages = alpha[:, :, None] * V[src]
        agg = jax.ops.segment_sum(messages, tgt, num_segments=n).reshape(n, HID)
        out = agg @ Wo + bo
        h = _layer_norm(x + out, ln1_g, ln1_b)
        ff = jax.nn.relu(h @ W1 + b1) @ W2 + b2
        return _layer_norm(h + ff, ln2_g, ln2_b)

    def _L3_gnn_ref(x, W, att_src, att_dst, bias, rel_w, edge_index, edge_type):
        import jax, jax.numpy as jnp
        import numpy as np
        N_NODES = 50000
        N_EDGES = 50000
        IN_DIM = 128
        HEADS = 4
        HEAD_DIM = 32
        N_REL = 3
        NEG_SLOPE = 0.2
        N = x.shape[0]
        NEG = jnp.float32(-1000000000.0)
        self_idx = jnp.arange(N, dtype=edge_index.dtype)
        src = jnp.concatenate([edge_index[0], self_idx])
        dst = jnp.concatenate([edge_index[1], self_idx])
        weights = jax.nn.softmax(rel_w)
        out = jnp.zeros((N, HEADS * HEAD_DIM), dtype=x.dtype)
        for r in range(N_REL):
            h = (x @ W[r]).reshape(N, HEADS, HEAD_DIM)
            a_s = jnp.einsum('nhc,hc->nh', h, att_src[r])
            a_d = jnp.einsum('nhc,hc->nh', h, att_dst[r])
            score = jax.nn.leaky_relu(a_s[src] + a_d[dst], NEG_SLOPE)
            mask = jnp.concatenate([edge_type == r, jnp.ones((N,), dtype=bool)])
            score = jnp.where(mask[:, None], score, NEG)
            smax = jax.ops.segment_max(score, dst, num_segments=N)
            ex = jnp.exp(score - smax[dst])
            denom = jax.ops.segment_sum(ex, dst, num_segments=N)
            alpha = ex / denom[dst]
            msg = alpha[:, :, None] * h[src]
            rel_out = jax.ops.segment_sum(msg, dst, num_segments=N).reshape(N, HEADS * HEAD_DIM)
            out = out + weights[r] * (rel_out + bias[r])
        return out
    edge_index = jnp.stack([src, dst])
    x = _layernorm(x + _L0_gnn_ref(x, edge_index, L0_gnn_W_src, L0_gnn_W_dst, L0_gnn_attn, L0_gnn_W_out, L0_gnn_b_out, L0_gnn_gamma, L0_gnn_beta), axis=-1)
    x = _layernorm(x + _L1_gnn_ref(x, edge_index, edge_attr_128, L1_gnn_WA, L1_gnn_bA, L1_gnn_WB, L1_gnn_bB, L1_gnn_WC, L1_gnn_bC, L1_gnn_WE, L1_gnn_bE, L1_gnn_Wres, L1_gnn_bres), axis=-1)
    x = _layernorm(x + _L2_gnn_ref(x, L2_gnn_Wq, L2_gnn_bq, L2_gnn_Wk, L2_gnn_bk, L2_gnn_Wv, L2_gnn_bv, L2_gnn_Wo, L2_gnn_bo, L2_gnn_ln1_g, L2_gnn_ln1_b, L2_gnn_W1, L2_gnn_b1, L2_gnn_W2, L2_gnn_b2, L2_gnn_ln2_g, L2_gnn_ln2_b, edge_index), axis=-1)
    x = _layernorm(x + _L3_gnn_ref(x, L3_gnn_W, L3_gnn_att_src, L3_gnn_att_dst, L3_gnn_bias, L3_gnn_rel_w, edge_index, edge_type_3), axis=-1)
    return x

_drawn_inputs = setup_inputs


def setup_inputs(seed=0):
    import zlib

    import numpy as np

    out = dict(_drawn_inputs(seed))
    spreads = {'L0_gnn_b_out': (0.0, 0.1),
     'L0_gnn_gamma': (1.0, 0.2),
     'L0_gnn_beta': (0.0, 0.1),
     'L2_gnn_bq': (0.0, 0.8),
     'L2_gnn_bk': (0.0, 2.0),
     'L2_gnn_bv': (0.0, 0.359),
     'L2_gnn_bo': (0.0, 0.1),
     'L2_gnn_ln1_g': (1.0, 0.2),
     'L2_gnn_ln1_b': (0.0, 0.1),
     'L2_gnn_b1': (0.0, 0.284),
     'L2_gnn_b2': (0.0, 0.1),
     'L2_gnn_ln2_g': (1.0, 0.2),
     'L2_gnn_ln2_b': (0.0, 0.1),
     'L3_gnn_bias': (0.0, 0.1),
     'L3_gnn_rel_w': (1.0, 0.2)}
    factors = {'L0_gnn_W_dst': 10.099,
     'L1_gnn_bA': 3.213,
     'L1_gnn_bB': 8.0,
     'L1_gnn_bC': 8.0,
     'L1_gnn_bE': 8.0,
     'L3_gnn_att_dst': 17.789}
    for name, (base, spread) in spreads.items():
        noise = np.random.default_rng([zlib.crc32(name.encode()), seed]).standard_normal(out[name].shape)
        drawn = base * np.exp(spread * noise) if base else spread * noise
        out[name] = jnp.asarray(drawn.astype(out[name].dtype))
    for name, factor in factors.items():
        out[name] = (out[name] * factor).astype(out[name].dtype)
    return out
```

```python
import numpy as np
import concourse.bass as bass
import concourse.mybir as mybir
from contextlib import ExitStack

F32 = mybir.dt.float32
I32 = mybir.dt.int32
ALU = mybir.AluOpType
ACT = mybir.ActivationFunctionType
AX = mybir.AxisListType

N_NODES, N_EDGES, D = 50000, 25000, 128
P = 125
T = N_EDGES // P
NT = N_NODES // P
G = 4
ESTEPS, NSTEPS = T // G, NT // G
ER = 2
BIG = 1.0e30
NEG = 1.0e9
EPS_LN = 1e-5
SKIP = 100000.0
SPLIT = 112
W3 = D + 12


class Step:

    def __init__(self, i, q, unroll):
        self.i, self.q, self.unroll = i, q, unroll
        self.j = i * unroll + q
        self.peeled = isinstance(i, int)

    def slot(self, ring):
        return self.q % ring

    def visits(self, ring):
        return self.i * (self.unroll // ring) + self.q // ring

    def has(self, back):
        return not self.peeled or self.j >= back

    def ready(self, eng, sem, per=1):
        eng.wait_ge(sem, (self.j + 1) * per)

    def freed(self, eng, sem, ring, per=1):
        if self.has(ring):
            eng.wait_ge(sem, (self.j - (ring - 1)) * per)

    def arrived(self, eng, sems, per):
        eng.wait_ge(sems[self.slot(len(sems))], (self.visits(len(sems)) + 1) * per)

    def sent(self, eng, sems, per):
        ring = len(sems)
        if self.has(ring):
            eng.wait_ge(sems[self.slot(ring)], self.visits(ring) * per)


def pipeline(eng, total, unroll, stages):
    most = max(lag for lag, _ in stages)
    warm = unroll * (1 + -(-most // unroll))

    def peeled(t):
        for lag, fn in stages:
            if 0 <= t - lag < total:
                fn(Step((t - lag) // unroll, (t - lag) % unroll, unroll))

    for t in range(warm):
        peeled(t)
    with eng.Fori(warm // unroll, total // unroll) as i:
        for r in range(unroll):
            for lag, fn in stages:
                back = (lag - r + unroll - 1) // unroll if lag > r else 0
                fn(Step(i - back if back else i, r - lag + back * unroll, unroll))
    for t in range(total, total + most):
        peeled(t)


def over_tiles(row, n=G):
    return row.unsqueeze(1).to_broadcast([row.shape[0], n, row.shape[1]])


def load_rows(eng, dst, src, sem):
    eng.dma_start(dst[0:SPLIT], src[0:SPLIT]).then_inc(sem, 16)
    eng.dma_start(dst[SPLIT:P], src[SPLIT:P]).then_inc(sem, 16)


def rows_of(v, n):
    return v.rearrange("(a c) -> a c", a=1).to_broadcast([n, v.shape[0]])


class Chain:

    def __init__(self, eng, sem):
        self.eng, self.sem, self.n = eng, sem, 0

    def __call__(self, *instructions):
        for i in instructions:
            i.then_inc(self.sem, 1)
        self.n += len(instructions)
        self.eng.wait_ge(self.sem, self.n)


class Builder:

    def __init__(self, nc, args, out, top):
        self.nc, self.a, self.out, self.top = nc, args, out, top
        self.used = []
        x_after = [nc.dram_tensor(f"x_after_{l}", (N_NODES, D), F32).ap() for l in range(3)]
        self.x = [args["x"], *x_after, out]
        self.agg = nc.dram_tensor("agg", (N_NODES, D), F32).ap()
        self.agg3 = nc.dram_tensor("agg3", (N_NODES, W3), F32).ap()
        sb = lambda name, shape, dt=F32: self.sb(top, name, shape, dt)
        self.ident = sb("ident", [128, 128])
        self.ones = sb("ones", [P, P])
        self.e0 = sb("e0", [128, P])
        self.eps = sb("eps", [128, 1])
        self.src_i = sb("src_i", [P, T], I32)
        self.dst_i = sb("dst_i", [P, T], I32)
        self.put_i = sb("put_i", [P, T], I32)
        self.fix_i = sb("fix_i", [P, 1], I32)
        self.same_prev = sb("same_prev", [P, T])
        self.same_next = sb("same_next", [P, T])
        self.in_row = sb("in_row", [P, T])
        self.pen_prev = sb("pen_prev", [P, T])
        self.pen_next = sb("pen_next", [P, T])
        self.carry_f = sb("carry_f", [P, P])
        self.carry_b = sb("carry_b", [P, P])
        self.pen_cf = sb("pen_cf", [P, P])
        self.pen_cb = sb("pen_cb", [P, P])

    def sem(self, name):
        handle = self.nc.alloc_semaphore(name)
        self.used.append(handle)
        return handle

    def recycle(self):
        self.nc.clear_and_free_semaphores(self.used)
        self.nc.all_engine_barrier()
        self.used = []

    def sb(self, ctx, name, shape, dt=F32):
        return ctx.enter_context(self.nc.sbuf_tensor(name, shape, dt))

    def ps(self, ctx, name, shape):
        return ctx.enter_context(self.nc.psum_tensor(name, shape, F32))

    def graph(self):
        nc, a, sem = self.nc, self.a, self.sem
        ident, ones, e0, eps = self.ident, self.ones, self.e0, self.eps
        carry_f, carry_b = self.carry_f, self.carry_b
        same_prev, same_next, in_row = self.same_prev, self.same_next, self.in_row
        Z, Z3 = 16, 8
        with ExitStack() as ctx:
            sb = lambda name, shape, dt=F32: self.sb(ctx, name, shape, dt)
            dpad = sb("dpad", [P, T + 2], I32)
            df = sb("df", [P, T + 2])
            last = sb("last", [P, T])
            put_f = sb("put_f", [P, T])
            diag = sb("diag", [P, P])
            fix = sb("fix", [P, 4])
            zero = sb("zero", [P, Z, D])
            zero3 = sb("zero3", [P, Z3, W3])
            ps_first = self.ps(ctx, "ps_first", [P, P])
            ps_tr = self.ps(ctx, "ps_tr", [P, P])
            frame, consts, loaded, fills, filled = (sem("g_" + n) for n in ("frame", "consts", "loaded", "fills", "filled"))
            own, diag_done, first_done = sem("g_own"), sem("g_diag"), sem("g_first")
            equal, upper, turned = sem("g_equal"), sem("g_upper"), sem("g_turned")
            block = ctx.enter_context(nc.Block())

            @block.gpsimd
            def _(pool):
                nc.gpsimd.memset(dpad[:], -1).then_inc(frame, 1)
                nc.gpsimd.memset(ident[:], 0.0).then_inc(consts, 1)
                nc.gpsimd.memset(e0[:], 0.0).then_inc(consts, 1)
                nc.gpsimd.memset(ones[:], 1.0).then_inc(consts, 1)
                nc.gpsimd.memset(eps[:], EPS_LN).then_inc(consts, 1)
                pool.wait_ge(consts, 4)
                nc.gpsimd.affine_select(out=ident[:], in_=ident[:], compare_op=ALU.not_equal, fill=1.0, base=0,
                                        pattern=[[-1, 128]], channel_multiplier=1).then_inc(consts, 1)
                nc.gpsimd.affine_select(out=e0[:], in_=e0[:], compare_op=ALU.not_equal, fill=1.0, base=0,
                                        pattern=[[0, P]], channel_multiplier=1).then_inc(consts, 1)
                pool.wait_ge(equal, 1)
                nc.gpsimd.affine_select(out=carry_f[:], in_=carry_f[:], compare_op=ALU.is_gt, fill=0.0, base=0,
                                        pattern=[[1, P]], channel_multiplier=-1).then_inc(upper, 1)

            @block.sync
            def _(sp):
                rows = a["dst"].rearrange("(p t) -> p t", p=P)
                sp.dma_start(self.src_i[:], a["src"].rearrange("(p t) -> p t", p=P)).then_inc(loaded, 16)
                sp.dma_start(self.dst_i[:], rows).then_inc(loaded, 16)
                sp.wait_ge(frame, 1)
                sp.dma_start(dpad[:, 1:T + 1], rows).then_inc(loaded, 16)
                with nc.allow_non_contiguous_dma(reason="one index of each row"):
                    sp.dma_start(dpad[1:P, 0:1], rows[0:P - 1, T - 1:T]).then_inc(loaded, 16)
                    sp.dma_start(dpad[0:P - 1, T + 1:T + 2], rows[1:P, 0:1]).then_inc(loaded, 16)
                sp.wait_ge(fills, 3)
                agg = self.agg.rearrange("(p n) d -> p n d", p=P)
                agg3 = self.agg3.rearrange("(p n) d -> p n d", p=P)
                with sp.Fori(0, NT // Z) as i:
                    load_rows(sp, agg[:, bass.ds(i * Z, Z), :], zero[:], filled)
                with sp.Fori(0, NT // Z3) as i:
                    load_rows(sp, agg3[:, bass.ds(i * Z3, Z3), :], zero3[:], filled)
                sp.wait_ge(filled, 32 * (NT // Z + NT // Z3))
                sp.wait_ge(loaded, 80)

            @block.vector
            def _(dve):
                V, ch = nc.vector, Chain(dve, own)
                V.memset(zero[:], 0.0).then_inc(fills, 1)
                V.memset(zero3[:, :, 0:D], 0.0).then_inc(fills, 1)
                V.memset(zero3[:, :, D:W3], 1.0).then_inc(fills, 1)
                dve.wait_ge(loaded, 80)
                ch(V.tensor_copy(df[:], dpad[:]))
                mine, prev, nxt = df[:, 1:T + 1], df[:, 0:T], df[:, 2:T + 2]
                ch(V.tensor_tensor(same_prev[:], mine, prev, ALU.is_equal),
                   V.tensor_tensor(same_next[:], mine, nxt, ALU.is_equal),
                   V.tensor_tensor(last[:], mine, nxt, ALU.not_equal))
                ch(V.tensor_copy(in_row[:], same_prev[:]),
                   V.tensor_scalar(self.pen_prev[:], same_prev[:], -1.0, BIG, ALU.add, ALU.mult),
                   V.tensor_scalar(self.pen_next[:], same_next[:], -1.0, BIG, ALU.add, ALU.mult),
                   V.tensor_scalar(put_f[:], last[:], -1.0, -SKIP, ALU.add, ALU.mult))
                ch(V.memset(in_row[:, 0:1], 0.0),
                   V.tensor_tensor(put_f[:], put_f[:], mine, ALU.add))
                ch(V.tensor_copy(self.put_i[:], put_f[:]),
                   V.tensor_tensor(fix[:, 0:1], df[:, 1:2], df[:, T + 1:T + 2], ALU.not_equal))
                ch(V.tensor_tensor(fix[:, 1:2], fix[:, 0:1], same_prev[:, 0:1], ALU.mult))
                ch(V.tensor_scalar(fix[:, 2:3], fix[:, 1:2], -1.0, -SKIP, ALU.add, ALU.mult))
                ch(V.tensor_tensor(fix[:, 3:4], fix[:, 2:3], df[:, 1:2], ALU.add))
                ch(V.tensor_copy(self.fix_i[:], fix[:, 3:4]))
                dve.wait_ge(consts, 6)
                V.tensor_scalar(diag[:], ident[0:P, 0:P], df[:, 1:2], None, ALU.mult).then_inc(diag_done, 1)
                dve.wait_ge(first_done, 1)
                V.tensor_scalar(carry_f[:], ps_first[:], df[:, T:T + 1], None, ALU.is_equal).then_inc(equal, 1)
                dve.wait_ge(upper, 1)
                dve.wait_ge(turned, 1)
                ch(V.tensor_copy(carry_b[:], ps_tr[:]))
                ch(V.tensor_scalar(self.pen_cf[:], carry_b[:], -1.0, BIG, ALU.add, ALU.mult),
                   V.tensor_scalar(self.pen_cb[:], carry_f[:], -1.0, BIG, ALU.add, ALU.mult))

            @block.tensor
            def _(pe):
                pe.wait_ge(consts, 6)
                pe.wait_ge(diag_done, 1)
                nc.tensor.matmul(ps_first[:], ones[:], diag[:], start=True, stop=True).then_inc(first_done, 1)
                pe.wait_ge(upper, 1)
                nc.tensor.transpose(ps_tr[:], carry_f[:], ident[0:P, 0:P]).then_inc(turned, 1)

    def running_sum(self, dve, st, ro, msg, msg_slot, put, summed):
        slot = st.slot(ER)
        st.sent(dve, put, 16 * G)
        for k in range(G):
            before = ro[:, slot, k - 1, 0:D] if k else ro[:, (slot - 1) % ER, G - 1, 0:D]
            if k or st.has(1):
                dve.wait_ge(summed, st.j * G + k)
            self.nc.vector.scalar_tensor_tensor(
                out=ro[:, slot, k, 0:D], in0=before, scalar=self.in_row[:, bass.ds(st.j * G + k, 1)],
                in1=msg[:, msg_slot, k, :], op0=ALU.mult, op1=ALU.add).then_inc(summed, 1)

    def scatter(self, pool, st, cols, ro, dst, put, copied, go, waits):
        slot = st.slot(ER)
        if st.has(ER):
            st.sent(pool, put, 16 * G)
            pool.sem_inc(go, 1)
        self.nc.gpsimd.tensor_copy(cols[:, slot], self.put_i[:, bass.ds(st.j * G, G)]).then_inc(copied, 1)
        st.ready(pool, copied)
        pool.sem_inc(go, 1)
        for s, per in waits:
            st.ready(pool, s, per)
            pool.sem_inc(go, 1)
        for k in range(G):
            self.nc.gpsimd.indirect_dma_start(
                dst, bass.IndirectOffsetOnAxis(cols[:, slot, k:k + 1], 0), ro[:, slot, k, :], None,
                bounds_check=N_NODES - 1, oob_is_err=False).then_inc(put[slot], 16)

    def carry_fix(self, l, ro, dst, width):
        nc = self.nc
        with ExitStack() as ctx:
            rows = self.sb(ctx, f"c{l}_rows", [P, width])
            ps_c = self.ps(ctx, f"c{l}_ps", [P, D])
            blank, got, summed, fixed, back = (self.sem(f"c{l}_" + n) for n in ("blank", "got", "summed", "fixed", "back"))
            block = ctx.enter_context(nc.Block())

            @block.tensor
            def _(pe):
                nc.tensor.matmul(ps_c[:], self.carry_f[:], ro[:, ER - 1, G - 1, 0:D], start=True, stop=True).then_inc(summed, 1)

            @block.gpsimd
            def _(pool):
                nc.gpsimd.memset(rows[:], 0.0).then_inc(blank, 1)
                pool.wait_ge(blank, 1)
                nc.gpsimd.indirect_dma_start(rows[:], None, dst, bass.IndirectOffsetOnAxis(self.fix_i[:, 0:1], 0),
                                             bounds_check=N_NODES - 1, oob_is_err=False).then_inc(got, 16)
                pool.wait_ge(fixed, 1)
                nc.gpsimd.indirect_dma_start(dst, bass.IndirectOffsetOnAxis(self.fix_i[:, 0:1], 0), rows[:], None,
                                             bounds_check=N_NODES - 1, oob_is_err=False).then_inc(back, 16)
                pool.wait_ge(back, 16)

            @block.vector
            def _(dve):
                dve.wait_ge(got, 16)
                dve.wait_ge(summed, 1)
                nc.vector.tensor_tensor(rows[:, 0:D], rows[:, 0:D], ps_c[:], ALU.add).then_inc(fixed, 1)

    def edge_pass(self, l, ctx, keep=None, S=None, SS=None, mk=None, w3s=None, wself=None, rel_w=None):
        nc, a, sem = self.nc, self.a, self.sem
        x_in, ident, pre = self.x[l], self.ident, f"e{l}_"
        sb = lambda c, name, shape, dt=F32: self.sb(c, pre + name, shape, dt)
        cols = {0: 256, 1: 256, 2: 384, 3: 408}[l]
        hold = 2 if cols <= 256 else 1
        nv = {0: 0, 1: 2, 2: 4, 3: 12}[l]
        with ExitStack() as c2:
            xs, xd = sb(c2, "xs", [P, ER, G, D]), sb(c2, "xd", [P, ER, G, D])
            ixs, ixd = sb(c2, "ixs", [P, ER, G], I32), sb(c2, "ixd", [P, ER, G], I32)
            xsT, xdT = sb(c2, "xsT", [128, ER, G, P]), sb(c2, "xdT", [128, ER, G, P])
            ws, wd = sb(c2, "ws", [D, cols]), sb(c2, "wd", [D, D])
            brow = sb(c2, "brow", [128, cols])
            t1, t2 = sb(c2, "t1", [P, ER, G, D]), sb(c2, "t2", [P, ER, G, D])
            ps_s, ps_d = self.ps(c2, pre + "ps_s", [128, G, 128]), self.ps(c2, pre + "ps_d", [128, G, 128])
            ps_h = [self.ps(c2, pre + f"ps_h{k}", [128, 512]) for k in range(4)]
            weights, weights_done, own = sem(pre + "weights"), sem(pre + "weights_done"), sem(pre + "own")
            copied, go = sem(pre + "copied"), sem(pre + "go")
            got = [sem(pre + f"got{k}") for k in range(ER)]
            tr_s, tr_d, ev_s, ev_d = (sem(pre + n) for n in ("tr_s", "tr_d", "ev_s", "ev_d"))
            prod, act_done, vec_done, reduced = (sem(pre + n) for n in ("prod", "act", "vec", "reduced"))
            if l == 1:
                ea, eaT = sb(c2, "ea", [P, ER, G, D]), sb(c2, "eaT", [128, ER, G, P])
                we, b3 = sb(c2, "we", [D, D]), sb(c2, "b3", [128, 3, D])
                ps_e = self.ps(c2, pre + "ps_e", [128, G, 128])
                got_e = [sem(pre + f"got_e{k}") for k in range(ER)]
                tr_e, ev_e, summed, pcopied = sem(pre + "tr_e"), sem(pre + "ev_e"), sem(pre + "summed"), sem(pre + "pcopied")
                put = [sem(pre + f"put{k}") for k in range(ER)]
                pcols = sb(c2, "pcols", [P, ER, G], I32)
                ro = sb(c2, "ro", [P, ER, G, D])
            if l == 0:
                attn_row = sb(c2, "attn", [P, D])
                vec_done0 = sem(pre + "vec0")
            if l == 3:
                w3, pr3 = sb(c2, "w3", [D, 3, D]), sb(c2, "pr3", [D, 3 * D])
                att_s, att_d = sb(c2, "att_s", [D, 3 * D]), sb(c2, "att_d", [D, 3 * D])
                rel = sb(c2, "rel", [D, 12])
                exped, neg_max = sem(pre + "exped"), sem(pre + "neg_max")

            def bank(st, k):
                if hold == 2:
                    return ps_h[2 * st.slot(2) + k // 2][0:P, 256 * (k % 2):256 * (k % 2) + cols]
                return ps_h[k][0:P, 0:cols]

            def units(st):
                if hold == 2:
                    return [(2 * h, 2, ps_h[2 * st.slot(2) + h][0:P, :].rearrange("p (k c) -> p k c", k=2)) for h in range(2)]
                return [(k, 1, ps_h[k][0:P, :].rearrange("p (k c) -> p k c", k=1)) for k in range(G)]

            W = {0: [(ws[:, 0:D], a["L0_gnn_W_src"]), (ws[:, D:2 * D], a["L0_gnn_W_src"]), (wd[:], a["L0_gnn_W_dst"])],
                 1: [(ws[:, 0:D], a["L1_gnn_WB"]), (ws[:, D:2 * D], a["L1_gnn_WA"]), (wd[:], a["L1_gnn_WC"])],
                 2: [(ws[:, 0:D], a["L2_gnn_Wk"]), (ws[:, D:2 * D], a["L2_gnn_Wv"]), (wd[:], a["L2_gnn_Wq"])],
                 3: []}[l]
            if l == 0:
                W += [(attn_row[:], rows_of(a["L0_gnn_attn"].rearrange("h d -> (h d)"), P))]
            if l == 1:
                W += [(we[:], a["L1_gnn_WE"]), (brow[:, D:2 * D], rows_of(a["L1_gnn_bA"], 128))]
                W += [(b3[:, k, :], rows_of(a["L1_gnn_b" + n], 128)) for k, n in enumerate("BCE")]
            if l == 2:
                W += [(brow[:, k * D:k * D + D], rows_of(a["L2_gnn_b" + n], 128)) for k, n in enumerate("kvq")]
            if l == 3:
                W += [(w3[:], a["L3_gnn_W"].rearrange("r i o -> i r o")), (rel[:, 0:3], rows_of(a["L3_gnn_rel_w"], D)),
                      (att_s[:], rows_of(a["L3_gnn_att_src"].rearrange("r h c -> (r h c)"), D)),
                      (att_d[:], rows_of(a["L3_gnn_att_dst"].rearrange("r h c -> (r h c)"), D))]
            with ExitStack() as c3:
                block = c3.enter_context(nc.Block())

                @block.sync
                def _(sp):
                    for to, of in W:
                        sp.dma_start(to, of).then_inc(weights, 16)
                    if l == 1:
                        ea_v = a["edge_attr_128"].rearrange("(p t) d -> p t d", p=P)

                        def load(st):
                            st.freed(sp, tr_e, ER)
                            load_rows(sp, ea[:, st.slot(ER)], ea_v[:, bass.ds(st.j * G, G), :], got_e[st.slot(ER)])

                        pipeline(sp, ESTEPS, ER, [(0, load)])

                @block.gpsimd
                def _(pool):
                    def gather(st):
                        slot = st.slot(ER)
                        if st.has(ER):
                            st.sent(pool, got, 32 * G)
                            pool.sem_inc(go, 1)
                            st.freed(pool, tr_s, ER)
                            pool.sem_inc(go, 1)
                            st.freed(pool, tr_d, ER)
                            pool.sem_inc(go, 1)
                        nc.gpsimd.tensor_copy(ixs[:, slot], self.src_i[:, bass.ds(st.j * G, G)]).then_inc(copied, 1)
                        nc.gpsimd.tensor_copy(ixd[:, slot], self.dst_i[:, bass.ds(st.j * G, G)]).then_inc(copied, 1)
                        st.ready(pool, copied, 2)
                        pool.sem_inc(go, 1)
                        for k in range(G):
                            for rows, ix in ((xs, ixs), (xd, ixd)):
                                nc.gpsimd.indirect_dma_start(
                                    rows[:, slot, k, :], None, x_in,
                                    bass.IndirectOffsetOnAxis(ix[:, slot, k:k + 1], 0)).then_inc(got[slot], 16)

                    stages = [(0, gather)]
                    if l == 1:
                        stages.append((2, lambda st: self.scatter(pool, st, pcols, ro, self.agg, put, pcopied, go, [(summed, G)])))
                    pipeline(pool, ESTEPS, ER, stages)
                    if l == 1:
                        for k in range(ER):
                            pool.wait_ge(put[k], 16 * G * (ESTEPS // ER))

                @block.tensor
                def _(pe):
                    kw = dict(skip_group_check=True)

                    def transposes(st):
                        slot = st.slot(ER)
                        st.arrived(pe, got, 32 * G)
                        st.freed(pe, ev_s, 1)
                        for k in range(G):
                            i = nc.tensor.transpose(ps_s[:, k, 0:P], xs[:, slot, k, :], ident[0:P, 0:P])
                        i.then_inc(tr_s, 1)
                        st.freed(pe, ev_d, 1)
                        for k in range(G):
                            i = nc.tensor.transpose(ps_d[:, k, 0:P], xd[:, slot, k, :], ident[0:P, 0:P])
                        i.then_inc(tr_d, 1)
                        if l == 1:
                            st.arrived(pe, got_e, 32)
                            st.freed(pe, ev_e, 1)
                            for k in range(G):
                                i = nc.tensor.transpose(ps_e[:, k, 0:P], ea[:, slot, k, :], ident[0:P, 0:P])
                            i.then_inc(tr_e, 1)

                    def products(st):
                        slot, mm = st.slot(ER), nc.tensor.matmul
                        st.ready(pe, ev_s)
                        st.ready(pe, ev_d)
                        if l == 1:
                            st.ready(pe, ev_e)
                        if l == 0:
                            st.freed(pe, act_done, hold)
                        else:
                            st.freed(pe, vec_done, hold, nv)
                        for k in range(G):
                            o, src_t, dst_t = bank(st, k), xsT[:, slot, k, :], xdT[:, slot, k, :]
                            if l == 0:
                                mm(o[:, 0:2 * D], src_t, ws[:], start=True, stop=False, **kw)
                                i = mm(o[:, D:2 * D], dst_t, wd[:], start=False, stop=True, **kw)
                            if l == 1:
                                mm(o[:, 0:2 * D], self.e0[:], brow[:], start=True, stop=False, **kw)
                                mm(o[:, 0:2 * D], src_t, ws[:], start=False, stop=False, **kw)
                                mm(o[:, 0:D], dst_t, wd[:], start=False, stop=False, **kw)
                                i = mm(o[:, 0:D], eaT[:, slot, k, :], we[:], start=False, stop=True, **kw)
                            if l == 2:
                                mm(o[:, 0:3 * D], self.e0[:], brow[:], start=True, stop=False, **kw)
                                mm(o[:, 0:2 * D], src_t, ws[:, 0:2 * D], start=False, stop=False, **kw)
                                i = mm(o[:, 2 * D:3 * D], dst_t, wd[:], start=False, stop=True, **kw)
                            if l == 3:
                                mm(o[:, 0:408], src_t, ws[:], start=True, stop=False, **kw)
                                i = mm(o[:, 384:408], dst_t, wd[:, 0:24], start=False, stop=True, **kw)
                        i.then_inc(prod, 1)

                    pe.wait_ge(weights, 16 * len(W))
                    pe.wait_ge(weights_done, 1)
                    pipeline(pe, ESTEPS, ER, [(0, transposes), (1, products)])

                @block.scalar
                def _(act):
                    A = nc.scalar
                    if l == 3:
                        act.wait_ge(neg_max, 1)
                        A.activation(rel[:, 4:7], rel[:, 0:3], ACT.Exp, bias=rel[:, 3:4]).then_inc(exped, 1)

                    def evac(st):
                        st.freed(act, prod, ER)
                        st.ready(act, tr_s)
                        A.copy(xsT[:, st.slot(ER)], ps_s[:, :, 0:P]).then_inc(ev_s, 1)
                        if l == 1:
                            st.ready(act, tr_e)
                            A.copy(eaT[:, st.slot(ER)], ps_e[:, :, 0:P]).then_inc(ev_e, 1)

                    def use(st):
                        slot = st.slot(ER)
                        st.ready(act, prod)
                        if l == 0:
                            st.freed(act, vec_done0, ER, 2)
                        if l in (1, 2):
                            st.freed(act, vec_done, ER, nv)
                        for k, m, h in units(st):
                            tiles = bass.ds(st.j * G + k, m)
                            if l == 0:
                                A.activation(keep[:, tiles, :], h[:, :, 0:D], ACT.Copy)
                                i = A.activation(t1[:, slot, k:k + m, :], h[:, :, D:2 * D], ACT.Copy)
                            if l == 1:
                                i = A.activation(t1[:, slot, k:k + m, :], h[:, :, 0:D], ACT.Sigmoid)
                            if l == 2:
                                A.activation(keep[:, tiles, :], h[:, :, D:2 * D], ACT.Copy)
                                i = A.activation(t1[:, slot, k:k + m, :], h[:, :, 2 * D:3 * D], ACT.Copy)
                            if l == 3:
                                A.activation(S[:, tiles, :], h[:, :, 384:396], ACT.Copy)
                                i = A.activation(SS[:, tiles, :], h[:, :, 396:408], ACT.Copy)
                        i.then_inc(act_done, 1)

                    pipeline(act, ESTEPS, ER, [(0, evac), (1, use)])

                @block.vector
                def _(dve):
                    V, ch = nc.vector, Chain(dve, own)
                    dve.wait_ge(weights, 16 * len(W))
                    if l == 1:
                        ch(V.tensor_tensor(b3[:, 0, :], b3[:, 0, :], b3[:, 1, :], ALU.add))
                        ch(V.tensor_tensor(brow[:, 0:D], b3[:, 0, :], b3[:, 2, :], ALU.add),
                           V.memset(ro[:, ER - 1, G - 1, :], 0.0))
                    if l == 3:
                        w3f, heads = w3[:].rearrange("i r o -> i (r o)"), lambda t: t[:].rearrange("i (q c) -> i q c", c=32)
                        V.tensor_reduce(rel[:, 3:4], rel[:, 0:3], AX.X, ALU.max, negate=True).then_inc(neg_max, 1)
                        ch(V.tensor_tensor(pr3[:], w3f, att_s[:], ALU.mult))
                        ch(V.tensor_reduce(ws[:, 384:396], heads(pr3), AX.X, ALU.add))
                        ch(V.tensor_tensor(pr3[:], w3f, att_d[:], ALU.mult))
                        dve.wait_ge(exped, 1)
                        ch(V.tensor_reduce(wd[:, 0:12], heads(pr3), AX.X, ALU.add),
                           V.tensor_reduce(rel[:, 7:8], rel[:, 4:7], AX.X, ALU.add),
                           V.memset(ws[:, 396:408], 0.0))
                        ch(V.tensor_tensor(wd[:, 12:24], wd[:, 0:12], ws[:, 384:396], ALU.add),
                           V.reciprocal(rel[:, 8:9], rel[:, 7:8]))
                        ch(V.tensor_scalar(rel_w[:], rel[:, 4:7], rel[:, 8:9], None, ALU.mult))
                        ch(*[V.tensor_scalar(ws[:, D * r:D * r + D], w3[:, r, :], rel_w[:, r:r + 1], None, ALU.mult)
                             for r in range(3)])
                        ch(V.tensor_copy(w3s[:], ws[:, 0:3 * D]))
                    V.memset(t2[:, 0, 0, 0:1], 0.0).then_inc(weights_done, 1)
                    dve.wait_ge(weights_done, 1)

                    def evac(st):
                        st.freed(dve, prod, ER)
                        st.ready(dve, tr_d)
                        V.tensor_copy(xdT[:, st.slot(ER)], ps_d[:, :, 0:P]).then_inc(ev_d, 1)

                    def heads16(st):
                        V.tensor_reduce(S[:, bass.ds(st.j * G, G), :], t2[:, st.slot(ER)].rearrange("p k (h c) -> p k h c", c=16),
                                        AX.X, ALU.add).then_inc(reduced, 1)

                    def use0(st):
                        st.ready(dve, act_done)
                        st.freed(dve, reduced, ER)
                        slot = st.slot(ER)
                        V.scalar_tensor_tensor(out=t2[:, slot], in0=t1[:, slot], scalar=0.2, in1=t1[:, slot],
                                               op0=ALU.mult, op1=ALU.max).then_inc(vec_done0, 1)
                        dve.wait_ge(vec_done0, st.j * 2 + 1)
                        V.tensor_tensor(t2[:, slot], t2[:, slot], over_tiles(attn_row[:]), ALU.mult).then_inc(vec_done0, 1)
                        st.ready(dve, vec_done0, 2)
                        heads16(st)

                    def use1(st):
                        slot = st.slot(ER)
                        st.ready(dve, act_done)
                        st.freed(dve, summed, ER, G)
                        for k, m, h in units(st):
                            V.tensor_tensor(t2[:, slot, k:k + m, :], h[:, :, D:2 * D], t1[:, slot, k:k + m, :], ALU.mult).then_inc(vec_done, 1)
                        st.ready(dve, vec_done, nv)
                        self.running_sum(dve, st, ro, t2, slot, put, summed)

                    def use2(st):
                        slot = st.slot(ER)
                        st.ready(dve, act_done)
                        st.freed(dve, reduced, ER)
                        for k, m, h in units(st):
                            V.tensor_tensor(t2[:, slot, k, :], h[:, 0, 0:D], t1[:, slot, k, :], ALU.mult).then_inc(vec_done, 1)
                        st.ready(dve, vec_done, nv)
                        heads16(st)

                    def use3(st):
                        slot = st.slot(ER)
                        st.ready(dve, act_done)
                        for r in range(3):
                            if r or st.has(1):
                                dve.wait_ge(vec_done, st.j * nv + 4 * r)
                            for k, m, h in units(st):
                                own_rel, hr = mk[:, bass.ds(st.j * G + k, 1), r], h[:, 0, D * r:D * r + D]
                                if r == 0:
                                    i = V.tensor_scalar(t2[:, slot, k, :], hr, own_rel, None, ALU.mult)
                                elif r == 1:
                                    i = V.scalar_tensor_tensor(out=t1[:, slot, k, :], in0=hr, scalar=own_rel,
                                                               in1=t2[:, slot, k, :], op0=ALU.mult, op1=ALU.add)
                                else:
                                    to = keep[:, bass.ds(st.j * G + k, 1), :].rearrange("p a d -> p (a d)")
                                    i = V.scalar_tensor_tensor(out=to, in0=hr, scalar=own_rel,
                                                               in1=t1[:, slot, k, :], op0=ALU.mult, op1=ALU.add)
                                i.then_inc(vec_done, 1)

                    pipeline(dve, ESTEPS, ER, [(0, evac), (1, (use0, use1, use2, use3)[l])])
            if l == 1:
                self.carry_fix(l, ro, self.agg, D)

    def softmax(self, l, H, S, SS=None, scale=1.0, eps=0.0, mk=None, sel=None):
        nc, pre = self.nc, f"s{l}_"
        NB = H // 4
        with ExitStack() as ctx:
            sb = lambda name, shape: self.sb(ctx, pre + name, shape)
            F, B = sb("F", [P, T, H]), sb("B", [P, T, H])
            cf, cb = sb("cf", [P, H]), sb("cb", [P, H])
            diag = sb("diag", [P, 2, H, P])
            pen = sb("pen", [P, H, P])
            ps = [self.ps(ctx, pre + f"ps{k}", [P, 4, 128]) for k in range(2 * NB)]
            own, ready, spread, maxed, exped, ends, carried = (self.sem(pre + n) for n in ("own", "ready", "spread", "maxed", "exped", "ends", "carried"))
            if l == 3:
                nm = sb("nm", [P, T, 3])
            block = ctx.enter_context(nc.Block())

            @block.tensor
            def _(pe):
                pe.wait_ge(ready, 1)
                for d in range(2):
                    for b in range(NB):
                        i = nc.tensor.matmul(ps[d * NB + b][:, :, 0:P], self.ones[:], diag[:, d, 4 * b:4 * b + 4, :],
                                             start=True, stop=True)
                i.then_inc(spread, 1)
                pe.wait_ge(ends, 1)
                nc.tensor.matmul(ps[0][:, 0, 0:H], self.carry_f[:], F[:, T - 1, :], start=True, stop=True)
                nc.tensor.matmul(ps[1][:, 0, 0:H], self.carry_b[:], B[:, 0, :], start=True, stop=True).then_inc(carried, 1)

            @block.scalar
            def _(act):
                act.wait_ge(maxed, 1)
                i = nc.scalar.activation(S[:], S[:], ACT.Exp, scale=scale)
                if l == 3:
                    i = nc.scalar.activation(SS[:], SS[:], ACT.Exp)
                i.then_inc(exped, 1)

            @block.vector
            def _(dve):
                V, ch = nc.vector, Chain(dve, own)

                def scans(mult, combine, prev, nxt, init_f, init_b):
                    ops = []
                    for h in range(H):
                        i_f = init_f if isinstance(init_f, float) else init_f[:, h:h + 1]
                        i_b = init_b if isinstance(init_b, float) else init_b[:, h:h + 1]
                        ops.append(V.tensor_tensor_scan(F[:, :, h], prev[:], S[:, :, h], i_f, mult, combine))
                        ops.append(V.tensor_tensor_scan(B[:, ::-1, h], nxt[:, ::-1], S[:, ::-1, h], i_b, mult, combine))
                    ch(*ops)

                if l == 3:
                    ch(*[V.scalar_tensor_tensor(out=z[:], in0=z[:], scalar=0.2, in1=z[:], op0=ALU.mult, op1=ALU.max)
                         for z in (S, SS)])
                    s4 = S[:].rearrange("p t (r h) -> p t r h", h=4)
                    wide = lambda m: m[:].unsqueeze(3).to_broadcast([P, T, 3, 4])
                    ch(V.tensor_tensor(s4, s4, wide(mk), ALU.mult), V.tensor_scalar(nm[:], mk[:], -1.0, NEG, ALU.add, ALU.mult))
                    ch(V.tensor_tensor(s4, s4, wide(nm), ALU.add))
                scans(ALU.add, ALU.max, self.pen_prev, self.pen_next, -BIG, -BIG)
                idb = self.ident[0:P, 0:P].unsqueeze(1).to_broadcast([P, H, P])
                ch(V.tensor_tensor(diag[:, 0], idb, F[:, T - 1, :].unsqueeze(2).to_broadcast([P, H, P]), ALU.mult),
                   V.tensor_tensor(diag[:, 1], idb, B[:, 0, :].unsqueeze(2).to_broadcast([P, H, P]), ALU.mult))
                V.memset(cf[:], 0.0).then_inc(ready, 1)
                dve.wait_ge(ready, 1)
                dve.wait_ge(spread, 1)
                for d, (pc, c) in enumerate(((self.pen_cf, cf), (self.pen_cb, cb))):
                    ch(*[V.tensor_tensor(pen[:, 4 * b:4 * b + 4, :], ps[d * NB + b][:, :, 0:P],
                                         pc[:].unsqueeze(1).to_broadcast([P, 4, P]), ALU.add) for b in range(NB)])
                    ch(V.tensor_reduce(c[:], pen[:], AX.X, ALU.max))
                scans(ALU.add, ALU.max, self.pen_prev, self.pen_next, cf, cb)
                ch(V.tensor_tensor(F[:], F[:], B[:], ALU.max))
                if l == 3:
                    ch(V.tensor_tensor(F[:], F[:], SS[:], ALU.max))
                    ch(V.tensor_tensor(SS[:], SS[:], F[:], ALU.subtract))
                V.tensor_tensor(S[:], S[:], F[:], ALU.subtract).then_inc(maxed, 1)
                dve.wait_ge(exped, 1)
                scans(ALU.mult, ALU.add, self.same_prev, self.same_next, 0.0, 0.0)
                V.memset(pen[:, 0, 0:1], 0.0).then_inc(ends, 1)
                dve.wait_ge(ends, 1)
                dve.wait_ge(carried, 1)
                ch(V.tensor_copy(cf[:], ps[0][:, 0, 0:H]), V.tensor_copy(cb[:], ps[1][:, 0, 0:H]))
                scans(ALU.mult, ALU.add, self.same_prev, self.same_next, cf, cb)
                ch(V.tensor_tensor(F[:], F[:], B[:], ALU.add))
                ch(V.tensor_tensor(F[:], F[:], S[:], ALU.subtract))
                if l == 3:
                    ch(V.tensor_tensor(F[:], F[:], SS[:], ALU.add))
                else:
                    ch(V.tensor_scalar(F[:], F[:], eps, None, ALU.add))
                ch(V.reciprocal(B[:], F[:]))
                ch(V.tensor_tensor(S[:], S[:], B[:], ALU.mult))
                if l == 3:
                    ch(V.tensor_tensor(SS[:], SS[:], B[:], ALU.mult))
                    ch(V.tensor_tensor(s4, s4, wide(mk), ALU.mult))
                    ch(V.tensor_reduce(sel[:], S[:].rearrange("p t (r h) -> p t h r", h=4), AX.X, ALU.add))

    def message_pass(self, l, keep, weight, H, dst, width, SS=None):
        nc, pre = self.nc, f"m{l}_"
        with ExitStack() as ctx:
            sb = lambda name, shape, dt=F32: self.sb(ctx, pre + name, shape, dt)
            ro, msg = sb("ro", [P, ER, G, width]), sb("msg", [P, ER, G, D])
            pcols = sb("pcols", [P, ER, G], I32)
            made, summed, copied, go, selfs = (self.sem(pre + n) for n in ("made", "summed", "copied", "go", "selfs"))
            put = [self.sem(pre + f"put{k}") for k in range(ER)]
            with ExitStack() as c2:
                block = c2.enter_context(nc.Block())

                @block.vector
                def _(dve):
                    nc.vector.memset(ro[:, ER - 1, G - 1, 0:D], 0.0).then_inc(made, 1)
                    dve.wait_ge(made, 1)

                    def make(st):
                        tiles = bass.ds(st.j * G, G)
                        st.freed(dve, summed, ER, G)
                        nc.vector.tensor_tensor(msg[:, st.slot(ER)].rearrange("p k (h c) -> p k h c", h=H),
                                                keep[:, tiles, :].rearrange("p k (h c) -> p k h c", h=H),
                                                weight[:, tiles, :].unsqueeze(3).to_broadcast([P, G, H, D // H]),
                                                ALU.mult).then_inc(made, 1)

                    def add(st):
                        dve.wait_ge(made, st.j + 2)
                        self.running_sum(dve, st, ro, msg, st.slot(ER), put, summed)

                    pipeline(dve, ESTEPS, ER, [(0, make), (1, add)])

                if l == 3:
                    @block.scalar
                    def _(act):
                        def self_weights(st):
                            st.sent(act, put, 16 * G)
                            nc.scalar.copy(ro[:, st.slot(ER), :, D:W3], SS[:, bass.ds(st.j * G, G), :]).then_inc(selfs, 1)

                        pipeline(act, ESTEPS, ER, [(0, self_weights)])

                @block.gpsimd
                def _(pool):
                    waits = [(summed, G)] + [(selfs, 1)] * (l == 3)
                    pipeline(pool, ESTEPS, ER, [(0, lambda st: self.scatter(pool, st, pcols, ro, dst, put, copied, go, waits))])
                    for k in range(ER):
                        pool.wait_ge(put[k], 16 * G * (ESTEPS // ER))
            self.carry_fix(l, ro, dst, width)

    def attention_layer(self, l):
        H = {0: 8, 2: 8, 3: 12}[l]
        nc = self.nc
        with ExitStack() as ctx:
            keep = self.sb(ctx, f"keep{l}", [P, T, D])
            S = self.sb(ctx, f"S{l}", [P, T, H])
            if l != 3:
                self.edge_pass(l, ctx, keep, S)
                self.softmax(l, H, S, scale=(1.0, None, 0.25)[l], eps=(1e-8, None, 1e-16)[l])
                self.message_pass(l, keep, S, H, self.agg, D)
                return
            SS = self.sb(ctx, "SS3", [P, T, H])
            mk = self.sb(ctx, "mk3", [P, T, 3])
            sel = self.sb(ctx, "sel3", [P, T, 4])
            with ExitStack() as c2:
                ty_i, ty = self.sb(c2, "ty_i", [P, T], I32), self.sb(c2, "ty", [P, T])
                loaded, own = self.sem("r_loaded"), self.sem("r_own")
                block = c2.enter_context(nc.Block())

                @block.sync
                def _(sp):
                    sp.dma_start(ty_i[:], self.a["edge_type_3"].rearrange("(p t) -> p t", p=P)).then_inc(loaded, 16)

                @block.vector
                def _(dve):
                    ch = Chain(dve, own)
                    dve.wait_ge(loaded, 16)
                    ch(nc.vector.tensor_copy(ty[:], ty_i[:]))
                    ch(*[nc.vector.tensor_scalar(mk[:, :, r], ty[:], float(r), None, ALU.is_equal) for r in range(3)])
            self.edge_pass(3, ctx, keep, S, SS, mk, self.w3s, None, self.rel_w)
            self.softmax(3, H, S, SS, mk=mk, sel=sel)
            self.message_pass(3, keep, sel, 4, self.agg3, W3, SS)

    def norm(self, ctx, name, ring):
        return LayerNorm(self, ctx, name, ring)

    def node_io(self, ctx, pre, l, ring, agg, width):
        b = self
        x, s = b.sb(ctx, pre + "x", [P, ring, G, D]), b.sb(ctx, pre + "s", [P, ring, G, width])
        got = [b.sem(pre + f"got{k}") for k in range(ring)]
        put = [b.sem(pre + f"put{k}") for k in range(ring)]
        x_v, s_v, o_v = (t.rearrange("(p n) d -> p n d", p=P) for t in (b.x[l], agg, b.x[l + 1]))

        def load(sp, st, readers):
            for s_read in readers:
                st.freed(sp, s_read, ring)
            slot, nodes = st.slot(ring), bass.ds(st.j * G, G)
            load_rows(sp, x[:, slot], x_v[:, nodes, :], got[slot])
            load_rows(sp, s[:, slot], s_v[:, nodes, :], got[slot])

        def store(sp, st, o, ready):
            st.ready(sp, ready)
            load_rows(sp, o_v[:, bass.ds(st.j * G, G), :], o[:, st.slot(ring)], put[st.slot(ring)])

        def finish(sp):
            for k in range(ring):
                sp.wait_ge(put[k], 32 * (NSTEPS // ring))

        return x, s, got, put, load, store, finish

    def load_consts(self, sp, loaded, pairs):
        for to, of in pairs:
            sp.dma_start(to, of).then_inc(loaded, 16)

    def nodes_simple(self, l):
        nc, a, pre, R = self.nc, self.a, f"n{l}_", 4
        with ExitStack() as ctx:
            sb = lambda name, shape: self.sb(ctx, pre + name, shape)
            x, s, got, put, load, store, finish = self.node_io(ctx, pre, l, R, self.agg, D)
            w, rows = sb("w", [D, D]), sb("rows", [P, 3, D])
            aT, y0, y1, t, u, g, o = sb("aT", [128, R, G, P]), *(sb(n, [P, R, G, D]) for n in ("y0", "y1", "t", "u", "g", "o"))
            ps_t = [self.ps(ctx, pre + f"ps_t{k}", [128, G, 128]) for k in range(2)]
            ps_o = [self.ps(ctx, pre + f"ps_o{k}", [128, G, 128]) for k in range(2)]
            loaded, tr, ev, mm, side, tsum, usum, scaled = (self.sem(pre + n) for n in
                                                            ("loaded", "tr", "ev", "mm", "side", "tsum", "usum", "scaled"))
            ln1 = self.norm(ctx, pre + "ln1", R) if l == 0 else None
            ln2 = self.norm(ctx, pre + "ln2", R)
            names = ("L0_gnn_W_out", "L0_gnn_b_out", "L0_gnn_gamma", "L0_gnn_beta") if l == 0 else ("L1_gnn_Wres", "L1_gnn_bres")
            fed, other = (s, x) if l == 0 else (x, s)
            out_lag = 5 if l == 0 else 3
            block = ctx.enter_context(nc.Block())

            @block.sync
            def _(sp):
                self.load_consts(sp, loaded, [(w[:], a[names[0]])] + [(rows[:, k, :], rows_of(a[n], P)) for k, n in enumerate(names[1:])])
                pipeline(sp, NSTEPS, R, [(0, lambda st: load(sp, st, [tr, side] + ([usum] if l == 1 else []))),
                                         (out_lag, lambda st: store(sp, st, o, ln2.scaled))])
                finish(sp)

            @block.tensor
            def _(pe):
                def transposes(st):
                    st.arrived(pe, got, 64)
                    st.freed(pe, ev, 2)
                    for k in range(G):
                        i = nc.tensor.transpose(ps_t[st.slot(2)][:, k, 0:P], fed[:, st.slot(R), k, 0:D], self.ident[0:P, 0:P])
                    i.then_inc(tr, 1)

                def products(st):
                    st.ready(pe, ev)
                    st.freed(pe, tsum, 2)
                    for k in range(G):
                        i = nc.tensor.matmul(ps_o[st.slot(2)][0:P, k, :], aT[:, st.slot(R), k, :], w[:],
                                             start=True, stop=True, skip_group_check=True)
                    i.then_inc(mm, 1)

                pe.wait_ge(loaded, 16 * len(names))
                pipeline(pe, NSTEPS, R, [(0, transposes), (1, products)])

            @block.scalar
            def _(act):
                def evac(st):
                    st.ready(act, tr)
                    st.freed(act, mm, R)
                    nc.scalar.copy(aT[:, st.slot(R)], ps_t[st.slot(2)][:, :, 0:P]).then_inc(ev, 1)

                stages = [(0, evac)]
                if l == 0:
                    stages += [(1, lambda st: ln1.root(act, st)), (3, lambda st: ln2.root(act, st))]
                else:
                    stages += [(1, lambda st: ln2.root(act, st))]
                pipeline(act, NSTEPS, R, stages)

            @block.gpsimd
            def _(pool):
                def sides(st):
                    slot = st.slot(R)
                    wait_pool(pool, go, lambda: st.arrived(pool, got, 64))
                    if st.has(R):
                        wait_pool(pool, go, lambda: st.freed(pool, tsum, R))
                        if l == 0:
                            wait_pool(pool, go, lambda: st.freed(pool, usum, R))
                    i = nc.gpsimd.tensor_tensor(y0[:, slot], other[:, slot], over_tiles(rows[:, 0, :]), ALU.add)
                    if l == 0:
                        i = nc.gpsimd.tensor_tensor(y1[:, slot], x[:, slot], over_tiles(rows[:, 2, :]), ALU.add)
                    i.then_inc(side, 1)

                def gamma(st):
                    slot = st.slot(R)
                    wait_pool(pool, go, lambda: st.ready(pool, ln1.scaled))
                    if st.has(R):
                        wait_pool(pool, go, lambda: st.freed(pool, usum, R))
                    nc.gpsimd.tensor_tensor(g[:, slot], u[:, slot], over_tiles(rows[:, 1, :]), ALU.mult).then_inc(scaled, 1)

                go = self.sem(pre + "go")
                wait_pool(pool, go, lambda: pool.wait_ge(loaded, 16 * len(names)))
                pipeline(pool, NSTEPS, R, [(0, sides)] + ([(2, gamma)] if l == 0 else []))

            @block.vector
            def _(dve):
                V = nc.vector

                def first(st):
                    slot = st.slot(R)
                    st.ready(dve, mm)
                    st.ready(dve, side)
                    if l == 0:
                        st.freed(dve, ln2.scaled, R)
                        V.tensor_tensor(t[:, slot], ps_o[st.slot(2)][0:P, :, :], y0[:, slot], ALU.add).then_inc(tsum, 1)
                        st.ready(dve, tsum)
                        ln1.stats(dve, st, t)
                    else:
                        st.freed(dve, usum, R)
                        V.tensor_tensor(t[:, slot], ps_o[st.slot(2)][0:P, :, :], y0[:, slot], ALU.add).then_inc(tsum, 1)
                        st.ready(dve, tsum)
                        V.scalar_tensor_tensor(out=u[:, slot], in0=t[:, slot], scalar=0.0, in1=x[:, slot],
                                               op0=ALU.max, op1=ALU.add).then_inc(usum, 1)
                        st.ready(dve, usum)
                        ln2.stats(dve, st, u)

                def second(st):
                    slot = st.slot(R)
                    st.ready(dve, scaled)
                    st.ready(dve, side)
                    V.tensor_tensor(t[:, slot], g[:, slot], y1[:, slot], ALU.add).then_inc(usum, 1)
                    st.ready(dve, usum)
                    ln2.stats(dve, st, t)

                if l == 0:
                    stages = [(1, first), (2, lambda st: ln1.scale(dve, st, t, u)), (3, second),
                              (4, lambda st: ln2.scale(dve, st, t, o, put))]
                else:
                    stages = [(1, first), (2, lambda st: ln2.scale(dve, st, u, o, put))]
                pipeline(dve, NSTEPS, R, stages)

    def nodes_transformer(self):
        nc, a, pre, l, R = self.nc, self.a, "n2_", 2, 10
        F = 4
        with ExitStack() as ctx:
            sb = lambda name, shape: self.sb(ctx, pre + name, shape)
            x, s, got, put, load, store, finish = self.node_io(ctx, pre, l, R, self.agg, D)
            wo, w1, w2 = sb("wo", [D, D]), sb("w1", [D, F * D]), sb("w2", [D, F, D])
            rows, b1 = sb("rows", [P, 6, D]), sb("b1", [D, F])
            aT, hT = sb("aT", [128, 2, G, P]), sb("hT", [128, 2, G, P])
            hid = sb("hid", [128, 2, F, G, P])
            y0, t, n1 = (sb(n, [P, 2, G, D]) for n in ("y0", "t", "n1"))
            h0, h, y1 = sb("h0", [P, 2, G, D]), sb("h", [P, 5, G, D]), sb("y1", [P, 5, G, D])
            v, n2, g2, y2, wv, o = (sb(n, [P, 2, G, D]) for n in ("v", "n2", "g2", "y2", "wv", "o_"))
            o = sb("o", [P, R, G, D])
            ps_t, ps_h, ps_o, ps_v = (self.ps(ctx, pre + n, [128, G, 128]) for n in ("ps_t", "ps_h", "ps_o", "ps_v"))
            ps_f = [self.ps(ctx, pre + f"ps_f{k}", [128, G, P]) for k in range(F)]
            loaded, tr, ev, mm, side, tsum = (self.sem(pre + n) for n in ("loaded", "tr", "ev", "mm", "side", "tsum"))
            hg, hb, trh, evh, f1, relu, f2, side2, vsum, g2d, side3, wsum, go = (self.sem(pre + n) for n in (
                "hg", "hb", "trh", "evh", "f1", "relu", "f2", "side2", "vsum", "g2d", "side3", "wsum", "go"))
            ln1, ln2, ln3 = (self.norm(ctx, pre + f"ln{k}", 2) for k in (1, 2, 3))
            vecs = ("bo", "ln1_g", "ln1_b", "b2", "ln2_g", "ln2_b")
            consts = [(wo[:], a["L2_gnn_Wo"]), (w1[:], a["L2_gnn_W1"]), (w2[:], a["L2_gnn_W2"].rearrange("(f i) o -> i f o", f=F))]
            consts += [(rows[:, k, :], rows_of(a["L2_gnn_" + n], P)) for k, n in enumerate(vecs)]
            n_const = 16 * (len(consts) + 1)
            row = lambda n: over_tiles(rows[:, vecs.index(n), :])
            block = ctx.enter_context(nc.Block())

            @block.sync
            def _(sp):
                self.load_consts(sp, loaded, consts)
                with nc.allow_non_contiguous_dma(reason="512 biases, one a partition and chunk"):
                    sp.dma_start(b1[:], a["L2_gnn_b1"].rearrange("(f i) -> i f", f=F)).then_inc(loaded, 16)
                pipeline(sp, NSTEPS, R, [(0, lambda st: load(sp, st, [tr, side3])),
                                         (9, lambda st: store(sp, st, o, ln3.scaled))])
                finish(sp)

            @block.tensor
            def _(pe):
                def turn(st, bank, buf, slot, done):
                    for k in range(G):
                        i = nc.tensor.transpose(bank[:, k, 0:P], buf[:, slot, k, :], self.ident[0:P, 0:P])
                    i.then_inc(done, 1)

                def turn_sums(st):
                    st.arrived(pe, got, 64)
                    st.freed(pe, ev, 1)
                    turn(st, ps_t, s, st.slot(R), tr)

                def out_product(st):
                    st.ready(pe, ev)
                    st.freed(pe, tsum, 1)
                    for k in range(G):
                        i = nc.tensor.matmul(ps_o[0:P, k, :], aT[:, st.slot(2), k, :], wo[:], start=True, stop=True, skip_group_check=True)
                    i.then_inc(mm, 1)

                def turn_h(st):
                    st.ready(pe, hb)
                    st.freed(pe, evh, 1)
                    turn(st, ps_h, h, st.slot(5), trh)

                def up(st):
                    st.ready(pe, evh)
                    for f in range(F):
                        if st.has(1):
                            pe.wait_ge(relu, st.j * F - (F - 1 - f))
                        nc.tensor.matmul(ps_f[f][:], w1[:, f * D:f * D + D], hT[:, st.slot(2)], start=True, stop=True).then_inc(f1, 1)

                def down(st):
                    st.ready(pe, relu, F)
                    st.freed(pe, vsum, 1)
                    for k in range(G):
                        for f in range(F):
                            i = nc.tensor.matmul(ps_v[0:P, k, :], hid[:, st.slot(2), f, k, :], w2[:, f, :],
                                                 start=(f == 0), stop=(f == F - 1), skip_group_check=True)
                    i.then_inc(f2, 1)

                pe.wait_ge(loaded, n_const)
                pipeline(pe, NSTEPS, R, [(0, turn_sums), (3, turn_h), (5, down), (1, out_product), (4, up)])

            @block.scalar
            def _(act):
                def evac(st):
                    st.ready(act, tr)
                    st.freed(act, mm, 2)
                    nc.scalar.copy(aT[:, st.slot(2)], ps_t[:, :, 0:P]).then_inc(ev, 1)

                def evac_h(st):
                    st.ready(act, trh)
                    st.freed(act, f1, 2, F)
                    nc.scalar.copy(hT[:, st.slot(2)], ps_h[:, :, 0:P]).then_inc(evh, 1)

                def relus(st):
                    st.freed(act, f2, 2)
                    for f in range(F):
                        act.wait_ge(f1, st.j * F + f + 1)
                        nc.scalar.activation(hid[:, st.slot(2), f], ps_f[f][:], ACT.Relu, bias=b1[:, f:f + 1]).then_inc(relu, 1)

                pipeline(act, NSTEPS, R, [(0, evac), (1, lambda st: ln1.root(act, st)), (3, evac_h), (4, relus),
                                          (5, lambda st: ln2.root(act, st)), (7, lambda st: ln3.root(act, st))])

            @block.gpsimd
            def _(pool):
                add = nc.gpsimd.tensor_tensor

                def side_x(st):
                    wait_pool(pool, go, lambda: st.arrived(pool, got, 64))
                    if st.has(2):
                        wait_pool(pool, go, lambda: st.freed(pool, tsum, 2))
                    add(y0[:, st.slot(2)], x[:, st.slot(R)], row("bo"), ALU.add).then_inc(side, 1)

                def make_h(st):
                    wait_pool(pool, go, lambda: st.ready(pool, ln1.scaled))
                    if st.has(2):
                        wait_pool(pool, go, lambda: st.freed(pool, hb, 2))
                    add(h0[:, st.slot(2)], n1[:, st.slot(2)], row("ln1_g"), ALU.mult).then_inc(hg, 1)
                    wait_pool(pool, go, lambda: st.ready(pool, hg))
                    if st.has(5):
                        wait_pool(pool, go, lambda: st.freed(pool, trh, 5))
                        wait_pool(pool, go, lambda: st.freed(pool, side2, 5))
                    add(h[:, st.slot(5)], h0[:, st.slot(2)], row("ln1_b"), ALU.add).then_inc(hb, 1)

                def side_h(st):
                    wait_pool(pool, go, lambda: st.ready(pool, hb))
                    if st.has(5):
                        wait_pool(pool, go, lambda: st.freed(pool, vsum, 5))
                    add(y1[:, st.slot(5)], h[:, st.slot(5)], row("b2"), ALU.add).then_inc(side2, 1)

                def second(st):
                    if st.has(2):
                        wait_pool(pool, go, lambda: st.freed(pool, wsum, 2))
                    add(y2[:, st.slot(2)], x[:, st.slot(R)], row("ln2_b"), ALU.add).then_inc(side3, 1)
                    wait_pool(pool, go, lambda: st.ready(pool, ln2.scaled))
                    add(g2[:, st.slot(2)], n2[:, st.slot(2)], row("ln2_g"), ALU.mult).then_inc(g2d, 1)

                wait_pool(pool, go, lambda: pool.wait_ge(loaded, n_const))
                pipeline(pool, NSTEPS, R, [(0, side_x), (2, make_h), (3, side_h), (6, second)])

            @block.vector
            def _(dve):
                add = nc.vector.tensor_tensor

                def first(st):
                    st.ready(dve, mm)
                    st.ready(dve, side)
                    st.freed(dve, ln1.scaled, 2)
                    add(t[:, st.slot(2)], ps_o[0:P], y0[:, st.slot(2)], ALU.add).then_inc(tsum, 1)
                    st.ready(dve, tsum)
                    ln1.stats(dve, st, t)

                def ffn(st):
                    st.ready(dve, f2)
                    st.ready(dve, side2)
                    st.freed(dve, ln2.scaled, 2)
                    add(v[:, st.slot(2)], ps_v[0:P], y1[:, st.slot(5)], ALU.add).then_inc(vsum, 1)
                    st.ready(dve, vsum)
                    ln2.stats(dve, st, v)

                def third(st):
                    st.ready(dve, g2d)
                    st.freed(dve, ln3.scaled, 2)
                    add(wv[:, st.slot(2)], g2[:, st.slot(2)], y2[:, st.slot(2)], ALU.add).then_inc(wsum, 1)
                    st.ready(dve, wsum)
                    ln3.stats(dve, st, wv)

                pipeline(dve, NSTEPS, R, [
                    (1, first), (2, lambda st: ln1.scale(dve, st, t, n1, None, hg)), (5, ffn),
                    (6, lambda st: ln2.scale(dve, st, v, n2, None, g2d)), (7, third),
                    (8, lambda st: ln3.scale(dve, st, wv, o, put))])

    def nodes_relational(self):
        nc, a, pre, l, R = self.nc, self.a, "n3_", 3, 4
        with ExitStack() as ctx:
            sb = lambda name, shape: self.sb(ctx, pre + name, shape)
            x, s, got, put, load, store, finish = self.node_io(ctx, pre, l, R, self.agg3, W3)
            b3, bias = sb("b3", [P, 3, D]), sb("bias", [P, 2, D])
            xT = sb("xT", [128, R, G, P])
            y0, y, u, o = (sb(n, [P, R, G, D]) for n in ("y0", "y", "u", "o"))
            m, r3 = sb("m", [P, 2, G, 3, D]), sb("r3", [P, 2, G, D])
            ps_t = [self.ps(ctx, pre + f"ps_t{k}", [128, G, 128]) for k in range(2)]
            ps_o = [self.ps(ctx, pre + f"ps_o{k}", [128, 512]) for k in range(G)]
            loaded, own, biased, tr, ev, mm, s0, side, weighted, summed, usum, go = (self.sem(pre + n) for n in (
                "loaded", "own", "biased", "tr", "ev", "mm", "s0", "side", "weighted", "summed", "usum", "go"))
            ln = self.norm(ctx, pre + "ln", R)
            block = ctx.enter_context(nc.Block())

            @block.sync
            def _(sp):
                self.load_consts(sp, loaded, [(b3[:, r, :], rows_of(a["L3_gnn_bias"][r, :], P)) for r in range(3)])
                pipeline(sp, NSTEPS, R, [(0, lambda st: load(sp, st, [tr, side, summed])),
                                         (3, lambda st: store(sp, st, o, ln.scaled))])
                finish(sp)

            @block.tensor
            def _(pe):
                def transposes(st):
                    st.arrived(pe, got, 64)
                    st.freed(pe, ev, 2)
                    for k in range(G):
                        i = nc.tensor.transpose(ps_t[st.slot(2)][:, k, 0:P], x[:, st.slot(R), k, :], self.ident[0:P, 0:P])
                    i.then_inc(tr, 1)

                def products(st):
                    st.ready(pe, ev)
                    for k in range(G):
                        if st.has(1):
                            pe.wait_ge(weighted, st.j * G - (G - 1 - k))
                        nc.tensor.matmul(ps_o[k][0:P, 0:3 * D], xT[:, st.slot(R), k, :], self.w3s[:],
                                         start=True, stop=True).then_inc(mm, 1)

                pipeline(pe, NSTEPS, R, [(0, transposes), (1, products)])

            @block.scalar
            def _(act):
                def evac(st):
                    st.ready(act, tr)
                    st.freed(act, mm, R, G)
                    nc.scalar.copy(xT[:, st.slot(R)], ps_t[st.slot(2)][:, :, 0:P]).then_inc(ev, 1)

                pipeline(act, NSTEPS, R, [(0, evac), (1, lambda st: ln.root(act, st))])

            @block.gpsimd
            def _(pool):
                def sides(st):
                    slot = st.slot(R)
                    wait_pool(pool, go, lambda: st.arrived(pool, got, 64))
                    if st.has(R):
                        wait_pool(pool, go, lambda: st.freed(pool, side, R))
                        wait_pool(pool, go, lambda: st.freed(pool, usum, R))
                    nc.gpsimd.tensor_tensor(y0[:, slot], s[:, slot, :, 0:D], over_tiles(bias[:, 0, :]), ALU.add).then_inc(s0, 1)
                    wait_pool(pool, go, lambda: st.ready(pool, s0))
                    nc.gpsimd.tensor_tensor(y[:, slot], y0[:, slot], x[:, slot], ALU.add).then_inc(side, 1)

                wait_pool(pool, go, lambda: pool.wait_ge(biased, 1))
                pipeline(pool, NSTEPS, R, [(0, sides)])

            @block.vector
            def _(dve):
                V, ch, rw = nc.vector, Chain(dve, own), self.rel_w
                dve.wait_ge(loaded, 48)
                ch(V.tensor_scalar(bias[:, 1, :], b3[:, 0, :], rw[0:P, 0:1], None, ALU.mult))
                ch(V.scalar_tensor_tensor(out=bias[:, 0, :], in0=b3[:, 1, :], scalar=rw[0:P, 1:2], in1=bias[:, 1, :], op0=ALU.mult, op1=ALU.add))
                ch(V.scalar_tensor_tensor(out=bias[:, 1, :], in0=b3[:, 2, :], scalar=rw[0:P, 2:3], in1=bias[:, 0, :], op0=ALU.mult, op1=ALU.add))
                V.tensor_copy(bias[:, 0, :], bias[:, 1, :]).then_inc(biased, 1)
                dve.wait_ge(biased, 1)

                def first(st):
                    slot = st.slot(R)
                    st.arrived(dve, got, 64)
                    st.freed(dve, summed, 2)
                    for k in range(G):
                        dve.wait_ge(mm, st.j * G + k + 1)
                        V.tensor_tensor(m[:, st.slot(2), k].rearrange("p r (h c) -> p (r h) c", h=4),
                                        ps_o[k][0:P, 0:3 * D].rearrange("p (q c) -> p q c", c=32),
                                        s[:, slot, k, D:W3].unsqueeze(2).to_broadcast([P, 12, 32]), ALU.mult).then_inc(weighted, 1)
                    st.ready(dve, weighted, G)
                    st.freed(dve, usum, 2)
                    V.tensor_reduce(r3[:, st.slot(2)], m[:, st.slot(2)].rearrange("p k r c -> p k c r"), AX.X, ALU.add).then_inc(summed, 1)
                    st.ready(dve, summed)
                    st.ready(dve, side)
                    V.tensor_tensor(u[:, slot], r3[:, st.slot(2)], y[:, slot], ALU.add).then_inc(usum, 1)
                    st.ready(dve, usum)
                    ln.stats(dve, st, u)

                pipeline(dve, NSTEPS, R, [(1, first), (2, lambda st: ln.scale(dve, st, u, o, put))])

    def run(self, layers=(0, 1, 2, 3)):
        self.graph()
        if 0 in layers:
            self.attention_layer(0)
            self.nodes_simple(0)
            self.recycle()
        if 1 in layers:
            with ExitStack() as ctx:
                self.edge_pass(1, ctx)
            self.nodes_simple(1)
            self.recycle()
        if 2 in layers:
            self.attention_layer(2)
            self.nodes_transformer()
            self.recycle()
        if 3 in layers:
            with ExitStack() as ctx:
                self.w3s = self.sb(ctx, "w3s", [D, 3 * D])
                self.rel_w = self.sb(ctx, "rel_w", [D, 3])
                self.attention_layer(3)
                self.nodes_relational()


def wait_pool(pool, go, wait):
    wait()
    pool.sem_inc(go, 1)


class LayerNorm:

    def __init__(self, b, ctx, name, ring):
        self.b, self.ring = b, ring
        self.bn = b.sb(ctx, name + "bn", [P, ring, G, 6])
        self.mv = b.sb(ctx, name + "mv", [P, ring, G, 2])
        self.sd = b.sb(ctx, name + "sd", [P, ring, G])
        self.rs = b.sb(ctx, name + "rs", [P, ring, G])
        self.parts, self.aggr, self.rooted, self.inverse, self.scaled, self.go = (
            b.sem(name + n) for n in ("parts", "aggr", "rooted", "inverse", "scaled", "go"))

    def stats(self, dve, st, x):
        V, slot = self.b.nc.vector, st.slot(self.ring)
        xslot = st.slot(x.shape[1])
        st.freed(dve, self.aggr, self.ring)
        for k in range(G):
            i = V.bn_stats(self.bn[:, slot, k, :], x[:, xslot, k, :])
        i.then_inc(self.parts, 1)
        st.ready(dve, self.parts)
        dve.sem_inc(self.go, 1)
        if st.has(self.ring):
            st.freed(dve, self.scaled, self.ring)
            dve.sem_inc(self.go, 1)
        for k in range(G):
            i = V.bn_aggr(self.mv[:, slot, k, :], self.bn[:, slot, k, :])
        i.then_inc(self.aggr, 1)

    def root(self, act, st):
        slot = st.slot(self.ring)
        st.ready(act, self.aggr)
        st.freed(act, self.inverse, self.ring)
        self.b.nc.scalar.activation(self.sd[:, slot], self.mv[:, slot, :, 1], ACT.Sqrt, bias=self.b.eps[0:P]).then_inc(self.rooted, 1)

    def scale(self, dve, st, x, out, put=None, used=None):
        V, slot, xs, os_ = self.b.nc.vector, st.slot(self.ring), st.slot(x.shape[1]), st.slot(out.shape[1])
        st.ready(dve, self.rooted)
        st.freed(dve, self.scaled, self.ring)
        V.reciprocal(self.rs[:, slot], self.sd[:, slot]).then_inc(self.inverse, 1)
        st.ready(dve, self.inverse)
        if put is not None:
            st.sent(dve, put, 32)
        if used is not None:
            st.freed(dve, used, out.shape[1])
        for k in range(G):
            i = V.tensor_scalar(out[:, os_, k, :], x[:, xs, k, :], self.mv[:, slot, k, 0:1], self.rs[:, slot, k:k + 1],
                                ALU.subtract, ALU.mult)
        i.then_inc(self.scaled, 1)


def build(nc, args, out):
    with ExitStack() as top:
        Builder(nc, args, out, top).run()


_INS = ["x", "src", "dst", "edge_attr_128", "edge_type_3", "L0_gnn_W_src", "L0_gnn_W_dst", "L0_gnn_attn", "L0_gnn_W_out",
        "L0_gnn_b_out", "L0_gnn_gamma", "L0_gnn_beta", "L1_gnn_WA", "L1_gnn_bA", "L1_gnn_WB", "L1_gnn_bB", "L1_gnn_WC",
        "L1_gnn_bC", "L1_gnn_WE", "L1_gnn_bE", "L1_gnn_Wres", "L1_gnn_bres", "L2_gnn_Wq", "L2_gnn_bq", "L2_gnn_Wk",
        "L2_gnn_bk", "L2_gnn_Wv", "L2_gnn_bv", "L2_gnn_Wo", "L2_gnn_bo", "L2_gnn_ln1_g", "L2_gnn_ln1_b", "L2_gnn_W1",
        "L2_gnn_b1", "L2_gnn_W2", "L2_gnn_b2", "L2_gnn_ln2_g", "L2_gnn_ln2_b", "L3_gnn_W", "L3_gnn_att_src",
        "L3_gnn_att_dst", "L3_gnn_bias", "L3_gnn_rel_w"]


def kernel(**inputs):
    import concourse.bacc as bacc
    from concourse.bass_utils import run_bass_kernel_spmd

    nc = bacc.Bacc("TRN2", target_bir_lowering=False, num_devices=1)
    arrays, args = {}, {}
    for name in _INS:
        arr = np.ascontiguousarray(inputs[name])
        arrays[f"in_{name}"] = arr
        args[name] = nc.dram_tensor(f"in_{name}", arr.shape, mybir.dt.from_np(arr.dtype), kind="ExternalInput").ap()
    out = nc.dram_tensor("out_x", (N_NODES, D), F32, kind="ExternalOutput").ap()
    build(nc, args, out)
    r = run_bass_kernel_spmd(nc, [arrays], core_ids=[0])
    return r.results[0]["out_x"]
```

```python
import numpy as np
import concourse.bass as bass
import concourse.mybir as mybir
from contextlib import ExitStack

F32 = mybir.dt.float32
I32 = mybir.dt.int32
ALU = mybir.AluOpType
ACT = mybir.ActivationFunctionType
AX = mybir.AxisListType

N_NODES, N_EDGES, D = 50000, 25000, 128
P = 125
T = N_EDGES // P
NT = N_NODES // P
G = 4
ESTEPS, NSTEPS = T // G, NT // G
ER = 2
NR = 10
MR = 5
LR = 5
BIG = 1.0e30
NEG = 1.0e9
EPS_LN = 1e-5
SKIP = 100000.0
SPLIT = 112
W3 = D + 12


class Step:

    def __init__(self, i, q, unroll):
        self.i, self.q, self.unroll = i, q, unroll
        self.j = i * unroll + q
        self.peeled = isinstance(i, int)

    def slot(self, ring):
        return self.q % ring

    def visits(self, ring):
        return self.i * (self.unroll // ring) + self.q // ring

    def has(self, back):
        return not self.peeled or self.j >= back

    def ready(self, eng, sem, per=1):
        eng.wait_ge(sem, (self.j + 1) * per)

    def freed(self, eng, sem, ring, per=1):
        if self.has(ring):
            eng.wait_ge(sem, (self.j - (ring - 1)) * per)

    def arrived(self, eng, sems, per):
        eng.wait_ge(sems[self.slot(len(sems))], (self.visits(len(sems)) + 1) * per)

    def sent(self, eng, sems, per):
        ring = len(sems)
        if self.has(ring):
            eng.wait_ge(sems[self.slot(ring)], self.visits(ring) * per)

    def pair_arrived(self, eng, sems):
        ring = 2 * len(sems)
        eng.wait_ge(sems[self.slot(ring) // 2], (self.visits(ring) + 1) * 64)

    def pair_sent(self, eng, sems):
        ring = 2 * len(sems)
        if self.has(ring):
            eng.wait_ge(sems[self.slot(ring) // 2], self.visits(ring) * 32)


def pipeline(eng, total, unroll, stages):
    most = max(lag for lag, _ in stages)
    warm = unroll * (1 + -(-most // unroll))

    def peeled(t):
        for lag, fn in stages:
            if 0 <= t - lag < total:
                fn(Step((t - lag) // unroll, (t - lag) % unroll, unroll))

    for t in range(warm):
        peeled(t)
    with eng.Fori(warm // unroll, total // unroll) as i:
        for r in range(unroll):
            for lag, fn in stages:
                back = (lag - r + unroll - 1) // unroll if lag > r else 0
                fn(Step(i - back if back else i, r - lag + back * unroll, unroll))
    for t in range(total, total + most):
        peeled(t)


def over_tiles(row, n=G):
    return row.unsqueeze(1).to_broadcast([row.shape[0], n, row.shape[1]])


def load_rows(eng, dst, src, sem):
    eng.dma_start(dst[0:SPLIT], src[0:SPLIT]).then_inc(sem, 16)
    eng.dma_start(dst[SPLIT:P], src[SPLIT:P]).then_inc(sem, 16)


def rows_of(v, n):
    return v.rearrange("(a c) -> a c", a=1).to_broadcast([n, v.shape[0]])


class Chain:

    def __init__(self, eng, sem):
        self.eng, self.sem, self.n = eng, sem, 0

    def __call__(self, *instructions):
        for i in instructions:
            i.then_inc(self.sem, 1)
        self.n += len(instructions)
        self.eng.wait_ge(self.sem, self.n)


class Builder:

    def __init__(self, nc, args, out, top):
        self.nc, self.a, self.out, self.top = nc, args, out, top
        self.filled = False
        self.used = []
        x_after = [nc.dram_tensor(f"x_after_{l}", (N_NODES, D), F32).ap() for l in range(3)]
        self.x = [args["x"], *x_after, out]
        self.agg = nc.dram_tensor("agg", (N_NODES, D), F32).ap()
        self.agg3 = nc.dram_tensor("agg3", (N_NODES, W3), F32).ap()
        sb = lambda name, shape, dt=F32: self.sb(top, name, shape, dt)
        self.ident = sb("ident", [128, 128])
        self.ones = sb("ones", [P, P])
        self.e0 = sb("e0", [128, P])
        self.ident_b = sb("ident_b", [P + 1, P])
        self.eps = sb("eps", [128, 1])
        self.src_i = sb("src_i", [P, T], I32)
        self.dst_i = sb("dst_i", [P, T], I32)
        self.put_i = sb("put_i", [P, T], I32)
        self.fix_i = sb("fix_i", [P, 1], I32)
        self.same_prev = sb("same_prev", [P, T])
        self.same_next = sb("same_next", [P, T])
        self.in_row = sb("in_row", [P, T])
        self.pen_prev = sb("pen_prev", [P, T])
        self.pen_next = sb("pen_next", [P, T])
        self.carry_f = sb("carry_f", [P, P])
        self.carry_b = sb("carry_b", [P, P])
        self.pen_cf = sb("pen_cf", [P, P])
        self.pen_cb = sb("pen_cb", [P, P])

    def sem(self, name):
        handle = self.nc.alloc_semaphore(name)
        self.used.append(handle)
        return handle

    def recycle(self):
        self.nc.clear_and_free_semaphores(self.used)
        self.nc.all_engine_barrier()
        self.used = []

    def sb(self, ctx, name, shape, dt=F32):
        return ctx.enter_context(self.nc.sbuf_tensor(name, shape, dt))

    def ps(self, ctx, name, shape):
        return ctx.enter_context(self.nc.psum_tensor(name, shape, F32))

    def graph(self):
        nc, a, sem = self.nc, self.a, self.sem
        ident, ones, e0, eps, ident_b = self.ident, self.ones, self.e0, self.eps, self.ident_b
        carry_f, carry_b = self.carry_f, self.carry_b
        same_prev, same_next, in_row = self.same_prev, self.same_next, self.in_row
        with ExitStack() as ctx:
            sb = lambda name, shape, dt=F32: self.sb(ctx, name, shape, dt)
            dpad = sb("dpad", [P, T + 2], I32)
            df = sb("df", [P, T + 2])
            last = sb("last", [P, T])
            put_f = sb("put_f", [P, T])
            diag = sb("diag", [P, P])
            fix = sb("fix", [P, 4])
            ps_first = self.ps(ctx, "ps_first", [P, P])
            ps_tr = self.ps(ctx, "ps_tr", [P, P])
            frame, consts, loaded = (sem("g_" + n) for n in ("frame", "consts", "loaded"))
            own, diag_done, first_done = sem("g_own"), sem("g_diag"), sem("g_first")
            equal, upper, turned = sem("g_equal"), sem("g_upper"), sem("g_turned")
            block = ctx.enter_context(nc.Block())

            @block.gpsimd
            def _(pool):
                nc.gpsimd.memset(dpad[:], -1).then_inc(frame, 1)
                nc.gpsimd.memset(ident[:], 0.0).then_inc(consts, 1)
                nc.gpsimd.memset(e0[:], 0.0).then_inc(consts, 1)
                nc.gpsimd.memset(ident_b[:], 0.0).then_inc(consts, 1)
                nc.gpsimd.memset(ones[:], 1.0).then_inc(consts, 1)
                nc.gpsimd.memset(eps[:], EPS_LN).then_inc(consts, 1)
                pool.wait_ge(consts, 5)
                nc.gpsimd.affine_select(out=ident[:], in_=ident[:], compare_op=ALU.not_equal, fill=1.0, base=0,
                                        pattern=[[-1, 128]], channel_multiplier=1).then_inc(consts, 1)
                nc.gpsimd.affine_select(out=e0[:], in_=e0[:], compare_op=ALU.not_equal, fill=1.0, base=0,
                                        pattern=[[0, P]], channel_multiplier=1).then_inc(consts, 1)
                nc.gpsimd.affine_select(out=ident_b[:], in_=ident_b[:], compare_op=ALU.not_equal, fill=1.0, base=0,
                                        pattern=[[-1, P]], channel_multiplier=1).then_inc(consts, 1)
                pool.wait_ge(consts, 8)
                nc.gpsimd.affine_select(out=ident_b[:], in_=ident_b[:], compare_op=ALU.not_equal, fill=1.0, base=-P,
                                        pattern=[[0, P]], channel_multiplier=1).then_inc(consts, 1)
                pool.wait_ge(equal, 1)
                nc.gpsimd.affine_select(out=carry_f[:], in_=carry_f[:], compare_op=ALU.is_gt, fill=0.0, base=0,
                                        pattern=[[1, P]], channel_multiplier=-1).then_inc(upper, 1)

            @block.sync
            def _(sp):
                rows = a["dst"].rearrange("(p t) -> p t", p=P)
                sp.dma_start(self.src_i[:], a["src"].rearrange("(p t) -> p t", p=P)).then_inc(loaded, 16)
                sp.dma_start(self.dst_i[:], rows).then_inc(loaded, 16)
                sp.wait_ge(frame, 1)
                sp.dma_start(dpad[:, 1:T + 1], rows).then_inc(loaded, 16)
                with nc.allow_non_contiguous_dma(reason="one index of each row"):
                    sp.dma_start(dpad[1:P, 0:1], rows[0:P - 1, T - 1:T]).then_inc(loaded, 16)
                    sp.dma_start(dpad[0:P - 1, T + 1:T + 2], rows[1:P, 0:1]).then_inc(loaded, 16)
                sp.wait_ge(loaded, 80)

            @block.vector
            def _(dve):
                V, ch = nc.vector, Chain(dve, own)
                dve.wait_ge(loaded, 80)
                ch(V.tensor_copy(df[:], dpad[:]))
                mine, prev, nxt = df[:, 1:T + 1], df[:, 0:T], df[:, 2:T + 2]
                ch(V.tensor_tensor(same_prev[:], mine, prev, ALU.is_equal),
                   V.tensor_tensor(same_next[:], mine, nxt, ALU.is_equal),
                   V.tensor_tensor(last[:], mine, nxt, ALU.not_equal))
                ch(V.tensor_copy(in_row[:], same_prev[:]),
                   V.tensor_scalar(self.pen_prev[:], same_prev[:], -1.0, BIG, ALU.add, ALU.mult),
                   V.tensor_scalar(self.pen_next[:], same_next[:], -1.0, BIG, ALU.add, ALU.mult),
                   V.tensor_scalar(put_f[:], last[:], -1.0, -SKIP, ALU.add, ALU.mult))
                ch(V.memset(in_row[:, 0:1], 0.0),
                   V.tensor_tensor(put_f[:], put_f[:], mine, ALU.add))
                ch(V.tensor_copy(self.put_i[:], put_f[:]),
                   V.tensor_tensor(fix[:, 0:1], df[:, 1:2], df[:, T + 1:T + 2], ALU.not_equal))
                ch(V.tensor_tensor(fix[:, 1:2], fix[:, 0:1], same_prev[:, 0:1], ALU.mult))
                ch(V.tensor_scalar(fix[:, 2:3], fix[:, 1:2], -1.0, -SKIP, ALU.add, ALU.mult))
                ch(V.tensor_tensor(fix[:, 3:4], fix[:, 2:3], df[:, 1:2], ALU.add))
                ch(V.tensor_copy(self.fix_i[:], fix[:, 3:4]))
                dve.wait_ge(consts, 9)
                V.tensor_scalar(diag[:], ident[0:P, 0:P], df[:, 1:2], None, ALU.mult).then_inc(diag_done, 1)
                dve.wait_ge(first_done, 1)
                V.tensor_scalar(carry_f[:], ps_first[:], df[:, T:T + 1], None, ALU.is_equal).then_inc(equal, 1)
                dve.wait_ge(upper, 1)
                dve.wait_ge(turned, 1)
                ch(V.tensor_copy(carry_b[:], ps_tr[:]))
                ch(V.tensor_scalar(self.pen_cf[:], carry_b[:], -1.0, BIG, ALU.add, ALU.mult),
                   V.tensor_scalar(self.pen_cb[:], carry_f[:], -1.0, BIG, ALU.add, ALU.mult))

            @block.tensor
            def _(pe):
                pe.wait_ge(consts, 9)
                pe.wait_ge(diag_done, 1)
                nc.tensor.matmul(ps_first[:], ones[:], diag[:], start=True, stop=True).then_inc(first_done, 1)
                pe.wait_ge(upper, 1)
                nc.tensor.transpose(ps_tr[:], carry_f[:], ident[0:P, 0:P]).then_inc(turned, 1)

    def running_sum(self, dve, st, ro, msg, msg_slot, put, summed):
        slot = st.slot(ER)
        st.sent(dve, put, 16 * G)
        for k in range(G):
            before = ro[:, slot, k - 1, 0:D] if k else ro[:, (slot - 1) % ER, G - 1, 0:D]
            if k or st.has(1):
                dve.wait_ge(summed, st.j * G + k)
            self.nc.vector.scalar_tensor_tensor(
                out=ro[:, slot, k, 0:D], in0=before, scalar=self.in_row[:, bass.ds(st.j * G + k, 1)],
                in1=msg[:, msg_slot, k, :], op0=ALU.mult, op1=ALU.add).then_inc(summed, 1)

    def scatter(self, pool, st, cols, ro, dst, put, copied, go, waits):
        slot = st.slot(ER)
        if st.has(ER):
            st.sent(pool, put, 16 * G)
            pool.sem_inc(go, 1)
        self.nc.gpsimd.tensor_copy(cols[:, slot], self.put_i[:, bass.ds(st.j * G, G)]).then_inc(copied, 1)
        st.ready(pool, copied)
        pool.sem_inc(go, 1)
        for s, per in waits:
            st.ready(pool, s, per)
            pool.sem_inc(go, 1)
        for k in range(G):
            self.nc.gpsimd.indirect_dma_start(
                dst, bass.IndirectOffsetOnAxis(cols[:, slot, k:k + 1], 0), ro[:, slot, k, :], None,
                bounds_check=N_NODES - 1, oob_is_err=False).then_inc(put[slot], 16)

    def carry_fix(self, l, ro, dst, width):
        nc = self.nc
        with ExitStack() as ctx:
            rows = self.sb(ctx, f"c{l}_rows", [P, width])
            ps_c = self.ps(ctx, f"c{l}_ps", [P, D])
            blank, got, summed, fixed, back = (self.sem(f"c{l}_" + n) for n in ("blank", "got", "summed", "fixed", "back"))
            block = ctx.enter_context(nc.Block())

            @block.tensor
            def _(pe):
                nc.tensor.matmul(ps_c[:], self.carry_f[:], ro[:, ER - 1, G - 1, 0:D], start=True, stop=True).then_inc(summed, 1)

            @block.gpsimd
            def _(pool):
                nc.gpsimd.memset(rows[:], 0.0).then_inc(blank, 1)
                pool.wait_ge(blank, 1)
                nc.gpsimd.indirect_dma_start(rows[:], None, dst, bass.IndirectOffsetOnAxis(self.fix_i[:, 0:1], 0),
                                             bounds_check=N_NODES - 1, oob_is_err=False).then_inc(got, 16)
                pool.wait_ge(fixed, 1)
                nc.gpsimd.indirect_dma_start(dst, bass.IndirectOffsetOnAxis(self.fix_i[:, 0:1], 0), rows[:], None,
                                             bounds_check=N_NODES - 1, oob_is_err=False).then_inc(back, 16)
                pool.wait_ge(back, 16)

            @block.vector
            def _(dve):
                dve.wait_ge(got, 16)
                dve.wait_ge(summed, 1)
                nc.vector.tensor_tensor(rows[:, 0:D], rows[:, 0:D], ps_c[:], ALU.add).then_inc(fixed, 1)

    def edge_pass(self, l, ctx, keep=None, S=None, SS=None, mk=None, w3s=None, wself=None, rel_w=None):
        nc, a, sem = self.nc, self.a, self.sem
        x_in, ident, pre = self.x[l], self.ident, f"e{l}_"
        sb = lambda c, name, shape, dt=F32: self.sb(c, pre + name, shape, dt)
        cols = {0: 256, 1: 256, 2: 384, 3: 408}[l]
        hold = 2 if cols <= 256 else 1
        nv = {0: 0, 1: 2, 2: 4, 3: 12}[l]
        fill, self.filled = not self.filled, True
        Z = NT // ESTEPS
        with ExitStack() as c2:
            xs, xd = sb(c2, "xs", [P, ER, G, D]), sb(c2, "xd", [P, ER, G, D])
            ixs, ixd = sb(c2, "ixs", [P, ER, G], I32), sb(c2, "ixd", [P, ER, G], I32)
            xsT, xdT = sb(c2, "xsT", [128, ER, G, P]), sb(c2, "xdT", [128, ER, G, P])
            ws, wd = sb(c2, "ws", [D, cols]), sb(c2, "wd", [D, D])
            brow = sb(c2, "brow", [128, cols])
            t1, t2 = sb(c2, "t1", [P, ER, G, D]), sb(c2, "t2", [P, ER, G, D])
            ps_s, ps_d = self.ps(c2, pre + "ps_s", [128, G, 128]), self.ps(c2, pre + "ps_d", [128, G, 128])
            ps_h = [self.ps(c2, pre + f"ps_h{k}", [128, 512]) for k in range(4)]
            weights, weights_done, own = sem(pre + "weights"), sem(pre + "weights_done"), sem(pre + "own")
            copied, go = sem(pre + "copied"), sem(pre + "go")
            got = [sem(pre + f"got{k}") for k in range(ER)]
            tr_s, tr_d, ev_s, ev_d = (sem(pre + n) for n in ("tr_s", "tr_d", "ev_s", "ev_d"))
            prod, act_done, vec_done, reduced = (sem(pre + n) for n in ("prod", "act", "vec", "reduced"))
            if fill:
                zero, zero3 = sb(c2, "zero", [P, Z, D]), sb(c2, "zero3", [P, Z, W3])
                fills, filled = sem(pre + "fills"), sem(pre + "filled")
            if l == 1:
                ea, eaT = sb(c2, "ea", [P, ER, G, D]), sb(c2, "eaT", [128, ER, G, P])
                we, b3 = sb(c2, "we", [D, D]), sb(c2, "b3", [128, 3, D])
                ps_e = self.ps(c2, pre + "ps_e", [128, G, 128])
                got_e = [sem(pre + f"got_e{k}") for k in range(ER)]
                tr_e, ev_e, summed, pcopied = sem(pre + "tr_e"), sem(pre + "ev_e"), sem(pre + "summed"), sem(pre + "pcopied")
                put = [sem(pre + f"put{k}") for k in range(ER)]
                pcols = sb(c2, "pcols", [P, ER, G], I32)
                ro = sb(c2, "ro", [P, ER, G, D])
            if l == 0:
                attn_row = sb(c2, "attn", [P, D])
                vec_done0 = sem(pre + "vec0")
            if l == 3:
                w3, pr3 = sb(c2, "w3", [D, 3, D]), sb(c2, "pr3", [D, 3 * D])
                att_s, att_d = sb(c2, "att_s", [D, 3 * D]), sb(c2, "att_d", [D, 3 * D])
                rel = sb(c2, "rel", [D, 12])
                exped, neg_max = sem(pre + "exped"), sem(pre + "neg_max")

            def bank(st, k):
                if hold == 2:
                    return ps_h[2 * st.slot(2) + k // 2][0:P, 256 * (k % 2):256 * (k % 2) + cols]
                return ps_h[k][0:P, 0:cols]

            def units(st):
                if hold == 2:
                    return [(2 * h, 2, ps_h[2 * st.slot(2) + h][0:P, :].rearrange("p (k c) -> p k c", k=2)) for h in range(2)]
                return [(k, 1, ps_h[k][0:P, :].rearrange("p (k c) -> p k c", k=1)) for k in range(G)]

            W = {0: [(ws[:, 0:D], a["L0_gnn_W_src"]), (ws[:, D:2 * D], a["L0_gnn_W_src"]), (wd[:], a["L0_gnn_W_dst"])],
                 1: [(ws[:, 0:D], a["L1_gnn_WB"]), (ws[:, D:2 * D], a["L1_gnn_WA"]), (wd[:], a["L1_gnn_WC"])],
                 2: [(ws[:, 0:D], a["L2_gnn_Wk"]), (ws[:, D:2 * D], a["L2_gnn_Wv"]), (wd[:], a["L2_gnn_Wq"])],
                 3: []}[l]
            if l == 0:
                W += [(attn_row[:], rows_of(a["L0_gnn_attn"].rearrange("h d -> (h d)"), P))]
            if l == 1:
                W += [(we[:], a["L1_gnn_WE"]), (brow[:, D:2 * D], rows_of(a["L1_gnn_bA"], 128))]
                W += [(b3[:, k, :], rows_of(a["L1_gnn_b" + n], 128)) for k, n in enumerate("BCE")]
            if l == 2:
                W += [(brow[:, k * D:k * D + D], rows_of(a["L2_gnn_b" + n], 128)) for k, n in enumerate("kvq")]
            if l == 3:
                W += [(w3[:], a["L3_gnn_W"].rearrange("r i o -> i r o")), (rel[:, 0:3], rows_of(a["L3_gnn_rel_w"], D)),
                      (att_s[:], rows_of(a["L3_gnn_att_src"].rearrange("r h c -> (r h c)"), D)),
                      (att_d[:], rows_of(a["L3_gnn_att_dst"].rearrange("r h c -> (r h c)"), D))]
            with ExitStack() as c3:
                block = c3.enter_context(nc.Block())

                @block.sync
                def _(sp):
                    for to, of in W:
                        sp.dma_start(to, of).then_inc(weights, 16)
                    if fill:
                        sp.wait_ge(fills, 3)
                        agg = self.agg.rearrange("(p n) d -> p n d", p=P)
                        agg3 = self.agg3.rearrange("(p n) d -> p n d", p=P)

                        def fill_rows(st):
                            st.freed(sp, tr_s, 1)
                            nodes = bass.ds(st.j * Z, Z)
                            load_rows(sp, agg[:, nodes, :], zero[:], filled)
                            load_rows(sp, agg3[:, nodes, :], zero3[:], filled)

                        pipeline(sp, ESTEPS, ER, [(0, fill_rows)])
                        sp.wait_ge(filled, 64 * ESTEPS)
                    if l == 1:
                        ea_v = a["edge_attr_128"].rearrange("(p t) d -> p t d", p=P)

                        def load(st):
                            st.freed(sp, tr_e, ER)
                            load_rows(sp, ea[:, st.slot(ER)], ea_v[:, bass.ds(st.j * G, G), :], got_e[st.slot(ER)])

                        pipeline(sp, ESTEPS, ER, [(0, load)])

                @block.gpsimd
                def _(pool):
                    def gather(st):
                        slot = st.slot(ER)
                        if st.has(ER):
                            st.sent(pool, got, 32 * G)
                            pool.sem_inc(go, 1)
                            st.freed(pool, tr_s, ER)
                            pool.sem_inc(go, 1)
                            st.freed(pool, tr_d, ER)
                            pool.sem_inc(go, 1)
                        nc.gpsimd.tensor_copy(ixs[:, slot], self.src_i[:, bass.ds(st.j * G, G)]).then_inc(copied, 1)
                        nc.gpsimd.tensor_copy(ixd[:, slot], self.dst_i[:, bass.ds(st.j * G, G)]).then_inc(copied, 1)
                        st.ready(pool, copied, 2)
                        pool.sem_inc(go, 1)
                        for k in range(G):
                            for rows, ix in ((xs, ixs), (xd, ixd)):
                                nc.gpsimd.indirect_dma_start(
                                    rows[:, slot, k, :], None, x_in,
                                    bass.IndirectOffsetOnAxis(ix[:, slot, k:k + 1], 0)).then_inc(got[slot], 16)

                    stages = [(0, gather)]
                    if l == 1:
                        stages.append((2, lambda st: self.scatter(pool, st, pcols, ro, self.agg, put, pcopied, go, [(summed, G)])))
                    pipeline(pool, ESTEPS, ER, stages)
                    if l == 1:
                        for k in range(ER):
                            pool.wait_ge(put[k], 16 * G * (ESTEPS // ER))

                @block.tensor
                def _(pe):
                    kw = dict(skip_group_check=True)

                    def transposes(st):
                        slot = st.slot(ER)
                        st.arrived(pe, got, 32 * G)
                        st.freed(pe, ev_s, 1)
                        for k in range(G):
                            i = nc.tensor.transpose(ps_s[:, k, 0:P], xs[:, slot, k, :], ident[0:P, 0:P])
                        i.then_inc(tr_s, 1)
                        st.freed(pe, ev_d, 1)
                        for k in range(G):
                            i = nc.tensor.transpose(ps_d[:, k, 0:P], xd[:, slot, k, :], ident[0:P, 0:P])
                        i.then_inc(tr_d, 1)
                        if l == 1:
                            st.arrived(pe, got_e, 32)
                            st.freed(pe, ev_e, 1)
                            for k in range(G):
                                i = nc.tensor.transpose(ps_e[:, k, 0:P], ea[:, slot, k, :], ident[0:P, 0:P])
                            i.then_inc(tr_e, 1)

                    def products(st):
                        slot, mm = st.slot(ER), nc.tensor.matmul
                        st.ready(pe, ev_s)
                        st.ready(pe, ev_d)
                        if l == 1:
                            st.ready(pe, ev_e)
                        if l == 0:
                            st.freed(pe, act_done, hold)
                        else:
                            st.freed(pe, vec_done, hold, nv)
                        for k in range(G):
                            o, src_t, dst_t = bank(st, k), xsT[:, slot, k, :], xdT[:, slot, k, :]
                            if l == 0:
                                mm(o[:, 0:2 * D], src_t, ws[:], start=True, stop=False, **kw)
                                i = mm(o[:, D:2 * D], dst_t, wd[:], start=False, stop=True, **kw)
                            if l == 1:
                                mm(o[:, 0:2 * D], self.e0[:], brow[:], start=True, stop=False, **kw)
                                mm(o[:, 0:2 * D], src_t, ws[:], start=False, stop=False, **kw)
                                mm(o[:, 0:D], dst_t, wd[:], start=False, stop=False, **kw)
                                i = mm(o[:, 0:D], eaT[:, slot, k, :], we[:], start=False, stop=True, **kw)
                            if l == 2:
                                mm(o[:, 0:3 * D], self.e0[:], brow[:], start=True, stop=False, **kw)
                                mm(o[:, 0:2 * D], src_t, ws[:, 0:2 * D], start=False, stop=False, **kw)
                                i = mm(o[:, 2 * D:3 * D], dst_t, wd[:], start=False, stop=True, **kw)
                            if l == 3:
                                mm(o[:, 0:408], src_t, ws[:], start=True, stop=False, **kw)
                                i = mm(o[:, 384:408], dst_t, wd[:, 0:24], start=False, stop=True, **kw)
                        i.then_inc(prod, 1)

                    pe.wait_ge(weights, 16 * len(W))
                    pe.wait_ge(weights_done, 1)
                    pipeline(pe, ESTEPS, ER, [(0, transposes), (1, products)])

                @block.scalar
                def _(act):
                    A = nc.scalar
                    if l == 3:
                        act.wait_ge(neg_max, 1)
                        A.activation(rel[:, 4:7], rel[:, 0:3], ACT.Exp, bias=rel[:, 3:4]).then_inc(exped, 1)

                    def evac(st):
                        st.freed(act, prod, ER)
                        st.ready(act, tr_s)
                        A.copy(xsT[:, st.slot(ER)], ps_s[:, :, 0:P]).then_inc(ev_s, 1)
                        if l == 1:
                            st.ready(act, tr_e)
                            A.copy(eaT[:, st.slot(ER)], ps_e[:, :, 0:P]).then_inc(ev_e, 1)

                    def use(st):
                        slot = st.slot(ER)
                        st.ready(act, prod)
                        if l == 0:
                            st.freed(act, vec_done0, ER, 2)
                        if l in (1, 2):
                            st.freed(act, vec_done, ER, nv)
                        for k, m, h in units(st):
                            tiles = bass.ds(st.j * G + k, m)
                            if l == 0:
                                A.activation(keep[:, tiles, :], h[:, :, 0:D], ACT.Copy)
                                i = A.activation(t1[:, slot, k:k + m, :], h[:, :, D:2 * D], ACT.Copy)
                            if l == 1:
                                i = A.activation(t1[:, slot, k:k + m, :], h[:, :, 0:D], ACT.Sigmoid)
                            if l == 2:
                                A.activation(keep[:, tiles, :], h[:, :, D:2 * D], ACT.Copy)
                                i = A.activation(t1[:, slot, k:k + m, :], h[:, :, 2 * D:3 * D], ACT.Copy)
                            if l == 3:
                                A.activation(S[:, tiles, :], h[:, :, 384:396], ACT.Copy)
                                i = A.activation(SS[:, tiles, :], h[:, :, 396:408], ACT.Copy)
                        i.then_inc(act_done, 1)

                    pipeline(act, ESTEPS, ER, [(0, evac), (1, use)])

                @block.vector
                def _(dve):
                    V, ch = nc.vector, Chain(dve, own)
                    if fill:
                        V.memset(zero[:], 0.0).then_inc(fills, 1)
                        V.memset(zero3[:, :, 0:D], 0.0).then_inc(fills, 1)
                        V.memset(zero3[:, :, D:W3], 1.0).then_inc(fills, 1)
                    dve.wait_ge(weights, 16 * len(W))
                    if l == 1:
                        ch(V.tensor_tensor(b3[:, 0, :], b3[:, 0, :], b3[:, 1, :], ALU.add))
                        ch(V.tensor_tensor(brow[:, 0:D], b3[:, 0, :], b3[:, 2, :], ALU.add),
                           V.memset(ro[:, ER - 1, G - 1, :], 0.0))
                    if l == 3:
                        w3f, heads = w3[:].rearrange("i r o -> i (r o)"), lambda t: t[:].rearrange("i (q c) -> i q c", c=32)
                        V.tensor_reduce(rel[:, 3:4], rel[:, 0:3], AX.X, ALU.max, negate=True).then_inc(neg_max, 1)
                        ch(V.tensor_tensor(pr3[:], w3f, att_s[:], ALU.mult))
                        ch(V.tensor_reduce(ws[:, 384:396], heads(pr3), AX.X, ALU.add))
                        ch(V.tensor_tensor(pr3[:], w3f, att_d[:], ALU.mult))
                        dve.wait_ge(exped, 1)
                        ch(V.tensor_reduce(wd[:, 0:12], heads(pr3), AX.X, ALU.add),
                           V.tensor_reduce(rel[:, 7:8], rel[:, 4:7], AX.X, ALU.add),
                           V.memset(ws[:, 396:408], 0.0))
                        ch(V.tensor_tensor(wd[:, 12:24], wd[:, 0:12], ws[:, 384:396], ALU.add),
                           V.reciprocal(rel[:, 8:9], rel[:, 7:8]))
                        ch(V.tensor_scalar(rel_w[:], rel[:, 4:7], rel[:, 8:9], None, ALU.mult))
                        ch(*[V.tensor_scalar(ws[:, D * r:D * r + D], w3[:, r, :], rel_w[:, r:r + 1], None, ALU.mult)
                             for r in range(3)])
                        ch(V.tensor_copy(w3s[:], ws[:, 0:3 * D]))
                    V.memset(t2[:, 0, 0, 0:1], 0.0).then_inc(weights_done, 1)
                    dve.wait_ge(weights_done, 1)

                    def evac(st):
                        st.freed(dve, prod, ER)
                        st.ready(dve, tr_d)
                        V.tensor_copy(xdT[:, st.slot(ER)], ps_d[:, :, 0:P]).then_inc(ev_d, 1)

                    def heads16(st):
                        V.tensor_reduce(S[:, bass.ds(st.j * G, G), :], t2[:, st.slot(ER)].rearrange("p k (h c) -> p k h c", c=16),
                                        AX.X, ALU.add).then_inc(reduced, 1)

                    def use0(st):
                        st.ready(dve, act_done)
                        st.freed(dve, reduced, ER)
                        slot = st.slot(ER)
                        V.scalar_tensor_tensor(out=t2[:, slot], in0=t1[:, slot], scalar=0.2, in1=t1[:, slot],
                                               op0=ALU.mult, op1=ALU.max).then_inc(vec_done0, 1)
                        dve.wait_ge(vec_done0, st.j * 2 + 1)
                        V.tensor_tensor(t2[:, slot], t2[:, slot], over_tiles(attn_row[:]), ALU.mult).then_inc(vec_done0, 1)
                        st.ready(dve, vec_done0, 2)
                        heads16(st)

                    def use1(st):
                        slot = st.slot(ER)
                        st.ready(dve, act_done)
                        st.freed(dve, summed, ER, G)
                        for k, m, h in units(st):
                            V.tensor_tensor(t2[:, slot, k:k + m, :], h[:, :, D:2 * D], t1[:, slot, k:k + m, :], ALU.mult).then_inc(vec_done, 1)
                        st.ready(dve, vec_done, nv)
                        self.running_sum(dve, st, ro, t2, slot, put, summed)

                    def use2(st):
                        slot = st.slot(ER)
                        st.ready(dve, act_done)
                        st.freed(dve, reduced, ER)
                        for k, m, h in units(st):
                            V.tensor_tensor(t2[:, slot, k, :], h[:, 0, 0:D], t1[:, slot, k, :], ALU.mult).then_inc(vec_done, 1)
                        st.ready(dve, vec_done, nv)
                        heads16(st)

                    def use3(st):
                        slot = st.slot(ER)
                        st.ready(dve, act_done)
                        for r in range(3):
                            if r or st.has(1):
                                dve.wait_ge(vec_done, st.j * nv + 4 * r)
                            for k, m, h in units(st):
                                own_rel, hr = mk[:, bass.ds(st.j * G + k, 1), r], h[:, 0, D * r:D * r + D]
                                if r == 0:
                                    i = V.tensor_scalar(t2[:, slot, k, :], hr, own_rel, None, ALU.mult)
                                elif r == 1:
                                    i = V.scalar_tensor_tensor(out=t1[:, slot, k, :], in0=hr, scalar=own_rel,
                                                               in1=t2[:, slot, k, :], op0=ALU.mult, op1=ALU.add)
                                else:
                                    to = keep[:, bass.ds(st.j * G + k, 1), :].rearrange("p a d -> p (a d)")
                                    i = V.scalar_tensor_tensor(out=to, in0=hr, scalar=own_rel,
                                                               in1=t1[:, slot, k, :], op0=ALU.mult, op1=ALU.add)
                                i.then_inc(vec_done, 1)

                    pipeline(dve, ESTEPS, ER, [(0, evac), (1, (use0, use1, use2, use3)[l])])
            if l == 1:
                self.carry_fix(l, ro, self.agg, D)

    def softmax(self, l, H, S, SS=None, scale=1.0, eps=0.0, mk=None, sel=None):
        nc, pre = self.nc, f"s{l}_"
        NB = H // 4
        with ExitStack() as ctx:
            sb = lambda name, shape: self.sb(ctx, pre + name, shape)
            F, B = sb("F", [P, T, H]), sb("B", [P, T, H])
            cf, cb = sb("cf", [P, H]), sb("cb", [P, H])
            diag = sb("diag", [P, 2, H, P])
            pen = sb("pen", [P, H, P])
            ps = [self.ps(ctx, pre + f"ps{k}", [P, 4, 128]) for k in range(2 * NB)]
            own, ready, spread, maxed, exped, ends, carried = (self.sem(pre + n) for n in ("own", "ready", "spread", "maxed", "exped", "ends", "carried"))
            if l == 3:
                nm = sb("nm", [P, T, 3])
            block = ctx.enter_context(nc.Block())

            @block.tensor
            def _(pe):
                pe.wait_ge(ready, 1)
                for d in range(2):
                    for b in range(NB):
                        i = nc.tensor.matmul(ps[d * NB + b][:, :, 0:P], self.ones[:], diag[:, d, 4 * b:4 * b + 4, :],
                                             start=True, stop=True)
                i.then_inc(spread, 1)
                pe.wait_ge(ends, 1)
                nc.tensor.matmul(ps[0][:, 0, 0:H], self.carry_f[:], F[:, T - 1, :], start=True, stop=True)
                nc.tensor.matmul(ps[1][:, 0, 0:H], self.carry_b[:], B[:, 0, :], start=True, stop=True).then_inc(carried, 1)

            @block.scalar
            def _(act):
                act.wait_ge(maxed, 1)
                i = nc.scalar.activation(S[:], S[:], ACT.Exp, scale=scale)
                if l == 3:
                    i = nc.scalar.activation(SS[:], SS[:], ACT.Exp)
                i.then_inc(exped, 1)

            @block.vector
            def _(dve):
                V, ch = nc.vector, Chain(dve, own)

                def scans(mult, combine, prev, nxt, init_f, init_b):
                    ops = []
                    for h in range(H):
                        i_f = init_f if isinstance(init_f, float) else init_f[:, h:h + 1]
                        i_b = init_b if isinstance(init_b, float) else init_b[:, h:h + 1]
                        ops.append(V.tensor_tensor_scan(F[:, :, h], prev[:], S[:, :, h], i_f, mult, combine))
                        ops.append(V.tensor_tensor_scan(B[:, ::-1, h], nxt[:, ::-1], S[:, ::-1, h], i_b, mult, combine))
                    ch(*ops)

                if l == 3:
                    ch(*[V.scalar_tensor_tensor(out=z[:], in0=z[:], scalar=0.2, in1=z[:], op0=ALU.mult, op1=ALU.max)
                         for z in (S, SS)])
                    s4 = S[:].rearrange("p t (r h) -> p t r h", h=4)
                    wide = lambda m: m[:].unsqueeze(3).to_broadcast([P, T, 3, 4])
                    ch(V.tensor_tensor(s4, s4, wide(mk), ALU.mult), V.tensor_scalar(nm[:], mk[:], -1.0, NEG, ALU.add, ALU.mult))
                    ch(V.tensor_tensor(s4, s4, wide(nm), ALU.add))
                scans(ALU.add, ALU.max, self.pen_prev, self.pen_next, -BIG, -BIG)
                idb = self.ident[0:P, 0:P].unsqueeze(1).to_broadcast([P, H, P])
                ch(V.tensor_tensor(diag[:, 0], idb, F[:, T - 1, :].unsqueeze(2).to_broadcast([P, H, P]), ALU.mult),
                   V.tensor_tensor(diag[:, 1], idb, B[:, 0, :].unsqueeze(2).to_broadcast([P, H, P]), ALU.mult))
                V.memset(cf[:], 0.0).then_inc(ready, 1)
                dve.wait_ge(ready, 1)
                dve.wait_ge(spread, 1)
                for d, (pc, c) in enumerate(((self.pen_cf, cf), (self.pen_cb, cb))):
                    ch(*[V.tensor_tensor(pen[:, 4 * b:4 * b + 4, :], ps[d * NB + b][:, :, 0:P],
                                         pc[:].unsqueeze(1).to_broadcast([P, 4, P]), ALU.add) for b in range(NB)])
                    ch(V.tensor_reduce(c[:], pen[:], AX.X, ALU.max))
                scans(ALU.add, ALU.max, self.pen_prev, self.pen_next, cf, cb)
                ch(V.tensor_tensor(F[:], F[:], B[:], ALU.max))
                if l == 3:
                    ch(V.tensor_tensor(F[:], F[:], SS[:], ALU.max))
                    ch(V.tensor_tensor(SS[:], SS[:], F[:], ALU.subtract))
                V.tensor_tensor(S[:], S[:], F[:], ALU.subtract).then_inc(maxed, 1)
                dve.wait_ge(exped, 1)
                scans(ALU.mult, ALU.add, self.same_prev, self.same_next, 0.0, 0.0)
                V.memset(pen[:, 0, 0:1], 0.0).then_inc(ends, 1)
                dve.wait_ge(ends, 1)
                dve.wait_ge(carried, 1)
                ch(V.tensor_copy(cf[:], ps[0][:, 0, 0:H]), V.tensor_copy(cb[:], ps[1][:, 0, 0:H]))
                scans(ALU.mult, ALU.add, self.same_prev, self.same_next, cf, cb)
                ch(V.tensor_tensor(F[:], F[:], B[:], ALU.add))
                ch(V.tensor_tensor(F[:], F[:], S[:], ALU.subtract))
                if l == 3:
                    ch(V.tensor_tensor(F[:], F[:], SS[:], ALU.add))
                else:
                    ch(V.tensor_scalar(F[:], F[:], eps, None, ALU.add))
                ch(V.reciprocal(B[:], F[:]))
                ch(V.tensor_tensor(S[:], S[:], B[:], ALU.mult))
                if l == 3:
                    ch(V.tensor_tensor(SS[:], SS[:], B[:], ALU.mult))
                    ch(V.tensor_tensor(s4, s4, wide(mk), ALU.mult))
                    ch(V.tensor_reduce(sel[:], S[:].rearrange("p t (r h) -> p t h r", h=4), AX.X, ALU.add))

    def message_pass(self, l, keep, weight, H, dst, width, SS=None):
        nc, pre = self.nc, f"m{l}_"
        with ExitStack() as ctx:
            sb = lambda name, shape, dt=F32: self.sb(ctx, pre + name, shape, dt)
            ro, msg = sb("ro", [P, ER, G, width]), sb("msg", [P, ER, G, D])
            pcols = sb("pcols", [P, ER, G], I32)
            made, summed, copied, go, selfs = (self.sem(pre + n) for n in ("made", "summed", "copied", "go", "selfs"))
            put = [self.sem(pre + f"put{k}") for k in range(ER)]
            with ExitStack() as c2:
                block = c2.enter_context(nc.Block())

                @block.vector
                def _(dve):
                    nc.vector.memset(ro[:, ER - 1, G - 1, 0:D], 0.0).then_inc(made, 1)
                    dve.wait_ge(made, 1)

                    def make(st):
                        tiles = bass.ds(st.j * G, G)
                        st.freed(dve, summed, ER, G)
                        nc.vector.tensor_tensor(msg[:, st.slot(ER)].rearrange("p k (h c) -> p k h c", h=H),
                                                keep[:, tiles, :].rearrange("p k (h c) -> p k h c", h=H),
                                                weight[:, tiles, :].unsqueeze(3).to_broadcast([P, G, H, D // H]),
                                                ALU.mult).then_inc(made, 1)

                    def add(st):
                        dve.wait_ge(made, st.j + 2)
                        self.running_sum(dve, st, ro, msg, st.slot(ER), put, summed)

                    pipeline(dve, ESTEPS, ER, [(0, make), (1, add)])

                if l == 3:
                    @block.scalar
                    def _(act):
                        def self_weights(st):
                            st.sent(act, put, 16 * G)
                            nc.scalar.copy(ro[:, st.slot(ER), :, D:W3], SS[:, bass.ds(st.j * G, G), :]).then_inc(selfs, 1)

                        pipeline(act, ESTEPS, ER, [(0, self_weights)])

                @block.gpsimd
                def _(pool):
                    waits = [(summed, G)] + [(selfs, 1)] * (l == 3)
                    pipeline(pool, ESTEPS, ER, [(0, lambda st: self.scatter(pool, st, pcols, ro, dst, put, copied, go, waits))])
                    for k in range(ER):
                        pool.wait_ge(put[k], 16 * G * (ESTEPS // ER))
            self.carry_fix(l, ro, dst, width)

    def attention_layer(self, l):
        H = {0: 8, 2: 8, 3: 12}[l]
        nc = self.nc
        with ExitStack() as ctx:
            keep = self.sb(ctx, f"keep{l}", [P, T, D])
            S = self.sb(ctx, f"S{l}", [P, T, H])
            if l != 3:
                self.edge_pass(l, ctx, keep, S)
                self.softmax(l, H, S, scale=(1.0, None, 0.25)[l], eps=(1e-8, None, 1e-16)[l])
                self.message_pass(l, keep, S, H, self.agg, D)
                return
            SS = self.sb(ctx, "SS3", [P, T, H])
            mk = self.sb(ctx, "mk3", [P, T, 3])
            sel = self.sb(ctx, "sel3", [P, T, 4])
            with ExitStack() as c2:
                ty_i, ty = self.sb(c2, "ty_i", [P, T], I32), self.sb(c2, "ty", [P, T])
                loaded, own = self.sem("r_loaded"), self.sem("r_own")
                block = c2.enter_context(nc.Block())

                @block.sync
                def _(sp):
                    sp.dma_start(ty_i[:], self.a["edge_type_3"].rearrange("(p t) -> p t", p=P)).then_inc(loaded, 16)

                @block.vector
                def _(dve):
                    ch = Chain(dve, own)
                    dve.wait_ge(loaded, 16)
                    ch(nc.vector.tensor_copy(ty[:], ty_i[:]))
                    ch(*[nc.vector.tensor_scalar(mk[:, :, r], ty[:], float(r), None, ALU.is_equal) for r in range(3)])
            self.edge_pass(3, ctx, keep, S, SS, mk, self.w3s, None, self.rel_w)
            self.softmax(3, H, S, SS, mk=mk, sel=sel)
            self.message_pass(3, keep, sel, 4, self.agg3, W3, SS)

    def node_io(self, ctx, pre, l, agg, width):
        b, ring = self, NR
        x, s = b.sb(ctx, pre + "x", [P + 1, ring, G, D]), b.sb(ctx, pre + "s", [P + 1, ring, G, width])
        got = [b.sem(pre + f"got{k}") for k in range(ring // 2)]
        put = [b.sem(pre + f"put{k}") for k in range(ring // 2)]
        x_v, s_v, o_v = (t.rearrange("(p n) d -> p n d", p=P) for t in (b.x[l], agg, b.x[l + 1]))

        tiles = lambda t, slot: t.rearrange("p r g d -> p (r g) d")[:, slot * G:(slot + 2) * G]

        def load(sp, st, readers):
            if st.q % 2:
                return
            slot, nodes = st.slot(ring), bass.ds(st.j * G, 2 * G)
            if st.has(ring):
                for read, per in readers:
                    sp.wait_ge(read, (st.j + 2 - ring) * per)
            load_rows(sp, tiles(x, slot), x_v[:, nodes, :], got[slot // 2])
            load_rows(sp, tiles(s, slot), s_v[:, nodes, :], got[slot // 2])

        def store(sp, st, o, ready):
            if st.q % 2:
                st.ready(sp, ready)
                slot = st.slot(ring) - 1
                load_rows(sp, o_v[:, bass.ds(st.j * G - G, 2 * G), :], tiles(o, slot), put[slot // 2])

        def finish(sp):
            for sem in put:
                sp.wait_ge(sem, 32 * (NSTEPS // ring))

        return x, s, got, put, load, store, finish

    def bias_row(self, sp, loaded, ring, v):
        n = ring.shape[1] * G
        sp.dma_start(ring[P:P + 1].rearrange("p r g d -> p (r g) d"), rows_of(v, n).unsqueeze(0)).then_inc(loaded, 16)

    def load_consts(self, sp, loaded, pairs):
        for to, of in pairs:
            sp.dma_start(to, of).then_inc(loaded, 16)

    def nodes_simple(self, l):
        nc, a, pre, R = self.nc, self.a, f"n{l}_", NR
        with ExitStack() as ctx:
            sb = lambda name, shape: self.sb(ctx, pre + name, shape)
            x, s, got, put, load, store, finish = self.node_io(ctx, pre, l, self.agg, D)
            w, rows = sb("w", [D, D]), sb("rows", [P, 2, D])
            aT, y1, t, u, g, o = sb("aT", [128, 2, G, P]), *(sb(n, [P, MR, G, D]) for n in ("y1", "t", "u", "g")), sb("o", [P, R, G, D])
            ps_t = [self.ps(ctx, pre + f"ps_t{k}", [128, G, 128]) for k in range(2)]
            ps_o = [self.ps(ctx, pre + f"ps_o{k}", [128, G, 128]) for k in range(MR)]
            loaded, tr, ev, mm, side, usum, scaled, go = (self.sem(pre + n) for n in
                                                          ("loaded", "tr", "ev", "mm", "side", "usum", "scaled", "go"))
            ln1 = LayerNorm(self, ctx, pre + "ln1") if l == 0 else None
            ln2 = LayerNorm(self, ctx, pre + "ln2")
            W, bias = ("L0_gnn_W_out", "L0_gnn_b_out") if l == 0 else ("L1_gnn_Wres", "L1_gnn_bres")
            n_const = 16 * (4 if l == 0 else 2)
            fed, other = (s, x) if l == 0 else (x, s)
            block = ctx.enter_context(nc.Block())

            @block.sync
            def _(sp):
                self.load_consts(sp, loaded, [(w[:], a[W])])
                self.bias_row(sp, loaded, other, a[bias])
                if l == 0:
                    self.load_consts(sp, loaded, [(rows[:, 0, :], rows_of(a["L0_gnn_gamma"], P)), (rows[:, 1, :], rows_of(a["L0_gnn_beta"], P))])
                pipeline(sp, NSTEPS, R, [(0, lambda st: load(sp, st, [(mm, 1), (side if l == 0 else usum, 1)])),
                                         (12 if l == 0 else 8, lambda st: store(sp, st, o, ln2.scaled))])
                finish(sp)

            @block.tensor
            def _(pe):
                def transposes(st):
                    st.pair_arrived(pe, got)
                    st.freed(pe, ev, 2)
                    for k in range(G):
                        i = nc.tensor.transpose(ps_t[st.slot(2)][:, k, 0:P], fed[0:P, st.slot(R), k, :], self.ident[0:P, 0:P])
                    i.then_inc(tr, 1)

                def products(st):
                    st.ready(pe, ev)
                    st.freed(pe, ln1.scaled if l == 0 else usum, MR)
                    bank = ps_o[st.slot(MR)]
                    nc.tensor.matmul(bank[0:P], self.ident_b[:], other[:, st.slot(R)], start=True, stop=False, skip_group_check=True)
                    for k in range(G):
                        i = nc.tensor.matmul(bank[0:P, k, :], aT[:, st.slot(2), k, :], w[:],
                                             start=False, stop=(k == G - 1), skip_group_check=True)
                    i.then_inc(mm, 1)

                pe.wait_ge(loaded, n_const)
                pipeline(pe, NSTEPS, R, [(0, transposes), (1, products)])

            @block.scalar
            def _(act):
                def evac(st):
                    st.ready(act, tr)
                    st.freed(act, mm, 2)
                    nc.scalar.copy(aT[:, st.slot(2)], ps_t[st.slot(2)][:, :, 0:P]).then_inc(ev, 1)

                def scale1(st):
                    st.freed(act, scaled, MR)
                    ln1.scale(act, st, ps_o[st.slot(MR)][0:P], u[:, st.slot(MR)])

                def scale2(st):
                    st.pair_sent(act, put)
                    ln2.scale(act, st, t[:, st.slot(MR)], o[:, st.slot(R)])

                if l == 0:
                    stages = [(3, lambda st: ln1.root(act, st)), (7, lambda st: ln2.root(act, st)), (0, evac), (4, scale1), (8, scale2)]
                else:
                    stages = [(3, lambda st: ln2.root(act, st)), (0, evac), (4, scale2)]
                pipeline(act, NSTEPS, R, stages)

            if l == 0:
                @block.gpsimd
                def _(pool):
                    def x_beta(st):
                        wait_pool(pool, go, lambda: st.pair_arrived(pool, got))
                        if st.has(MR):
                            wait_pool(pool, go, lambda: st.freed(pool, usum, MR))
                        nc.gpsimd.tensor_tensor(y1[:, st.slot(MR)], x[0:P, st.slot(R)], over_tiles(rows[:, 1, :]), ALU.add).then_inc(side, 1)

                    def gamma(st):
                        wait_pool(pool, go, lambda: st.ready(pool, ln1.scaled))
                        if st.has(MR):
                            wait_pool(pool, go, lambda: st.freed(pool, usum, MR))
                        nc.gpsimd.tensor_tensor(g[:, st.slot(MR)], u[:, st.slot(MR)], over_tiles(rows[:, 0, :]), ALU.mult).then_inc(scaled, 1)

                    wait_pool(pool, go, lambda: pool.wait_ge(loaded, n_const))
                    pipeline(pool, NSTEPS, R, [(2, x_beta), (5, gamma)])

            @block.vector
            def _(dve):
                V = nc.vector

                def stats1(st):
                    st.ready(dve, mm)
                    ln1.stats(dve, st, ps_o[st.slot(MR)][0:P])

                def add2(st):
                    slot = st.slot(MR)
                    st.freed(dve, ln2.scaled, MR)
                    if l == 0:
                        st.ready(dve, scaled)
                        st.ready(dve, side)
                        V.tensor_tensor(t[:, slot], g[:, slot], y1[:, slot], ALU.add).then_inc(usum, 1)
                    else:
                        st.ready(dve, mm)
                        V.scalar_tensor_tensor(out=t[:, slot], in0=ps_o[st.slot(MR)][0:P], scalar=0.0, in1=x[0:P, st.slot(R)],
                                               op0=ALU.max, op1=ALU.add).then_inc(usum, 1)

                def stats2(st):
                    st.ready(dve, usum)
                    ln2.stats(dve, st, t[:, st.slot(MR)])

                if l == 0:
                    stages = [(6, add2), (2, stats1), (6, stats2), (7, lambda st: ln2.inverse(dve, st)), (3, lambda st: ln1.inverse(dve, st)),
                              (7, lambda st: ln2.negated(dve, st)), (3, lambda st: ln1.negated(dve, st)),
                              (2, lambda st: ln1.aggregate(dve, st)), (6, lambda st: ln2.aggregate(dve, st))]
                else:
                    stages = [(2, add2), (3, lambda st: ln2.inverse(dve, st)), (2, stats2),
                              (3, lambda st: ln2.negated(dve, st)), (2, lambda st: ln2.aggregate(dve, st))]
                pipeline(dve, NSTEPS, R, stages)

    def nodes_transformer(self):
        nc, a, pre, l, R = self.nc, self.a, "n2_", 2, NR
        F = 4
        with ExitStack() as ctx:
            sb = lambda name, ring, rows=P, cols=D: self.sb(ctx, pre + name, [rows, ring, G, cols])
            x, s, got, put, load, store, finish = self.node_io(ctx, pre, l, self.agg, D)
            wo, w1, w2 = (self.sb(ctx, pre + n, shape) for n, shape in (("wo", [D, D]), ("w1", [D, F * D]), ("w2", [D, F, D])))
            rows, b1 = self.sb(ctx, pre + "rows", [P, 6, D]), self.sb(ctx, pre + "b1", [D, F])
            aT, hT = sb("aT", 2, 128, P), sb("hT", 2, 128, P)
            hid = self.sb(ctx, pre + "hid", [128, 2, F, G, P])
            y0, n1, h0, h, n2, g2 = (sb(n, 2) for n in ("y0", "n1", "h0", "h", "n2", "g2"))
            t, y1, v, wv = (sb(n, MR) for n in ("t", "y1", "v", "wv"))
            y2, o = sb("y2", R), sb("o", R)
            ps_t, ps_h, ps_o, ps_v = (self.ps(ctx, pre + n, [128, G, 128]) for n in ("ps_t", "ps_h", "ps_o", "ps_v"))
            ps_f = [self.ps(ctx, pre + f"ps_f{k}", [128, G, P]) for k in range(F)]
            loaded, tr, ev, mm, side, tsum = (self.sem(pre + n) for n in ("loaded", "tr", "ev", "mm", "side", "tsum"))
            hg, hb, trh, evh, f1, relu, f2, side2, vsum, g2d, side3, wsum, go = (self.sem(pre + n) for n in (
                "hg", "hb", "trh", "evh", "f1", "relu", "f2", "side2", "vsum", "g2d", "side3", "wsum", "go"))
            ln1 = LayerNorm(self, ctx, pre + "ln1", on_vector=True)
            ln2, ln3 = LayerNorm(self, ctx, pre + "ln2"), LayerNorm(self, ctx, pre + "ln3")
            vecs = ("bo", "ln1_g", "ln1_b", "b2", "ln2_g", "ln2_b")
            consts = [(wo[:], a["L2_gnn_Wo"]), (w1[:], a["L2_gnn_W1"]), (w2[:], a["L2_gnn_W2"].rearrange("(f i) o -> i f o", f=F))]
            consts += [(rows[:, k, :], rows_of(a["L2_gnn_" + n], P)) for k, n in enumerate(vecs)]
            n_const = 16 * (len(consts) + 1)
            row = lambda n: over_tiles(rows[:, vecs.index(n), :])
            block = ctx.enter_context(nc.Block())

            @block.sync
            def _(sp):
                self.load_consts(sp, loaded, consts)
                with nc.allow_non_contiguous_dma(reason="512 biases, one a partition and chunk"):
                    sp.dma_start(b1[:], a["L2_gnn_b1"].rearrange("(f i) -> i f", f=F)).then_inc(loaded, 16)
                pipeline(sp, NSTEPS, R, [(0, lambda st: load(sp, st, [(tr, 1), (side, 1), (side3, 1)])),
                                         (19, lambda st: store(sp, st, o, ln3.scaled))])
                finish(sp)

            @block.tensor
            def _(pe):
                def turn(bank, tiles, done):
                    for k in range(G):
                        i = nc.tensor.transpose(bank[:, k, 0:P], tiles[:, k, :], self.ident[0:P, 0:P])
                    i.then_inc(done, 1)

                def turn_sums(st):
                    st.pair_arrived(pe, got)
                    st.freed(pe, ev, 1)
                    turn(ps_t, s[0:P, st.slot(R)], tr)

                def out_product(st):
                    st.ready(pe, ev)
                    st.freed(pe, tsum, 1)
                    for k in range(G):
                        i = nc.tensor.matmul(ps_o[0:P, k, :], aT[:, st.slot(2), k, :], wo[:], start=True, stop=True, skip_group_check=True)
                    i.then_inc(mm, 1)

                def turn_h(st):
                    st.ready(pe, hb)
                    st.freed(pe, evh, 1)
                    turn(ps_h, h[:, st.slot(2)], trh)

                def up(st):
                    st.ready(pe, evh)
                    for f in range(F):
                        if st.has(1):
                            pe.wait_ge(relu, st.j * F - (F - 1 - f))
                        nc.tensor.matmul(ps_f[f][:], w1[:, f * D:f * D + D], hT[:, st.slot(2)], start=True, stop=True).then_inc(f1, 1)

                def down(st):
                    st.ready(pe, relu, F)
                    st.freed(pe, vsum, 1)
                    for k in range(G):
                        for f in range(F):
                            i = nc.tensor.matmul(ps_v[0:P, k, :], hid[:, st.slot(2), f, k, :], w2[:, f, :],
                                                 start=(f == 0), stop=(f == F - 1), skip_group_check=True)
                    i.then_inc(f2, 1)

                pe.wait_ge(loaded, n_const)
                pipeline(pe, NSTEPS, R, [(0, turn_sums), (7, turn_h), (9, down), (1, out_product), (8, up)])

            @block.scalar
            def _(act):
                def evac(st):
                    st.ready(act, tr)
                    st.freed(act, mm, 2)
                    nc.scalar.copy(aT[:, st.slot(2)], ps_t[:, :, 0:P]).then_inc(ev, 1)

                def evac_h(st):
                    st.ready(act, trh)
                    st.freed(act, f1, 2, F)
                    nc.scalar.copy(hT[:, st.slot(2)], ps_h[:, :, 0:P]).then_inc(evh, 1)

                def relus(st):
                    st.freed(act, f2, 2)
                    for f in range(F):
                        act.wait_ge(f1, st.j * F + f + 1)
                        nc.scalar.activation(hid[:, st.slot(2), f], ps_f[f][:], ACT.Relu, bias=b1[:, f:f + 1]).then_inc(relu, 1)

                def scale2(st):
                    st.freed(act, g2d, 2)
                    ln2.scale(act, st, v[:, st.slot(MR)], n2[:, st.slot(2)])

                def scale3(st):
                    st.pair_sent(act, put)
                    ln3.scale(act, st, wv[:, st.slot(MR)], o[:, st.slot(R)])

                pipeline(act, NSTEPS, R, [(3, lambda st: ln1.root(act, st)), (11, lambda st: ln2.root(act, st)),
                                          (15, lambda st: ln3.root(act, st)), (0, evac), (7, evac_h),
                                          (12, scale2), (16, scale3), (8, relus)])

            @block.gpsimd
            def _(pool):
                tt = nc.gpsimd.tensor_tensor

                def x_bo(st):
                    wait_pool(pool, go, lambda: st.pair_arrived(pool, got))
                    if st.has(2):
                        wait_pool(pool, go, lambda: st.freed(pool, tsum, 2))
                    tt(y0[:, st.slot(2)], x[0:P, st.slot(R)], row("bo"), ALU.add).then_inc(side, 1)

                def x_ln2_b(st):
                    if st.has(R):
                        wait_pool(pool, go, lambda: st.freed(pool, wsum, R))
                    tt(y2[:, st.slot(R)], x[0:P, st.slot(R)], row("ln2_b"), ALU.add).then_inc(side3, 1)

                def h_gain(st):
                    wait_pool(pool, go, lambda: st.ready(pool, ln1.scaled))
                    if st.has(2):
                        wait_pool(pool, go, lambda: st.freed(pool, hb, 2))
                    tt(h0[:, st.slot(2)], n1[:, st.slot(2)], row("ln1_g"), ALU.mult).then_inc(hg, 1)

                def h_bias(st):
                    wait_pool(pool, go, lambda: st.ready(pool, hg))
                    if st.has(2):
                        wait_pool(pool, go, lambda: st.freed(pool, trh, 2))
                        wait_pool(pool, go, lambda: st.freed(pool, side2, 2))
                    tt(h[:, st.slot(2)], h0[:, st.slot(2)], row("ln1_b"), ALU.add).then_inc(hb, 1)

                def h_b2(st):
                    wait_pool(pool, go, lambda: st.ready(pool, hb))
                    if st.has(MR):
                        wait_pool(pool, go, lambda: st.freed(pool, vsum, MR))
                    tt(y1[:, st.slot(MR)], h[:, st.slot(2)], row("b2"), ALU.add).then_inc(side2, 1)

                def n2_gain(st):
                    wait_pool(pool, go, lambda: st.ready(pool, ln2.scaled))
                    if st.has(2):
                        wait_pool(pool, go, lambda: st.freed(pool, wsum, 2))
                    tt(g2[:, st.slot(2)], n2[:, st.slot(2)], row("ln2_g"), ALU.mult).then_inc(g2d, 1)

                wait_pool(pool, go, lambda: pool.wait_ge(loaded, n_const))
                pipeline(pool, NSTEPS, R, [(6, h_bias), (5, h_gain), (1, x_bo), (7, h_b2), (6, x_ln2_b), (13, n2_gain)])

            @block.vector
            def _(dve):
                add = nc.vector.tensor_tensor

                def first(st):
                    st.ready(dve, mm)
                    st.ready(dve, side)
                    st.freed(dve, ln1.scaled, MR)
                    add(t[:, st.slot(MR)], ps_o[0:P], y0[:, st.slot(2)], ALU.add).then_inc(tsum, 1)

                def ffn(st):
                    st.ready(dve, f2)
                    st.ready(dve, side2)
                    st.freed(dve, ln2.scaled, MR)
                    add(v[:, st.slot(MR)], ps_v[0:P], y1[:, st.slot(MR)], ALU.add).then_inc(vsum, 1)

                def third(st):
                    st.ready(dve, g2d)
                    st.ready(dve, side3)
                    st.freed(dve, ln3.scaled, MR)
                    add(wv[:, st.slot(MR)], g2[:, st.slot(2)], y2[:, st.slot(R)], ALU.add).then_inc(wsum, 1)

                def stats(ln, summed, of):
                    def fn(st):
                        st.ready(dve, summed)
                        ln.stats(dve, st, of[:, st.slot(MR)])
                    return fn

                def scale1(st):
                    st.freed(dve, hg, 2)
                    ln1.scale(dve, st, t[:, st.slot(MR)], n1[:, st.slot(2)])

                pipeline(dve, NSTEPS, R, [
                    (2, first), (14, third), (10, ffn), (2, stats(ln1, tsum, t)), (14, stats(ln3, wsum, wv)), (10, stats(ln2, vsum, v)),
                    (3, lambda st: ln1.inverse(dve, st)), (11, lambda st: ln2.inverse(dve, st)), (15, lambda st: ln3.inverse(dve, st)),
                    (4, scale1), (11, lambda st: ln2.negated(dve, st)), (15, lambda st: ln3.negated(dve, st)),
                    (2, lambda st: ln1.aggregate(dve, st)), (14, lambda st: ln3.aggregate(dve, st)), (10, lambda st: ln2.aggregate(dve, st))])

    def nodes_relational(self):
        nc, a, pre, l, R = self.nc, self.a, "n3_", 3, NR
        with ExitStack() as ctx:
            sb = lambda name, shape: self.sb(ctx, pre + name, shape)
            x, s, got, put, load, store, finish = self.node_io(ctx, pre, l, self.agg3, W3)
            b3, bias = sb("b3", [P, 3, D]), sb("bias", [P, 2, D])
            xT, m = sb("xT", [128, 2, G, P]), sb("m", [P, 2, G, 3, D])
            r01, r3 = sb("r01", [P, 2, G, D]), sb("r3", [P, 2, G, D])
            u, o = sb("u", [P, MR, G, D]), sb("o", [P, R, G, D])
            ps_t, ps_y = ([self.ps(ctx, pre + f"{n}{k}", [128, G, 128]) for k in range(2)] for n in ("ps_t", "ps_y"))
            ps_o = [self.ps(ctx, pre + f"ps_o{k}", [128, 512]) for k in range(G)]
            loaded, own, biased, tr, ev, mm, added, weighted, part, summed, usum, go = (self.sem(pre + n) for n in (
                "loaded", "own", "biased", "tr", "ev", "mm", "added", "weighted", "part", "summed", "usum", "go"))
            ln = LayerNorm(self, ctx, pre + "ln")
            block = ctx.enter_context(nc.Block())

            @block.sync
            def _(sp):
                self.load_consts(sp, loaded, [(b3[:, r, :], rows_of(a["L3_gnn_bias"][r, :], P)) for r in range(3)])
                sp.wait_ge(biased, 1)
                sp.dma_start(x[P:P + 1].rearrange("p r g d -> p (r g) d"), over_tiles(bias[0:1, 0, :], R * G)).then_inc(loaded, 16)
                pipeline(sp, NSTEPS, R, [(0, lambda st: load(sp, st, [(weighted, G), (tr, 1), (added, 1)])),
                                         (10, lambda st: store(sp, st, o, ln.scaled))])
                finish(sp)

            @block.tensor
            def _(pe):
                def transposes(st):
                    st.pair_arrived(pe, got)
                    st.freed(pe, ev, 2)
                    for k in range(G):
                        i = nc.tensor.transpose(ps_t[st.slot(2)][:, k, 0:P], x[0:P, st.slot(R), k, :], self.ident[0:P, 0:P])
                    i.then_inc(tr, 1)

                def products(st):
                    st.ready(pe, ev)
                    for k in range(G):
                        if st.has(1):
                            pe.wait_ge(weighted, st.j * G - (G - 1 - k))
                        nc.tensor.matmul(ps_o[k][0:P, 0:3 * D], xT[:, st.slot(2), k, :], self.w3s[:],
                                         start=True, stop=True).then_inc(mm, 1)

                def adds(st):
                    st.freed(pe, usum, 2)
                    bank = ps_y[st.slot(2)]
                    nc.tensor.matmul(bank[0:P], self.ident_b[:], x[:, st.slot(R)], start=True, stop=False, skip_group_check=True)
                    nc.tensor.matmul(bank[0:P], self.ident_b[0:P], s[0:P, st.slot(R), :, 0:D], start=False, stop=True,
                                     skip_group_check=True).then_inc(added, 1)

                pe.wait_ge(loaded, 64)
                pipeline(pe, NSTEPS, R, [(0, transposes), (3, adds), (1, products)])

            @block.scalar
            def _(act):
                def evac(st):
                    st.ready(act, tr)
                    st.freed(act, mm, 2, G)
                    nc.scalar.copy(xT[:, st.slot(2)], ps_t[st.slot(2)][:, :, 0:P]).then_inc(ev, 1)

                def scale(st):
                    st.pair_sent(act, put)
                    ln.scale(act, st, u[:, st.slot(MR)], o[:, st.slot(R)])

                pipeline(act, NSTEPS, R, [(5, lambda st: ln.root(act, st)), (0, evac), (6, scale)])

            @block.gpsimd
            def _(pool):
                def relations(st):
                    slot = st.slot(2)
                    wait_pool(pool, go, lambda: st.ready(pool, weighted, G))
                    if st.has(2):
                        wait_pool(pool, go, lambda: st.freed(pool, usum, 2))
                    nc.gpsimd.tensor_tensor(r01[:, slot], m[:, slot, :, 0, :], m[:, slot, :, 1, :], ALU.add).then_inc(part, 1)
                    wait_pool(pool, go, lambda: st.ready(pool, part))
                    nc.gpsimd.tensor_tensor(r3[:, slot], r01[:, slot], m[:, slot, :, 2, :], ALU.add).then_inc(summed, 1)

                pipeline(pool, NSTEPS, R, [(3, relations)])

            @block.vector
            def _(dve):
                V, ch, rw = nc.vector, Chain(dve, own), self.rel_w
                dve.wait_ge(loaded, 48)
                ch(V.tensor_scalar(bias[:, 1, :], b3[:, 0, :], rw[0:P, 0:1], None, ALU.mult))
                ch(V.scalar_tensor_tensor(out=bias[:, 0, :], in0=b3[:, 1, :], scalar=rw[0:P, 1:2], in1=bias[:, 1, :], op0=ALU.mult, op1=ALU.add))
                ch(V.scalar_tensor_tensor(out=bias[:, 1, :], in0=b3[:, 2, :], scalar=rw[0:P, 2:3], in1=bias[:, 0, :], op0=ALU.mult, op1=ALU.add))
                V.tensor_copy(bias[:, 0, :], bias[:, 1, :]).then_inc(biased, 1)

                def weigh(st):
                    st.pair_arrived(dve, got)
                    st.freed(dve, summed, 2)
                    for k in range(G):
                        dve.wait_ge(mm, st.j * G + k + 1)
                        V.tensor_tensor(m[:, st.slot(2), k].rearrange("p r (h c) -> p (r h) c", h=4),
                                        ps_o[k][0:P, 0:3 * D].rearrange("p (q c) -> p q c", c=32),
                                        s[0:P, st.slot(R), k, D:W3].unsqueeze(2).to_broadcast([P, 12, 32]), ALU.mult).then_inc(weighted, 1)

                def total(st):
                    st.ready(dve, added)
                    st.ready(dve, summed)
                    st.freed(dve, ln.scaled, MR)
                    V.tensor_tensor(u[:, st.slot(MR)], ps_y[st.slot(2)][0:P], r3[:, st.slot(2)], ALU.add).then_inc(usum, 1)

                def stats(st):
                    st.ready(dve, usum)
                    ln.stats(dve, st, u[:, st.slot(MR)])

                pipeline(dve, NSTEPS, R, [(2, weigh), (4, total), (5, lambda st: ln.inverse(dve, st)), (4, stats),
                                          (5, lambda st: ln.negated(dve, st)), (4, lambda st: ln.aggregate(dve, st))])

    def run(self, layers=(0, 1, 2, 3)):
        self.graph()
        if 0 in layers:
            self.attention_layer(0)
            self.nodes_simple(0)
            self.recycle()
        if 1 in layers:
            with ExitStack() as ctx:
                self.edge_pass(1, ctx)
            self.nodes_simple(1)
            self.recycle()
        if 2 in layers:
            self.attention_layer(2)
            self.nodes_transformer()
            self.recycle()
        if 3 in layers:
            with ExitStack() as ctx:
                self.w3s = self.sb(ctx, "w3s", [D, 3 * D])
                self.rel_w = self.sb(ctx, "rel_w", [D, 3])
                self.attention_layer(3)
                self.nodes_relational()


def wait_pool(pool, go, wait):
    wait()
    pool.sem_inc(go, 1)


class LayerNorm:

    def __init__(self, b, ctx, name, on_vector=False):
        self.b, self.on_vector = b, on_vector
        sb = lambda n, shape: b.sb(ctx, name + n, shape)
        self.bn, self.mv = sb("bn", [P, LR, G, 6]), sb("mv", [P, LR, G, 2])
        self.sd, self.rs, self.nb = (sb(n, [P, LR, G]) for n in ("sd", "rs", "nb"))
        self.parts, self.aggr, self.rooted, self.inverted, self.offset, self.scaled, self.go = (
            b.sem(name + n) for n in ("parts", "aggr", "rooted", "inverted", "offset", "scaled", "go"))

    def stats(self, dve, st, x):
        st.freed(dve, self.aggr, LR)
        for k in range(G):
            i = self.b.nc.vector.bn_stats(self.bn[:, st.slot(LR), k, :], x[:, k, :])
        i.then_inc(self.parts, 1)

    def aggregate(self, dve, st):
        st.ready(dve, self.parts)
        dve.sem_inc(self.go, 1)
        if st.has(LR):
            st.freed(dve, self.scaled if self.on_vector else self.offset, LR)
            dve.sem_inc(self.go, 1)
        for k in range(G):
            i = self.b.nc.vector.bn_aggr(self.mv[:, st.slot(LR), k, :], self.bn[:, st.slot(LR), k, :])
        i.then_inc(self.aggr, 1)

    def root(self, act, st):
        slot = st.slot(LR)
        st.ready(act, self.aggr)
        st.freed(act, self.inverted, LR)
        self.b.nc.scalar.activation(self.sd[:, slot], self.mv[:, slot, :, 1], ACT.Sqrt, bias=self.b.eps[0:P]).then_inc(self.rooted, 1)

    def inverse(self, dve, st):
        st.ready(dve, self.rooted)
        st.freed(dve, self.scaled, LR)
        self.b.nc.vector.reciprocal(self.rs[:, st.slot(LR)], self.sd[:, st.slot(LR)]).then_inc(self.inverted, 1)

    def negated(self, dve, st):
        slot = st.slot(LR)
        st.ready(dve, self.inverted)
        self.b.nc.vector.scalar_tensor_tensor(out=self.nb[:, slot], in0=self.mv[:, slot, :, 0], scalar=-1.0, in1=self.rs[:, slot],
                                              op0=ALU.mult, op1=ALU.mult).then_inc(self.offset, 1)

    def scale(self, eng, st, x, out):
        slot = st.slot(LR)
        st.ready(eng, self.inverted if self.on_vector else self.offset)
        for k in range(G):
            if self.on_vector:
                i = self.b.nc.vector.tensor_scalar(out[:, k, :], x[:, k, :], self.mv[:, slot, k, 0:1], self.rs[:, slot, k:k + 1],
                                                   ALU.subtract, ALU.mult)
            else:
                i = self.b.nc.scalar.activation(out[:, k, :], x[:, k, :], ACT.Identity, bias=self.nb[:, slot, k:k + 1],
                                                scale=self.rs[:, slot, k:k + 1])
        i.then_inc(self.scaled, 1)


def build(nc, args, out):
    with ExitStack() as top:
        Builder(nc, args, out, top).run()


_INS = ["x", "src", "dst", "edge_attr_128", "edge_type_3", "L0_gnn_W_src", "L0_gnn_W_dst", "L0_gnn_attn", "L0_gnn_W_out",
        "L0_gnn_b_out", "L0_gnn_gamma", "L0_gnn_beta", "L1_gnn_WA", "L1_gnn_bA", "L1_gnn_WB", "L1_gnn_bB", "L1_gnn_WC",
        "L1_gnn_bC", "L1_gnn_WE", "L1_gnn_bE", "L1_gnn_Wres", "L1_gnn_bres", "L2_gnn_Wq", "L2_gnn_bq", "L2_gnn_Wk",
        "L2_gnn_bk", "L2_gnn_Wv", "L2_gnn_bv", "L2_gnn_Wo", "L2_gnn_bo", "L2_gnn_ln1_g", "L2_gnn_ln1_b", "L2_gnn_W1",
        "L2_gnn_b1", "L2_gnn_W2", "L2_gnn_b2", "L2_gnn_ln2_g", "L2_gnn_ln2_b", "L3_gnn_W", "L3_gnn_att_src",
        "L3_gnn_att_dst", "L3_gnn_bias", "L3_gnn_rel_w"]


def kernel(**inputs):
    import concourse.bacc as bacc
    from concourse.bass_utils import run_bass_kernel_spmd

    nc = bacc.Bacc("TRN2", target_bir_lowering=False, num_devices=1)
    arrays, args = {}, {}
    for name in _INS:
        arr = np.ascontiguousarray(inputs[name])
        arrays[f"in_{name}"] = arr
        args[name] = nc.dram_tensor(f"in_{name}", arr.shape, mybir.dt.from_np(arr.dtype), kind="ExternalInput").ap()
    out = nc.dram_tensor("out_x", (N_NODES, D), F32, kind="ExternalOutput").ap()
    build(nc, args, out)
    r = run_bass_kernel_spmd(nc, [arrays], core_ids=[0])
    return r.results[0]["out_x"]
```

```python
import numpy as np
import concourse.bass as bass
import concourse.mybir as mybir
from contextlib import ExitStack

F32 = mybir.dt.float32
I32 = mybir.dt.int32
ALU = mybir.AluOpType
ACT = mybir.ActivationFunctionType
AX = mybir.AxisListType

N_NODES, N_EDGES, D = 50000, 25000, 128
P = 125
T = N_EDGES // P
NT = N_NODES // P
G = 4
ESTEPS, NSTEPS = T // G, NT // G
EU = 10
ER = 2
XR = 5
NR = 10
MR = 5
LR = 5
BIG = 1.0e30
NEG = 1.0e9
EPS_LN = 1e-5
SKIP = 100000.0
SPLIT = 112
W3 = D + 12


class Step:

    def __init__(self, i, q, unroll):
        self.i, self.q, self.unroll = i, q, unroll
        self.j = i * unroll + q
        self.peeled = isinstance(i, int)

    def slot(self, ring):
        return self.q % ring

    def visits(self, ring):
        return self.i * (self.unroll // ring) + self.q // ring

    def has(self, back):
        return not self.peeled or self.j >= back

    def ready(self, eng, sem, per=1):
        eng.wait_ge(sem, (self.j + 1) * per)

    def freed(self, eng, sem, ring, per=1):
        if self.has(ring):
            eng.wait_ge(sem, (self.j - (ring - 1)) * per)

    def arrived(self, eng, sems, per):
        eng.wait_ge(sems[self.slot(len(sems))], (self.visits(len(sems)) + 1) * per)

    def sent(self, eng, sems, per):
        ring = len(sems)
        if self.has(ring):
            eng.wait_ge(sems[self.slot(ring)], self.visits(ring) * per)

    def pair_arrived(self, eng, sems):
        ring = 2 * len(sems)
        eng.wait_ge(sems[self.slot(ring) // 2], (self.visits(ring) + 1) * 64)

    def pair_sent(self, eng, sems):
        ring = 2 * len(sems)
        if self.has(ring):
            eng.wait_ge(sems[self.slot(ring) // 2], self.visits(ring) * 32)


def pipeline(eng, total, unroll, stages):
    most = max(lag for lag, _ in stages)
    warm = unroll * (1 + -(-most // unroll))

    def peeled(t):
        for lag, fn in stages:
            if 0 <= t - lag < total:
                fn(Step((t - lag) // unroll, (t - lag) % unroll, unroll))

    for t in range(warm):
        peeled(t)
    with eng.Fori(warm // unroll, total // unroll) as i:
        for r in range(unroll):
            for lag, fn in stages:
                back = (lag - r + unroll - 1) // unroll if lag > r else 0
                fn(Step(i - back if back else i, r - lag + back * unroll, unroll))
    for t in range(total, total + most):
        peeled(t)


def over_tiles(row, n=G):
    return row.unsqueeze(1).to_broadcast([row.shape[0], n, row.shape[1]])


def load_rows(eng, dst, src, sem):
    eng.dma_start(dst[0:SPLIT], src[0:SPLIT]).then_inc(sem, 16)
    eng.dma_start(dst[SPLIT:P], src[SPLIT:P]).then_inc(sem, 16)


def rows_of(v, n):
    return v.rearrange("(a c) -> a c", a=1).to_broadcast([n, v.shape[0]])


class Chain:

    def __init__(self, eng, sem):
        self.eng, self.sem, self.n = eng, sem, 0

    def __call__(self, *instructions):
        for i in instructions:
            i.then_inc(self.sem, 1)
        self.n += len(instructions)
        self.eng.wait_ge(self.sem, self.n)


class Builder:

    def __init__(self, nc, args, out, top):
        self.nc, self.a, self.out, self.top = nc, args, out, top
        self.filled = False
        self.used = []
        x_after = [nc.dram_tensor(f"x_after_{l}", (N_NODES, D), F32).ap() for l in range(3)]
        self.x = [args["x"], *x_after, out]
        self.agg = nc.dram_tensor("agg", (N_NODES, D), F32).ap()
        self.agg3 = nc.dram_tensor("agg3", (N_NODES, W3), F32).ap()
        sb = lambda name, shape, dt=F32: self.sb(top, name, shape, dt)
        self.ident = sb("ident", [128, 128])
        self.ones = sb("ones", [P, P])
        self.e0 = sb("e0", [128, P])
        self.ident_b = sb("ident_b", [P + 1, P])
        self.eps = sb("eps", [128, 1])
        self.src_i = sb("src_i", [P, T], I32)
        self.dst_i = sb("dst_i", [P, T], I32)
        self.type_i = sb("type_i", [P, T], I32)
        self.flag = sb("flag", [1, 1], I32)
        self.recs = nc.dram_tensor("recs", (N_EDGES, 3), I32).ap()
        self.ea_sorted = nc.dram_tensor("ea_sorted", (N_EDGES, D), F32).ap()
        self.put_i = sb("put_i", [P, T], I32)
        self.fix_i = sb("fix_i", [P, 1], I32)
        self.same_prev = sb("same_prev", [P, T])
        self.same_next = sb("same_next", [P, T])
        self.in_row = sb("in_row", [P, T])
        self.pen_prev = sb("pen_prev", [P, T])
        self.pen_next = sb("pen_next", [P, T])
        self.pen_ends = sb("pen_ends", [P, 2, T])
        self.carry_f = sb("carry_f", [P, P])
        self.carry_b = sb("carry_b", [P, P])
        self.row_pens = sb("row_pens", [16, 4, P])

    def sem(self, name):
        handle = self.nc.alloc_semaphore(name)
        self.used.append(handle)
        return handle

    def recycle(self):
        self.nc.clear_and_free_semaphores(self.used)
        self.nc.all_engine_barrier()
        self.used = []

    def sb(self, ctx, name, shape, dt=F32):
        return ctx.enter_context(self.nc.sbuf_tensor(name, shape, dt))

    def ps(self, ctx, name, shape):
        return ctx.enter_context(self.nc.psum_tensor(name, shape, F32))

    def order_edges(self):
        nc, a = self.nc, self.a
        C = 5
        src_i, dst_i, type_i, flag = self.src_i, self.dst_i, self.type_i, self.flag
        by_row = lambda v: v.rearrange("(p t) -> p t", p=P)
        with ExitStack() as ctx:
            sb = lambda name, shape, dt=F32: self.sb(ctx, "o_" + name, shape, dt)
            next_i, df, nf, over = sb("next_i", [P, 1], I32), sb("df", [P, T]), sb("nf", [P, T]), sb("over", [P, T])
            count, one = sb("count", [P, 1]), sb("one", [P, 1])
            ps = self.ps(ctx, "o_ps", [1, 1])
            own, blank, loaded, counted, total = (self.sem("o_" + n) for n in ("own", "blank", "loaded", "counted", "total"))
            with ExitStack() as c2:
                block = c2.enter_context(nc.Block())

                @block.sync
                def _(sp):
                    for to, of in ((src_i, "src"), (dst_i, "dst"), (type_i, "edge_type_3")):
                        sp.dma_start(to[:], by_row(a[of])).then_inc(loaded, 16)
                    sp.wait_ge(blank, 1)
                    with nc.allow_non_contiguous_dma(reason="one index of each row"):
                        sp.dma_start(next_i[0:P - 1, :], by_row(a["dst"])[1:P, 0:1]).then_inc(loaded, 16)

                @block.vector
                def _(dve):
                    V, ch = nc.vector, Chain(dve, own)
                    V.memset(next_i[:], N_NODES).then_inc(blank, 1)
                    ch(V.memset(one[:], 1.0))
                    dve.wait_ge(loaded, 64)
                    ch(V.tensor_copy(df[:], dst_i[:]))
                    ch(V.tensor_copy(nf[:, 0:T - 1], df[:, 1:T]), V.tensor_copy(nf[:, T - 1:T], next_i[:]))
                    ch(V.tensor_tensor(over[:], df[:], nf[:], ALU.is_gt))
                    V.tensor_reduce(count[:], over[:], AX.X, ALU.add).then_inc(counted, 1)
                    dve.wait_ge(total, 1)
                    ch(V.tensor_copy(flag[:], ps[:]))

                @block.tensor
                def _(pe):
                    pe.wait_ge(counted, 1)
                    nc.tensor.matmul(ps[:], count[:], one[:], start=True, stop=True).then_inc(total, 1)

            keys = sb("keys", [P, N_EDGES])
            ints, less = sb("ints", [P, N_EDGES // C], I32), sb("less", [P, N_EDGES // C])
            before, diag = sb("before", [P, P]), sb("diag", [P, P])
            counts, rank = sb("counts", [P, T, C]), sb("rank", [P, T], I32)
            recs, rec_t, rank_t, ea_t = sb("recs", [P, T, 3], I32), sb("rec_t", [P, 3], I32), sb("rank_t", [P, 1], I32), sb("ea_t", [P, D])
            keys_by_row = keys[:].rearrange("p (q t) -> p q t", t=T)
            staged, taken, masks, step, done, ea_in, picked, put, back = (self.sem("o_" + n) for n in (
                "staged", "taken", "masks", "step", "done", "ea_in", "picked", "put", "back"))
            rec_v = self.recs.rearrange("(p t) c -> p t c", p=P)
            ea_v = a["edge_attr_128"].rearrange("(p t) d -> p t d", p=P)
            go = self.sem("o_go")
            block = ctx.enter_context(nc.Block())

            @block.sync
            def _(sp):
                with sp.If(sp.value_load(flag[0:1, 0:1], min_val=0, max_val=N_EDGES) > 0):
                    for c in range(C):
                        if c:
                            sp.wait_ge(taken, c)
                        n = N_EDGES // C
                        sp.dma_start(ints[:], rows_of(a["dst"][c * n:(c + 1) * n], P)).then_inc(staged, 16)
                    sp.wait_ge(done, 1)
                    sp.dma_start(ea_t[:], ea_v[:, 0, :]).then_inc(ea_in, 16)
                    with sp.Fori(1, T) as t:
                        sp.wait_ge(put, t * 32)
                        sp.dma_start(ea_t[:], ea_v[:, bass.ds(t, 1), :].rearrange("p t d -> p (t d)")).then_inc(ea_in, 16)
                    sp.wait_ge(put, T * 32)
                    sp.dma_start(recs[:], rec_v).then_inc(back, 16)

            @block.gpsimd
            def _(pool):
                with pool.If(pool.value_load(flag[0:1, 0:1], min_val=0, max_val=N_EDGES) > 0):
                    nc.gpsimd.memset(before[:], 0.0).then_inc(masks, 1)
                    nc.gpsimd.memset(diag[:], 0.0).then_inc(masks, 1)
                    pool.wait_ge(masks, 2)
                    nc.gpsimd.affine_select(out=before[:], in_=before[:], compare_op=ALU.is_ge, fill=-0.5, base=0,
                                            pattern=[[1, P]], channel_multiplier=-1).then_inc(masks, 1)
                    nc.gpsimd.affine_select(out=diag[:], in_=diag[:], compare_op=ALU.not_equal, fill=-0.5, base=0,
                                            pattern=[[-1, P]], channel_multiplier=1).then_inc(masks, 1)
                    with pool.Fori(0, T) as t:
                        wait_pool(pool, go, lambda: pool.wait_ge(picked, t + 1))
                        wait_pool(pool, go, lambda: pool.wait_ge(ea_in, t * 16 + 16))
                        for to, rows in ((self.recs, rec_t), (self.ea_sorted, ea_t)):
                            nc.gpsimd.indirect_dma_start(to, bass.IndirectOffsetOnAxis(rank_t[:, 0:1], 0), rows[:], None,
                                                         bounds_check=N_EDGES - 1, oob_is_err=False).then_inc(put, 16)
                    pool.wait_ge(put, T * 32)

            @block.vector
            def _(dve):
                V, ch = nc.vector, Chain(dve, step)
                with dve.If(dve.value_load(flag[0:1, 0:1], min_val=0, max_val=N_EDGES) > 0):
                    n = N_EDGES // C
                    for c in range(C):
                        dve.wait_ge(staged, 16 * (c + 1))
                        V.tensor_copy(keys[:, c * n:(c + 1) * n], ints[:]).then_inc(taken, 1)
                    dve.wait_ge(taken, C)
                    dve.wait_ge(masks, 4)
                    ch(V.tensor_tensor(keys_by_row, keys_by_row, before[:].unsqueeze(2).to_broadcast([P, P, T]), ALU.add))
                    for k, column in enumerate((src_i, dst_i, type_i)):
                        ch(V.tensor_copy(recs[:, :, k], column[:]))
                    base = ch.n
                    with dve.Fori(0, T) as t:
                        for c in range(C):
                            V.tensor_scalar(less[:], keys[:, c * n:(c + 1) * n], df[:, bass.ds(t, 1)], 0.0, ALU.is_lt, ALU.add,
                                            accum_out=counts[:, bass.ds(t, 1), c]).then_inc(step, 1)
                            dve.wait_ge(step, t * (C + 1) + (base + c + 1))
                        now = keys_by_row[:, :, bass.ds(t, 1)].rearrange("p q t -> p (q t)")
                        V.tensor_tensor(now, now, diag[:], ALU.add).then_inc(step, 1)
                        dve.wait_ge(step, t * (C + 1) + (base + C + 1))
                    V.tensor_reduce(over[:], counts[:], AX.X, ALU.add).then_inc(step, 1)
                    dve.wait_ge(step, base + T * (C + 1) + 1)
                    V.tensor_copy(rank[:], over[:]).then_inc(done, 1)
                    dve.wait_ge(done, 1)

                    def pick(t):
                        V.tensor_copy(rank_t[:], rank[:, bass.ds(t, 1)])
                        V.tensor_copy(rec_t[:], recs[:, bass.ds(t, 1), :].rearrange("p t c -> p (t c)")).then_inc(picked, 1)

                    pick(0)
                    with dve.Fori(1, T) as t:
                        dve.wait_ge(put, t * 32)
                        pick(t)
                    dve.wait_ge(back, 16)
                    for k, column in enumerate((src_i, dst_i, type_i)):
                        V.tensor_copy(column[:], recs[:, :, k]).then_inc(done, 1)
                    dve.wait_ge(done, 4)

    def graph(self):
        nc, sem = self.nc, self.sem
        ident, ones, e0, eps, ident_b = self.ident, self.ones, self.e0, self.eps, self.ident_b
        carry_f, carry_b = self.carry_f, self.carry_b
        same_prev, same_next, in_row = self.same_prev, self.same_next, self.in_row
        with ExitStack() as ctx:
            sb = lambda name, shape, dt=F32: self.sb(ctx, name, shape, dt)
            dpad = sb("dpad", [P, T + 2], I32)
            df = sb("df", [P, T + 2])
            last = sb("last", [P, T])
            put_f = sb("put_f", [P, T])
            diag = sb("diag", [P, P])
            fix = sb("fix", [P, 4])
            single, links, links_diag = sb("single", [P, 1]), sb("links", [P, 4]), sb("links_diag", [P, 4, P])
            ps_rows = self.ps(ctx, "ps_rows", [16, 4, 128])
            rows_done = sem("g_rows")
            ps_first = self.ps(ctx, "ps_first", [P, P])
            ps_tr = self.ps(ctx, "ps_tr", [P, P])
            frame, consts, loaded = (sem("g_" + n) for n in ("frame", "consts", "loaded"))
            own, diag_done, first_done = sem("g_own"), sem("g_diag"), sem("g_first")
            equal, upper, turned = sem("g_equal"), sem("g_upper"), sem("g_turned")
            block = ctx.enter_context(nc.Block())

            @block.gpsimd
            def _(pool):
                nc.gpsimd.memset(dpad[:], -1).then_inc(frame, 1)
                nc.gpsimd.memset(ident[:], 0.0).then_inc(consts, 1)
                nc.gpsimd.memset(e0[:], 0.0).then_inc(consts, 1)
                nc.gpsimd.memset(ident_b[:], 0.0).then_inc(consts, 1)
                nc.gpsimd.memset(ones[:], 1.0).then_inc(consts, 1)
                nc.gpsimd.memset(eps[:], EPS_LN).then_inc(consts, 1)
                pool.wait_ge(consts, 5)
                nc.gpsimd.affine_select(out=ident[:], in_=ident[:], compare_op=ALU.not_equal, fill=1.0, base=0,
                                        pattern=[[-1, 128]], channel_multiplier=1).then_inc(consts, 1)
                nc.gpsimd.affine_select(out=e0[:], in_=e0[:], compare_op=ALU.not_equal, fill=1.0, base=0,
                                        pattern=[[0, P]], channel_multiplier=1).then_inc(consts, 1)
                nc.gpsimd.affine_select(out=ident_b[:], in_=ident_b[:], compare_op=ALU.not_equal, fill=1.0, base=0,
                                        pattern=[[-1, P]], channel_multiplier=1).then_inc(consts, 1)
                pool.wait_ge(consts, 8)
                nc.gpsimd.affine_select(out=ident_b[:], in_=ident_b[:], compare_op=ALU.not_equal, fill=1.0, base=-P,
                                        pattern=[[0, P]], channel_multiplier=1).then_inc(consts, 1)
                pool.wait_ge(equal, 1)
                nc.gpsimd.affine_select(out=carry_f[:], in_=carry_f[:], compare_op=ALU.is_gt, fill=0.0, base=0,
                                        pattern=[[1, P]], channel_multiplier=-1).then_inc(upper, 1)

            @block.sync
            def _(sp):
                sp.wait_ge(frame, 1)
                dst = self.dst_i
                with nc.allow_non_contiguous_dma(reason="one index of each row"):
                    sp.dma_start(dpad[1:P, 0:1], dst[0:P - 1, T - 1:T]).then_inc(loaded, 16)
                    sp.dma_start(dpad[0:P - 1, T + 1:T + 2], dst[1:P, 0:1]).then_inc(loaded, 16)
                sp.wait_ge(loaded, 32)

            @block.vector
            def _(dve):
                V, ch = nc.vector, Chain(dve, own)
                dve.wait_ge(loaded, 32)
                ch(V.tensor_copy(df[:], dpad[:]))
                ch(V.tensor_copy(df[:, 1:T + 1], self.dst_i[:]))
                mine, prev, nxt = df[:, 1:T + 1], df[:, 0:T], df[:, 2:T + 2]
                ch(V.tensor_tensor(same_prev[:], mine, prev, ALU.is_equal),
                   V.tensor_tensor(same_next[:], mine, nxt, ALU.is_equal),
                   V.tensor_tensor(last[:], mine, nxt, ALU.not_equal))
                ch(V.tensor_copy(in_row[:], same_prev[:]),
                   V.tensor_scalar(self.pen_prev[:], same_prev[:], -1.0, BIG, ALU.add, ALU.mult),
                   V.tensor_scalar(self.pen_next[:], same_next[:], -1.0, BIG, ALU.add, ALU.mult),
                   V.tensor_scalar(put_f[:], last[:], -1.0, -SKIP, ALU.add, ALU.mult))
                ch(V.tensor_scalar(self.pen_ends[:, 0, :], mine, df[:, T:T + 1], -1.0, ALU.is_equal, ALU.add),
                   V.tensor_scalar(self.pen_ends[:, 1, :], mine, df[:, 1:2], -1.0, ALU.is_equal, ALU.add))
                ch(V.tensor_scalar(self.pen_ends[:], self.pen_ends[:], BIG, None, ALU.mult),
                   V.memset(in_row[:, 0:1], 0.0),
                   V.tensor_tensor(put_f[:], put_f[:], mine, ALU.add))
                ch(V.tensor_copy(self.put_i[:], put_f[:]),
                   V.tensor_tensor(fix[:, 0:1], df[:, 1:2], df[:, T + 1:T + 2], ALU.not_equal))
                ch(V.tensor_tensor(fix[:, 1:2], fix[:, 0:1], same_prev[:, 0:1], ALU.mult))
                ch(V.tensor_scalar(fix[:, 2:3], fix[:, 1:2], -1.0, -SKIP, ALU.add, ALU.mult))
                ch(V.tensor_tensor(fix[:, 3:4], fix[:, 2:3], df[:, 1:2], ALU.add))
                ch(V.tensor_copy(self.fix_i[:], fix[:, 3:4]))
                dve.wait_ge(consts, 9)
                V.tensor_scalar(diag[:], ident[0:P, 0:P], df[:, 1:2], None, ALU.mult).then_inc(diag_done, 1)
                ch(V.tensor_tensor(single[:], df[:, 1:2], df[:, T:T + 1], ALU.is_equal),
                   V.tensor_copy(links[:, 0:1], same_next[:, T - 1:T]), V.tensor_copy(links[:, 1:2], same_prev[:, 0:1]))
                ch(V.tensor_scalar(links[:, 2:4], links[:, 0:2], single[:, 0:1], None, ALU.mult))
                V.tensor_tensor(links_diag[:], ident[0:P, 0:P].unsqueeze(1).to_broadcast([P, 4, P]),
                                links[:].unsqueeze(2).to_broadcast([P, 4, P]), ALU.mult).then_inc(diag_done, 1)
                dve.wait_ge(first_done, 1)
                V.tensor_scalar(carry_f[:], ps_first[:], df[:, T:T + 1], None, ALU.is_equal).then_inc(equal, 1)
                dve.wait_ge(upper, 1)
                dve.wait_ge(turned, 1)
                ch(V.tensor_copy(carry_b[:], ps_tr[:]))
                dve.wait_ge(rows_done, 1)
                ch(V.tensor_scalar(self.row_pens[:], ps_rows[:, :, 0:P], -1.0, BIG, ALU.add, ALU.mult))

            @block.tensor
            def _(pe):
                pe.wait_ge(consts, 9)
                pe.wait_ge(diag_done, 1)
                nc.tensor.matmul(ps_first[:], ones[:], diag[:], start=True, stop=True).then_inc(first_done, 1)
                pe.wait_ge(upper, 1)
                nc.tensor.transpose(ps_tr[:], carry_f[:], ident[0:P, 0:P]).then_inc(turned, 1)
                pe.wait_ge(diag_done, 2)
                nc.tensor.matmul(ps_rows[:, :, 0:P], ones[:, 0:16], links_diag[:], start=True, stop=True).then_inc(rows_done, 1)

    def running_sum(self, dve, st, ro, msg, msg_slot, put, summed):
        slot = st.slot(XR)
        st.sent(dve, put, 16 * G)
        for k in range(G):
            before = ro[:, slot, k - 1, 0:D] if k else ro[:, (slot - 1) % XR, G - 1, 0:D]
            if k or st.has(1):
                dve.wait_ge(summed, st.j * G + k)
            self.nc.vector.scalar_tensor_tensor(
                out=ro[:, slot, k, 0:D], in0=before, scalar=self.in_row[:, bass.ds(st.j * G + k, 1)],
                in1=msg[:, msg_slot, k, :], op0=ALU.mult, op1=ALU.add).then_inc(summed, 1)

    def columns(self, eng, st, pairs, sems, per, copied):
        st.sent(eng, sems, per)
        for to, of in pairs:
            i = self.nc.vector.tensor_copy(to[:, st.slot(XR)], of[:, bass.ds(st.j * G, G)])
        i.then_inc(copied, 1)

    def scatter(self, pool, st, cols, ro, dst, put, copied, go, waits):
        slot = st.slot(XR)
        wait_pool(pool, go, lambda: st.ready(pool, copied))
        for s, per in waits:
            wait_pool(pool, go, lambda: st.ready(pool, s, per))
        for k in range(G):
            self.nc.gpsimd.indirect_dma_start(
                dst, bass.IndirectOffsetOnAxis(cols[:, slot, k:k + 1], 0), ro[:, slot, k, :], None,
                bounds_check=N_NODES - 1, oob_is_err=False).then_inc(put[slot], 16)

    def carry_fix(self, l, ro, dst, width):
        nc = self.nc
        with ExitStack() as ctx:
            rows = self.sb(ctx, f"c{l}_rows", [P, width])
            ps_c = self.ps(ctx, f"c{l}_ps", [P, D])
            blank, got, summed, fixed, back = (self.sem(f"c{l}_" + n) for n in ("blank", "got", "summed", "fixed", "back"))
            block = ctx.enter_context(nc.Block())

            @block.tensor
            def _(pe):
                nc.tensor.matmul(ps_c[:], self.carry_f[:], ro[:, XR - 1, G - 1, 0:D], start=True, stop=True).then_inc(summed, 1)

            @block.gpsimd
            def _(pool):
                nc.gpsimd.memset(rows[:], 0.0).then_inc(blank, 1)
                pool.wait_ge(blank, 1)
                nc.gpsimd.indirect_dma_start(rows[:], None, dst, bass.IndirectOffsetOnAxis(self.fix_i[:, 0:1], 0),
                                             bounds_check=N_NODES - 1, oob_is_err=False).then_inc(got, 16)
                pool.wait_ge(fixed, 1)
                nc.gpsimd.indirect_dma_start(dst, bass.IndirectOffsetOnAxis(self.fix_i[:, 0:1], 0), rows[:], None,
                                             bounds_check=N_NODES - 1, oob_is_err=False).then_inc(back, 16)
                pool.wait_ge(back, 16)

            @block.vector
            def _(dve):
                dve.wait_ge(got, 16)
                dve.wait_ge(summed, 1)
                nc.vector.tensor_tensor(rows[:, 0:D], rows[:, 0:D], ps_c[:], ALU.add).then_inc(fixed, 1)

    def edge_pass(self, l, keep=None, S=None, SS=None, ends=None, mk=None, nm=None, w3s=None, rel_w=None):
        nc, a, sem = self.nc, self.a, self.sem
        x_in, ident, pre = self.x[l], self.ident, f"e{l}_"
        sb = lambda c, name, shape, dt=F32: self.sb(c, pre + name, shape, dt)
        cols = {0: 256, 1: 256, 2: 384, 3: 408}[l]
        hold = 2 if cols <= 256 else 1
        per = 2 if hold == 2 else G
        nv = {0: 0, 1: 2, 2: 4, 3: 8}[l]
        fill, self.filled = not self.filled, True
        Z = NT // ESTEPS
        with ExitStack() as c2:
            xs, xd = sb(c2, "xs", [P, XR, G, D]), sb(c2, "xd", [P, XR, G, D])
            ixs, ixd = sb(c2, "ixs", [P, XR, G], I32), sb(c2, "ixd", [P, XR, G], I32)
            xsT, xdT = sb(c2, "xsT", [128, ER, G, P]), sb(c2, "xdT", [128, ER, G, P])
            ws, wd = sb(c2, "ws", [D, cols]), sb(c2, "wd", [D, D])
            brow = sb(c2, "brow", [128, cols])
            t1, t2 = sb(c2, "t1", [P, ER, G, D]), sb(c2, "t2", [P, ER, G, D])
            ps_s, ps_d = self.ps(c2, pre + "ps_s", [128, G, 128]), self.ps(c2, pre + "ps_d", [128, G, 128])
            ps_h = [self.ps(c2, pre + f"ps_h{k}", [128, 512]) for k in range(4)]
            weights, weights_done, own = sem(pre + "weights"), sem(pre + "weights_done"), sem(pre + "own")
            copied, go = sem(pre + "copied"), sem(pre + "go")
            got = [sem(pre + f"got{k}") for k in range(XR)]
            tr_s, tr_d, ev_s, ev_d = (sem(pre + n) for n in ("tr_s", "tr_d", "ev_s", "ev_d"))
            prod, act_done, vec_done, reduced = (sem(pre + n) for n in ("prod", "act", "vec", "reduced"))
            if fill:
                zero, zero3 = sb(c2, "zero", [P, Z, D]), sb(c2, "zero3", [P, Z, W3])
                fills, filled = sem(pre + "fills"), sem(pre + "filled")
            if l == 1:
                ea, eaT = sb(c2, "ea", [P, ER, G, D]), sb(c2, "eaT", [128, ER, G, P])
                we, b3 = sb(c2, "we", [D, D]), sb(c2, "b3", [128, 3, D])
                ps_e = self.ps(c2, pre + "ps_e", [128, G, 128])
                got_e = [sem(pre + f"got_e{k}") for k in range(ER)]
                tr_e, ev_e, summed, pcopied = sem(pre + "tr_e"), sem(pre + "ev_e"), sem(pre + "summed"), sem(pre + "pcopied")
                put = [sem(pre + f"put{k}") for k in range(XR)]
                pcols = sb(c2, "pcols", [P, XR, G], I32)
                ro = sb(c2, "ro", [P, XR, G, D])
            if l != 1:
                H = S.shape[2]
                segs, best = sb(c2, "segs", [P, 2, G, H]), sb(c2, "best", [P, 2, H])
                ends_done = sem(pre + "ends_done")
            if l == 0:
                attn_row = sb(c2, "attn", [P, D])
                vec_done0 = sem(pre + "vec0")
            if l == 3:
                w3, pr3 = sb(c2, "w3", [D, 3, D]), sb(c2, "pr3", [D, 3 * D])
                att_s, att_d = sb(c2, "att_s", [D, 3 * D]), sb(c2, "att_d", [D, 3 * D])
                rel = sb(c2, "rel", [D, 12])
                raw, relu = sb(c2, "raw", [P, ER, G, 24]), sb(c2, "relu", [P, ER, G, 24])
                masked = sb(c2, "masked", [P, ER, G, 12])
                scored = sem(pre + "scored")
                exped, neg_max = sem(pre + "exped"), sem(pre + "neg_max")

            def bank(st, k):
                if hold == 2:
                    return ps_h[2 * st.slot(2) + k // 2][0:P, 256 * (k % 2):256 * (k % 2) + cols]
                return ps_h[k][0:P, 0:cols]

            def units(st):
                if hold == 2:
                    return [(2 * h, 2, ps_h[2 * st.slot(2) + h][0:P, :].rearrange("p (k c) -> p k c", k=2)) for h in range(2)]
                return [(k, 1, ps_h[k][0:P, :].rearrange("p (k c) -> p k c", k=1)) for k in range(G)]

            W = {0: [(ws[:, 0:D], a["L0_gnn_W_src"]), (ws[:, D:2 * D], a["L0_gnn_W_src"]), (wd[:], a["L0_gnn_W_dst"])],
                 1: [(ws[:, 0:D], a["L1_gnn_WB"]), (ws[:, D:2 * D], a["L1_gnn_WA"]), (wd[:], a["L1_gnn_WC"])],
                 2: [(ws[:, 0:D], a["L2_gnn_Wk"]), (ws[:, D:2 * D], a["L2_gnn_Wv"]), (wd[:], a["L2_gnn_Wq"])],
                 3: []}[l]
            if l == 0:
                W += [(attn_row[:], rows_of(a["L0_gnn_attn"].rearrange("h d -> (h d)"), P))]
            if l == 1:
                W += [(we[:], a["L1_gnn_WE"]), (brow[:, D:2 * D], rows_of(a["L1_gnn_bA"], 128))]
                W += [(b3[:, k, :], rows_of(a["L1_gnn_b" + n], 128)) for k, n in enumerate("BCE")]
            if l == 2:
                W += [(brow[:, k * D:k * D + D], rows_of(a["L2_gnn_b" + n], 128)) for k, n in enumerate("kvq")]
            if l == 3:
                W += [(w3[:], a["L3_gnn_W"].rearrange("r i o -> i r o")), (rel[:, 0:3], rows_of(a["L3_gnn_rel_w"], D)),
                      (att_s[:], rows_of(a["L3_gnn_att_src"].rearrange("r h c -> (r h c)"), D)),
                      (att_d[:], rows_of(a["L3_gnn_att_dst"].rearrange("r h c -> (r h c)"), D))]
            with ExitStack() as c3:
                block = c3.enter_context(nc.Block())

                @block.sync
                def _(sp):
                    for to, of in W:
                        sp.dma_start(to, of).then_inc(weights, 16)
                    stages = []
                    if fill:
                        sp.wait_ge(fills, 3)
                        agg = self.agg.rearrange("(p n) d -> p n d", p=P)
                        agg3 = self.agg3.rearrange("(p n) d -> p n d", p=P)

                        def fill_rows(st):
                            st.freed(sp, tr_s, 1)
                            nodes = bass.ds(st.j * Z, Z)
                            load_rows(sp, agg[:, nodes, :], zero[:], filled)
                            load_rows(sp, agg3[:, nodes, :], zero3[:], filled)

                        stages.append((0, fill_rows))
                    if l == 1:
                        inputs, ordered = (v.rearrange("(p t) d -> p t d", p=P) for v in (a["edge_attr_128"], self.ea_sorted))

                        def load(st, ea_v):
                            st.freed(sp, tr_e, ER)
                            load_rows(sp, ea[:, st.slot(ER)], ea_v[:, bass.ds(st.j * G, G), :], got_e[st.slot(ER)])

                        moved = sp.value_load(self.flag[0:1, 0:1], min_val=0, max_val=N_EDGES)
                        with sp.If(moved > 0):
                            pipeline(sp, ESTEPS, EU, [*stages, (0, lambda st: load(st, ordered))])
                        with sp.Else():
                            pipeline(sp, ESTEPS, EU, [*stages, (0, lambda st: load(st, inputs))])
                    elif stages:
                        pipeline(sp, ESTEPS, EU, stages)
                    if fill:
                        sp.wait_ge(filled, 64 * ESTEPS)

                @block.gpsimd
                def _(pool):
                    def gather(st):
                        slot = st.slot(XR)
                        if st.has(XR):
                            wait_pool(pool, go, lambda: st.freed(pool, tr_s, XR))
                            wait_pool(pool, go, lambda: st.freed(pool, tr_d, XR))
                        wait_pool(pool, go, lambda: st.ready(pool, copied))
                        for k in range(G):
                            for rows, ix in ((xs, ixs), (xd, ixd)):
                                nc.gpsimd.indirect_dma_start(
                                    rows[:, slot, k, :], None, x_in,
                                    bass.IndirectOffsetOnAxis(ix[:, slot, k:k + 1], 0)).then_inc(got[slot], 16)

                    stages = [(0, gather)]
                    if l == 1:
                        stages.append((3, lambda st: self.scatter(pool, st, pcols, ro, self.agg, put, pcopied, go, [(summed, G)])))
                    pipeline(pool, ESTEPS, EU, stages)
                    if l == 1:
                        for k in range(XR):
                            pool.wait_ge(put[k], 16 * G * (ESTEPS // XR))

                @block.tensor
                def _(pe):
                    kw = dict(skip_group_check=True)

                    def transposes(st):
                        slot, xslot = st.slot(ER), st.slot(XR)
                        st.arrived(pe, got, 32 * G)
                        st.freed(pe, ev_s, 1)
                        for k in range(G):
                            i = nc.tensor.transpose(ps_s[:, k, 0:P], xs[:, xslot, k, :], ident[0:P, 0:P])
                        i.then_inc(tr_s, 1)
                        st.freed(pe, ev_d, 1)
                        for k in range(G):
                            i = nc.tensor.transpose(ps_d[:, k, 0:P], xd[:, xslot, k, :], ident[0:P, 0:P])
                        i.then_inc(tr_d, 1)
                        if l == 1:
                            st.arrived(pe, got_e, 32)
                            st.freed(pe, ev_e, 1)
                            for k in range(G):
                                i = nc.tensor.transpose(ps_e[:, k, 0:P], ea[:, slot, k, :], ident[0:P, 0:P])
                            i.then_inc(tr_e, 1)

                    def products(st):
                        slot, mm = st.slot(ER), nc.tensor.matmul
                        st.ready(pe, ev_s)
                        st.ready(pe, ev_d)
                        if l == 1:
                            st.ready(pe, ev_e)
                        if l == 0:
                            st.freed(pe, act_done, hold, per)
                        if l == 1:
                            st.freed(pe, vec_done, hold, nv)
                        for k in range(G):
                            if l in (2, 3) and st.has(1):
                                pe.wait_ge(vec_done, st.j * nv - (G - 1 - k))
                            o, src_t, dst_t = bank(st, k), xsT[:, slot, k, :], xdT[:, slot, k, :]
                            if l == 0:
                                mm(o[:, 0:2 * D], src_t, ws[:], start=True, stop=False, **kw)
                                i = mm(o[:, D:2 * D], dst_t, wd[:], start=False, stop=True, **kw)
                            if l == 1:
                                mm(o[:, 0:2 * D], self.e0[:], brow[:], start=True, stop=False, **kw)
                                mm(o[:, 0:2 * D], src_t, ws[:], start=False, stop=False, **kw)
                                mm(o[:, 0:D], dst_t, wd[:], start=False, stop=False, **kw)
                                i = mm(o[:, 0:D], eaT[:, slot, k, :], we[:], start=False, stop=True, **kw)
                            if l == 2:
                                mm(o[:, 0:3 * D], self.e0[:], brow[:], start=True, stop=False, **kw)
                                mm(o[:, 0:2 * D], src_t, ws[:, 0:2 * D], start=False, stop=False, **kw)
                                i = mm(o[:, 2 * D:3 * D], dst_t, wd[:], start=False, stop=True, **kw)
                            if l == 3:
                                mm(o[:, 0:408], src_t, ws[:], start=True, stop=False, **kw)
                                i = mm(o[:, 384:408], dst_t, wd[:, 0:24], start=False, stop=True, **kw)
                            if hold == 1 or k % 2:
                                i.then_inc(prod, 1)

                    pe.wait_ge(weights, 16 * len(W))
                    pe.wait_ge(weights_done, 1)
                    stages = [(0, transposes), (1, products)]
                    pipeline(pe, ESTEPS, EU, stages if l == 3 else stages[::-1])

                @block.scalar
                def _(act):
                    A = nc.scalar
                    if l == 3:
                        act.wait_ge(neg_max, 1)
                        A.activation(rel[:, 4:7], rel[:, 0:3], ACT.Exp, bias=rel[:, 3:4]).then_inc(exped, 1)

                    def evac(st):
                        st.freed(act, prod, ER, per)
                        st.ready(act, tr_s)
                        A.copy(xsT[:, st.slot(ER)], ps_s[:, :, 0:P]).then_inc(ev_s, 1)
                        if l == 1:
                            st.ready(act, tr_e)
                            A.copy(eaT[:, st.slot(ER)], ps_e[:, :, 0:P]).then_inc(ev_e, 1)

                    def use(st):
                        slot = st.slot(ER)
                        if l == 0:
                            st.freed(act, vec_done0, ER, 2)
                        if l != 0:
                            st.freed(act, vec_done, ER, nv)
                        if l == 3:
                            st.freed(act, scored, ER, 3)
                        for k, m, h in units(st):
                            tiles = bass.ds(st.j * G + k, m)
                            act.wait_ge(prod, st.j * per + k // m + 1)
                            if l == 0:
                                A.activation(keep[:, tiles, :], h[:, :, 0:D], ACT.Copy)
                                i = A.activation(t1[:, slot, k:k + m, :], h[:, :, D:2 * D], ACT.Copy)
                            if l == 1:
                                i = A.activation(t1[:, slot, k:k + m, :], h[:, :, 0:D], ACT.Sigmoid)
                            if l == 2:
                                A.activation(keep[:, tiles, :], h[:, :, D:2 * D], ACT.Copy)
                                i = A.activation(t1[:, slot, k:k + m, :], h[:, :, 2 * D:3 * D], ACT.Copy)
                            if l == 3:
                                A.activation(raw[:, slot, k:k + 1, :], h[:, :, 384:408], ACT.Copy)
                                i = A.activation(t2[:, slot, k, :], h[:, 0, 0:D], ACT.Identity, scale=mk[:, bass.ds(st.j * G + k, 1), 0])
                            i.then_inc(act_done, 1)

                    pipeline(act, ESTEPS, EU, [(0, evac), (1, use)])

                @block.vector
                def _(dve):
                    V, ch = nc.vector, Chain(dve, own)

                    def gather_columns(st):
                        self.columns(dve, st, [(ixs, self.src_i), (ixd, self.dst_i)], got, 32 * G, copied)

                    for j in range(XR):
                        gather_columns(Step(0, j, EU))
                    if fill:
                        V.memset(zero[:], 0.0).then_inc(fills, 1)
                        V.memset(zero3[:, :, 0:D], 0.0).then_inc(fills, 1)
                        V.memset(zero3[:, :, D:W3], 1.0).then_inc(fills, 1)
                    dve.wait_ge(weights, 16 * len(W))
                    if l == 1:
                        ch(V.tensor_tensor(b3[:, 0, :], b3[:, 0, :], b3[:, 1, :], ALU.add))
                        ch(V.tensor_tensor(brow[:, 0:D], b3[:, 0, :], b3[:, 2, :], ALU.add),
                           V.memset(ro[:, XR - 1, G - 1, :], 0.0))
                    if l == 3:
                        w3f, heads = w3[:].rearrange("i r o -> i (r o)"), lambda t: t[:].rearrange("i (q c) -> i q c", c=32)
                        V.tensor_reduce(rel[:, 3:4], rel[:, 0:3], AX.X, ALU.max, negate=True).then_inc(neg_max, 1)
                        ch(V.tensor_tensor(pr3[:], w3f, att_s[:], ALU.mult))
                        ch(V.tensor_reduce(ws[:, 384:396], heads(pr3), AX.X, ALU.add))
                        ch(V.tensor_tensor(pr3[:], w3f, att_d[:], ALU.mult))
                        dve.wait_ge(exped, 1)
                        ch(V.tensor_reduce(wd[:, 0:12], heads(pr3), AX.X, ALU.add),
                           V.tensor_reduce(rel[:, 7:8], rel[:, 4:7], AX.X, ALU.add),
                           V.memset(ws[:, 396:408], 0.0))
                        ch(V.tensor_tensor(wd[:, 12:24], wd[:, 0:12], ws[:, 384:396], ALU.add),
                           V.reciprocal(rel[:, 8:9], rel[:, 7:8]))
                        ch(V.tensor_scalar(rel_w[:], rel[:, 4:7], rel[:, 8:9], None, ALU.mult))
                        ch(*[V.tensor_scalar(ws[:, D * r:D * r + D], w3[:, r, :], rel_w[:, r:r + 1], None, ALU.mult)
                             for r in range(3)])
                        ch(V.tensor_copy(w3s[:], ws[:, 0:3 * D]))
                    if l != 1:
                        ch(V.memset(ends[:], -BIG))
                    V.memset(t2[:, 0, 0, 0:1], 0.0).then_inc(weights_done, 1)
                    dve.wait_ge(weights_done, 1)

                    def evac(st):
                        st.freed(dve, prod, ER, per)
                        st.ready(dve, tr_d)
                        V.tensor_copy(xdT[:, st.slot(ER)], ps_d[:, :, 0:P]).then_inc(ev_d, 1)

                    def heads16(st):
                        V.tensor_reduce(S[:, bass.ds(st.j * G, G), :], t2[:, st.slot(ER)].rearrange("p k (h c) -> p k h c", c=16),
                                        AX.X, ALU.add).then_inc(reduced, 1)

                    def use0(st):
                        st.ready(dve, act_done, per)
                        st.freed(dve, reduced, ER)
                        slot = st.slot(ER)
                        V.scalar_tensor_tensor(out=t2[:, slot], in0=t1[:, slot], scalar=0.2, in1=t1[:, slot],
                                               op0=ALU.mult, op1=ALU.max).then_inc(vec_done0, 1)
                        dve.wait_ge(vec_done0, st.j * 2 + 1)
                        V.tensor_tensor(t2[:, slot], t2[:, slot], over_tiles(attn_row[:]), ALU.mult).then_inc(vec_done0, 1)
                        st.ready(dve, vec_done0, 2)
                        heads16(st)

                    def use1(st):
                        slot = st.slot(ER)
                        st.freed(dve, summed, ER, G)
                        for k, m, h in units(st):
                            dve.wait_ge(act_done, st.j * per + k // m + 1)
                            V.tensor_tensor(t2[:, slot, k:k + m, :], h[:, :, D:2 * D], t1[:, slot, k:k + m, :], ALU.mult).then_inc(vec_done, 1)
                        st.ready(dve, vec_done, nv)
                        self.running_sum(dve, st, ro, t2, slot, put, summed)

                    def use2(st):
                        slot = st.slot(ER)
                        st.freed(dve, reduced, ER)
                        for k, m, h in units(st):
                            dve.wait_ge(act_done, st.j * per + k // m + 1)
                            V.tensor_tensor(t2[:, slot, k, :], h[:, 0, 0:D], t1[:, slot, k, :], ALU.mult).then_inc(vec_done, 1)
                        st.ready(dve, vec_done, nv)
                        heads16(st)

                    def use3(st):
                        slot = st.slot(ER)
                        st.freed(dve, vec_done, 1, nv)
                        for r in range(1, 3):
                            for k, m, h in units(st):
                                dve.wait_ge(*((act_done, st.j * per + k + 1) if r == 1 else (vec_done, st.j * nv + k + 1)))
                                own_rel, hr = mk[:, bass.ds(st.j * G + k, 1), r], h[:, 0, D * r:D * r + D]
                                to = t1[:, slot, k, :] if r == 1 else keep[:, bass.ds(st.j * G + k, 1), :].rearrange("p a d -> p (a d)")
                                V.scalar_tensor_tensor(out=to, in0=hr, scalar=own_rel, in1=(t2 if r == 1 else t1)[:, slot, k, :],
                                                       op0=ALU.mult, op1=ALU.add).then_inc(vec_done, 1)

                    def leaky(st):
                        st.ready(dve, act_done, per)
                        st.freed(dve, scored, ER, 3)
                        V.scalar_tensor_tensor(out=relu[:, st.slot(ER)], in0=raw[:, st.slot(ER)], scalar=0.2, in1=raw[:, st.slot(ER)],
                                               op0=ALU.mult, op1=ALU.max).then_inc(scored, 1)

                    def mask(st):
                        slot, tiles = st.slot(ER), bass.ds(st.j * G, G)
                        wide = lambda m: m[:, tiles, :].unsqueeze(3).to_broadcast([P, G, 3, 4])
                        by_rel = lambda v: v.rearrange("p k (r h) -> p k r h", h=4)
                        dve.wait_ge(scored, st.j * 3 + 1)
                        V.tensor_tensor(by_rel(masked[:, slot]), by_rel(relu[:, slot, :, 0:12]), wide(mk), ALU.mult).then_inc(scored, 1)
                        V.tensor_copy(SS[:, tiles, :], relu[:, slot, :, 12:24])
                        dve.wait_ge(scored, st.j * 3 + 2)
                        V.tensor_tensor(by_rel(S[:, tiles, :]), by_rel(masked[:, slot]), wide(nm), ALU.add).then_inc(scored, 1)

                    def end_maxima(st):
                        tiles = bass.ds(st.j * G, G)
                        st.ready(dve, *((scored, 3) if l == 3 else (reduced, 1)))
                        st.freed(dve, ends_done, 1, 4)
                        for d in range(2):
                            V.tensor_tensor(segs[:, d], S[:, tiles, :], self.pen_ends[:, d, tiles].unsqueeze(2).to_broadcast([P, G, H]),
                                            ALU.add).then_inc(ends_done, 1)
                        dve.wait_ge(ends_done, st.j * 4 + 2)
                        V.tensor_reduce(best[:], segs[:].rearrange("p d t h -> p d h t"), AX.X, ALU.max).then_inc(ends_done, 1)
                        dve.wait_ge(ends_done, st.j * 4 + 3)
                        V.tensor_tensor(ends[:], ends[:], best[:], ALU.max).then_inc(ends_done, 1)

                    stages = [(0, lambda st: gather_columns(st) if st.has(XR) else None)]
                    if l == 1:
                        stages.append((2, lambda st: self.columns(dve, st, [(pcols, self.put_i)], put, 16 * G, pcopied)))
                    stages += [(2, evac), (3, (use0, use1, use2, use3)[l])]
                    if l == 3:
                        stages[-1:] = [(3, leaky), stages[-1], (3, mask)]
                    if l != 1:
                        stages.append((4, end_maxima))
                    pipeline(dve, ESTEPS, EU, stages)
            if l == 1:
                self.carry_fix(l, ro, self.agg, D)

    def softmax(self, l, H, S, F, tops, SS=None, scale=1.0, eps=0.0):
        nc, pre = self.nc, f"s{l}_"
        with ExitStack() as ctx:
            sb = lambda name, shape: self.sb(ctx, pre + name, shape)
            B = sb("B", [P, T, H])
            carry = sb("carry", [P, 2, H])
            ends, passed = sb("ends", [H, 2, P]), sb("passed", [H, 2, P + 1])
            ps_rows = self.ps(ctx, pre + "ps_rows", [H, 2, 128])
            ps_c, ps_d = self.ps(ctx, pre + "ps_c", [P, 2, 16]), self.ps(ctx, pre + "ps_d", [P, 2, 16])
            own, turned, linked, returned, maxed, exped, summed, carried = (self.sem(pre + n) for n in (
                "own", "turned", "linked", "returned", "maxed", "exped", "summed", "carried"))
            block = ctx.enter_context(nc.Block())

            @block.tensor
            def _(pe):
                idp, idh, turn = self.ident[0:P, 0:P], self.ident[0:H, 0:H], nc.tensor.transpose
                turn(ps_rows[:, 0, 0:P], tops[:, 0, :], idp)
                turn(ps_rows[:, 1, 0:P], tops[:, 1, :], idp).then_inc(turned, 1)
                pe.wait_ge(linked, 1)
                turn(ps_c[:, 0, 0:H], passed[:, 0, 0:P], idh)
                turn(ps_c[:, 1, 0:H], passed[:, 1, 1:P + 1], idh).then_inc(returned, 1)
                pe.wait_ge(summed, 1)
                nc.tensor.matmul(ps_d[:, 0, 0:H], self.carry_f[:], F[:, T - 1, :], start=True, stop=True, skip_group_check=True)
                nc.tensor.matmul(ps_d[:, 1, 0:H], self.carry_b[:], B[:, 0, :], start=True, stop=True, skip_group_check=True).then_inc(carried, 1)

            @block.scalar
            def _(act):
                act.wait_ge(maxed, 1)
                nc.scalar.activation(S[:], S[:], ACT.Exp, scale=scale).then_inc(exped, 1)
                if l == 3:
                    nc.scalar.activation(SS[:], SS[:], ACT.Exp).then_inc(exped, 1)

            @block.vector
            def _(dve):
                V, ch = nc.vector, Chain(dve, own)

                def scans(mult, combine, prev, nxt, init_f, init_b):
                    ops = []
                    for h in range(H):
                        i_f = init_f if isinstance(init_f, float) else init_f[:, h:h + 1]
                        i_b = init_b if isinstance(init_b, float) else init_b[:, h:h + 1]
                        ops.append(V.tensor_tensor_scan(F[:, :, h], prev[:], S[:, :, h], i_f, mult, combine))
                        ops.append(V.tensor_tensor_scan(B[:, ::-1, h], nxt[:, ::-1], S[:, ::-1, h], i_b, mult, combine))
                    ch(*ops)

                ch(V.memset(passed[:], -BIG))
                dve.wait_ge(turned, 1)
                ch(V.tensor_tensor(ends[:], ps_rows[:, :, 0:P], self.row_pens[0:H, 0:2, :], ALU.add))
                V.tensor_tensor_scan(passed[:, 0, 1:P + 1], self.row_pens[0:H, 2, :], ends[:, 0, :], -BIG, ALU.add, ALU.max)
                V.tensor_tensor_scan(passed[:, 1, P - 1::-1], self.row_pens[0:H, 3, ::-1], ends[:, 1, ::-1], -BIG, ALU.add, ALU.max).then_inc(linked, 1)
                dve.wait_ge(returned, 1)
                ch(V.tensor_copy(carry[:], ps_c[:, :, 0:H]))
                cf, cb = carry[:, 0, :], carry[:, 1, :]
                scans(ALU.add, ALU.max, self.pen_prev, self.pen_next, cf, cb)
                ch(V.tensor_tensor(F[:], F[:], B[:], ALU.max))
                if l == 3:
                    ch(V.tensor_tensor(F[:], F[:], SS[:], ALU.max))
                    ch(V.tensor_tensor(SS[:], SS[:], F[:], ALU.subtract))
                V.tensor_tensor(S[:], S[:], F[:], ALU.subtract).then_inc(maxed, 1)
                dve.wait_ge(exped, 1)
                scans(ALU.mult, ALU.add, self.same_prev, self.same_next, 0.0, 0.0)
                V.memset(ends[:, 0, 0:1], 0.0).then_inc(summed, 1)
                dve.wait_ge(summed, 1)
                dve.wait_ge(carried, 1)
                ch(V.tensor_copy(carry[:], ps_d[:, :, 0:H]))
                scans(ALU.mult, ALU.add, self.same_prev, self.same_next, cf, cb)
                ch(V.tensor_tensor(F[:], F[:], B[:], ALU.add))
                ch(V.scalar_tensor_tensor(out=F[:], in0=F[:], scalar=eps, in1=S[:], op0=ALU.add, op1=ALU.subtract))
                if l == 3:
                    dve.wait_ge(exped, 2)
                    ch(V.tensor_tensor(F[:], F[:], SS[:], ALU.add))

    def message_pass(self, l, keep, S, F, H, dst, width, SS=None):
        nc, pre = self.nc, f"m{l}_"
        HV = 4 if l == 3 else H
        with ExitStack() as ctx:
            sb = lambda name, shape, dt=F32: self.sb(ctx, pre + name, shape, dt)
            ro, msg = sb("ro", [P, XR, G, width]), sb("msg", [P, ER, G, D])
            inv, weight, sel = sb("inv", [P, XR, G, H]), sb("weight", [P, XR, G, H]), sb("sel", [P, ER, G, HV])
            pcols = sb("pcols", [P, XR, G], I32)
            inverted, weighted, selected, made, summed, copied, go, blank = (self.sem(pre + n) for n in (
                "inverted", "weighted", "selected", "made", "summed", "copied", "go", "blank"))
            put = [self.sem(pre + f"put{k}") for k in range(XR)]
            with ExitStack() as c2:
                block = c2.enter_context(nc.Block())

                @block.vector
                def _(dve):
                    V = nc.vector
                    V.memset(ro[:, XR - 1, G - 1, 0:D], 0.0).then_inc(blank, 1)
                    dve.wait_ge(blank, 1)

                    def invert(st):
                        st.freed(dve, made, XR)
                        V.reciprocal(inv[:, st.slot(XR)], F[:, bass.ds(st.j * G, G), :]).then_inc(inverted, 1)

                    def weigh(st):
                        st.ready(dve, inverted)
                        st.freed(dve, made, XR)
                        V.tensor_tensor(weight[:, st.slot(XR)], S[:, bass.ds(st.j * G, G), :], inv[:, st.slot(XR)], ALU.mult).then_inc(weighted, 1)

                    def select(st):
                        st.ready(dve, weighted)
                        st.freed(dve, made, ER)
                        V.tensor_reduce(sel[:, st.slot(ER)], weight[:, st.slot(XR)].rearrange("p t (r h) -> p t h r", h=4),
                                        AX.X, ALU.add).then_inc(selected, 1)

                    def make(st):
                        tiles = bass.ds(st.j * G, G)
                        w = sel[:, st.slot(ER)] if l == 3 else weight[:, st.slot(XR)]
                        st.ready(dve, selected if l == 3 else weighted)
                        st.freed(dve, summed, ER, G)
                        if l == 3:
                            st.sent(dve, put, 16 * G)
                            V.tensor_tensor(ro[:, st.slot(XR), :, D:W3], SS[:, tiles, :], inv[:, st.slot(XR)], ALU.mult)
                        V.tensor_tensor(msg[:, st.slot(ER)].rearrange("p k (h c) -> p k h c", h=HV),
                                        keep[:, tiles, :].rearrange("p k (h c) -> p k h c", h=HV),
                                        w.unsqueeze(3).to_broadcast([P, G, HV, D // HV]), ALU.mult).then_inc(made, 1)

                    def add(st):
                        st.ready(dve, made)
                        self.running_sum(dve, st, ro, msg, st.slot(ER), put, summed)

                    columns = lambda st: self.columns(dve, st, [(pcols, self.put_i)], put, 16 * G, copied)
                    pipeline(dve, ESTEPS, EU, [(2, columns), (4, add), (3, make)] + [(2, select)] * (l == 3) + [(1, weigh), (0, invert)])

                @block.gpsimd
                def _(pool):
                    pipeline(pool, ESTEPS, EU, [(0, lambda st: self.scatter(pool, st, pcols, ro, dst, put, copied, go, [(summed, G)]))])
                    for k in range(XR):
                        pool.wait_ge(put[k], 16 * G * (ESTEPS // XR))
            self.carry_fix(l, ro, dst, width)

    def attention_layer(self, l):
        H = {0: 8, 2: 8, 3: 12}[l]
        nc = self.nc
        with ExitStack() as ctx:
            keep = self.sb(ctx, f"keep{l}", [P, T, D])
            S = self.sb(ctx, f"S{l}", [P, T, H])
            ends = self.sb(ctx, f"ends{l}", [P, 2, H])
            if l != 3:
                self.edge_pass(l, keep, S, ends=ends)
                F = self.sb(ctx, f"F{l}", [P, T, H])
                self.softmax(l, H, S, F, ends, scale=(1.0, None, 0.25)[l], eps=(1e-8, None, 1e-16)[l])
                self.message_pass(l, keep, S, F, H, self.agg, D)
                return
            SS = self.sb(ctx, "SS3", [P, T, H])
            mk = self.sb(ctx, "mk3", [P, T, 3])
            nm = self.sb(ctx, "nm3", [P, T, 3])
            with ExitStack() as c2:
                ty = self.sb(c2, "ty", [P, T])
                own = self.sem("r_own")
                block = c2.enter_context(nc.Block())

                @block.vector
                def _(dve):
                    ch = Chain(dve, own)
                    ch(nc.vector.tensor_copy(ty[:], self.type_i[:]))
                    ch(*[nc.vector.tensor_scalar(mk[:, :, r], ty[:], float(r), None, ALU.is_equal) for r in range(3)])
                    ch(nc.vector.tensor_scalar(nm[:], mk[:], -1.0, NEG, ALU.add, ALU.mult))
            self.edge_pass(3, keep, S, SS, ends, mk, nm, self.w3s, self.rel_w)
            F = self.sb(ctx, "F3", [P, T, H])
            self.softmax(3, H, S, F, ends, SS)
            self.message_pass(3, keep, S, F, H, self.agg3, W3, SS)

    def node_io(self, ctx, pre, l, agg, width):
        b, ring = self, NR
        x, s = b.sb(ctx, pre + "x", [P + 1, ring, G, D]), b.sb(ctx, pre + "s", [P + 1, ring, G, width])
        got = [b.sem(pre + f"got{k}") for k in range(ring // 2)]
        put = [b.sem(pre + f"put{k}") for k in range(ring // 2)]
        x_v, s_v, o_v = (t.rearrange("(p n) d -> p n d", p=P) for t in (b.x[l], agg, b.x[l + 1]))

        tiles = lambda t, slot: t.rearrange("p r g d -> p (r g) d")[:, slot * G:(slot + 2) * G]

        def load(sp, st, used):
            if st.q % 2:
                return
            slot, nodes = st.slot(ring), bass.ds(st.j * G, 2 * G)
            if st.has(ring):
                for read, per in used:
                    sp.wait_ge(read, (st.j + 2 - ring) * per)
            load_rows(sp, tiles(x, slot), x_v[:, nodes, :], got[slot // 2])
            load_rows(sp, tiles(s, slot), s_v[:, nodes, :], got[slot // 2])

        def store(sp, st, o, ln):
            if st.q % 2:
                ln.output_ready(sp, st)
                slot = st.slot(ring) - 1
                load_rows(sp, o_v[:, bass.ds(st.j * G - G, 2 * G), :], tiles(o, slot), put[slot // 2])

        def finish(sp):
            for sem in put:
                sp.wait_ge(sem, 32 * (NSTEPS // ring))

        return x, s, got, put, load, store, finish

    def bias_row(self, eng, loaded, ring, v):
        n = ring.shape[1] * G
        eng.dma_start(ring[P:P + 1].rearrange("p r g d -> p (r g) d"), rows_of(v, n).unsqueeze(0)).then_inc(loaded, 16)

    def load_consts(self, eng, loaded, pairs):
        for to, of in pairs:
            eng.dma_start(to, of).then_inc(loaded, 16)

    def nodes_simple(self, l):
        nc, a, pre, R = self.nc, self.a, f"n{l}_", NR
        with ExitStack() as ctx:
            sb = lambda name, shape: self.sb(ctx, pre + name, shape)
            x, s, got, put, load, store, finish = self.node_io(ctx, pre, l, self.agg, D)
            w, rows = sb("w", [D, D]), sb("rows", [P, 2, D])
            aT, y1, t, u, g, o = sb("aT", [128, 2, G, P]), *(sb(n, [P, MR, G, D]) for n in ("y1", "t", "u", "g")), sb("o", [P, R, G, D])
            ps_t = [self.ps(ctx, pre + f"ps_t{k}", [128, G, 128]) for k in range(2)]
            ps_o = [self.ps(ctx, pre + f"ps_o{k}", [128, G, 128]) for k in range(MR)]
            loaded, tr, ev, mm, side, usum, scaled, go = (self.sem(pre + n) for n in
                                                          ("loaded", "tr", "ev", "mm", "side", "usum", "scaled", "go"))
            ln1 = LayerNorm(self, ctx, pre + "ln1") if l == 0 else None
            ln2 = LayerNorm(self, ctx, pre + "ln2", shared=2 if l == 0 else 0)
            W, bias = ("L0_gnn_W_out", "L0_gnn_b_out") if l == 0 else ("L1_gnn_Wres", "L1_gnn_bres")
            n_const = 16 * (4 if l == 0 else 2)
            fed, other = (s, x) if l == 0 else (x, s)
            block = ctx.enter_context(nc.Block())

            @block.sync
            def _(sp):
                pipeline(sp, NSTEPS, R, [(0, lambda st: load(sp, st, [(mm, 1), (side if l == 0 else usum, 1)])),
                                         (12 if l == 0 else 8, lambda st: store(sp, st, o, ln2))])
                finish(sp)

            @block.tensor
            def _(pe):
                def transposes(st):
                    st.pair_arrived(pe, got)
                    st.freed(pe, ev, 2)
                    for k in range(G):
                        i = nc.tensor.transpose(ps_t[st.slot(2)][:, k, 0:P], fed[0:P, st.slot(R), k, :], self.ident[0:P, 0:P])
                    i.then_inc(tr, 1)

                def products(st):
                    if st.peeled and st.j == 0:
                        pe.wait_ge(loaded, n_const)
                    st.ready(pe, ev)
                    st.freed(pe, ln1.scaled if l == 0 else usum, MR)
                    bank = ps_o[st.slot(MR)]
                    nc.tensor.matmul(bank[0:P], self.ident_b[:], other[:, st.slot(R)], start=True, stop=False, skip_group_check=True)
                    for k in range(G):
                        i = nc.tensor.matmul(bank[0:P, k, :], aT[:, st.slot(2), k, :], w[:],
                                             start=False, stop=(k == G - 1), skip_group_check=True)
                    i.then_inc(mm, 1)

                pipeline(pe, NSTEPS, R, [(0, transposes), (1, products)])

            @block.scalar
            def _(act):
                def evac(st):
                    st.ready(act, tr)
                    st.freed(act, mm, 2)
                    nc.scalar.copy(aT[:, st.slot(2)], ps_t[st.slot(2)][:, :, 0:P]).then_inc(ev, 1)

                self.load_consts(act, loaded, [(w[:], a[W])])
                self.bias_row(act, loaded, other, a[bias])
                if l == 0:
                    self.load_consts(act, loaded, [(rows[:, 0, :], rows_of(a["L0_gnn_gamma"], P)), (rows[:, 1, :], rows_of(a["L0_gnn_beta"], P))])

                def scale1(st):
                    st.freed(act, scaled, MR)
                    ln1.scale(act, st, ps_o[st.slot(MR)][0:P], u[:, st.slot(MR)])

                def scale2(st):
                    st.pair_sent(act, put)
                    ln2.scale(act, st, t[:, st.slot(MR)], o[:, st.slot(R)])

                if l == 0:
                    stages = [(3, lambda st: ln1.root(act, st)), (7, lambda st: ln2.root(act, st)), (0, evac), (4, scale1), (8, scale2)]
                else:
                    stages = [(3, lambda st: ln2.root(act, st)), (0, evac), (4, scale2)]
                pipeline(act, NSTEPS, R, stages)

            if l == 0:
                @block.gpsimd
                def _(pool):
                    def scale_too(st):
                        wait_pool(pool, go, lambda: st.ready(pool, ln2.offset))
                        if st.has(R):
                            wait_pool(pool, go, lambda: st.pair_sent(pool, put))
                        ln2.scale_shared(st, t[:, st.slot(MR)], o[:, st.slot(R)])

                    def x_beta(st):
                        wait_pool(pool, go, lambda: st.pair_arrived(pool, got))
                        if st.has(MR):
                            wait_pool(pool, go, lambda: st.freed(pool, usum, MR))
                        nc.gpsimd.tensor_tensor(y1[:, st.slot(MR)], x[0:P, st.slot(R)], over_tiles(rows[:, 1, :]), ALU.add).then_inc(side, 1)

                    def gamma(st):
                        wait_pool(pool, go, lambda: st.ready(pool, ln1.scaled))
                        if st.has(MR):
                            wait_pool(pool, go, lambda: st.freed(pool, usum, MR))
                        nc.gpsimd.tensor_tensor(g[:, st.slot(MR)], u[:, st.slot(MR)], over_tiles(rows[:, 0, :]), ALU.mult).then_inc(scaled, 1)

                    wait_pool(pool, go, lambda: pool.wait_ge(loaded, n_const))
                    pipeline(pool, NSTEPS, R, [(2, x_beta), (5, gamma), (8, scale_too)])

            @block.vector
            def _(dve):
                V = nc.vector

                def stats1(st):
                    st.ready(dve, mm)
                    ln1.stats(dve, st, ps_o[st.slot(MR)][0:P])

                def add2(st):
                    slot = st.slot(MR)
                    ln2.output_read_from(dve, st, MR)
                    if l == 0:
                        st.ready(dve, scaled)
                        st.ready(dve, side)
                        V.tensor_tensor(t[:, slot], g[:, slot], y1[:, slot], ALU.add).then_inc(usum, 1)
                    else:
                        st.ready(dve, mm)
                        V.scalar_tensor_tensor(out=t[:, slot], in0=ps_o[st.slot(MR)][0:P], scalar=0.0, in1=x[0:P, st.slot(R)],
                                               op0=ALU.max, op1=ALU.add).then_inc(usum, 1)

                def stats2(st):
                    st.ready(dve, usum)
                    ln2.stats(dve, st, t[:, st.slot(MR)])

                if l == 0:
                    stages = [(6, add2), (2, stats1), (7, lambda st: ln2.inverse(dve, st)), (3, lambda st: ln1.inverse(dve, st)), (6, stats2),
                              (7, lambda st: ln2.negated(dve, st)), (3, lambda st: ln1.negated(dve, st)),
                              (2, lambda st: ln1.aggregate(dve, st)), (6, lambda st: ln2.aggregate(dve, st))]
                else:
                    stages = [(2, add2), (3, lambda st: ln2.inverse(dve, st)), (2, stats2),
                              (3, lambda st: ln2.negated(dve, st)), (2, lambda st: ln2.aggregate(dve, st))]
                pipeline(dve, NSTEPS, R, stages)

    def nodes_transformer(self):
        nc, a, pre, l, R = self.nc, self.a, "n2_", 2, NR
        F = 4
        with ExitStack() as ctx:
            sb = lambda name, ring, rows=P, cols=D: self.sb(ctx, pre + name, [rows, ring, G, cols])
            x, s, got, put, load, store, finish = self.node_io(ctx, pre, l, self.agg, D)
            wo, w1, w2 = (self.sb(ctx, pre + n, shape) for n, shape in (("wo", [D, D]), ("w1", [D, F * D]), ("w2", [D, F, D])))
            rows, b1 = self.sb(ctx, pre + "rows", [P, 6, D]), self.sb(ctx, pre + "b1", [D, F])
            aT, hT = sb("aT", 2, 128, P), sb("hT", 2, 128, P)
            hid = self.sb(ctx, pre + "hid", [128, 2, F, G, P])
            y0, n1, h0, h, n2, g2 = (sb(n, 2) for n in ("y0", "n1", "h0", "h", "n2", "g2"))
            t, y1, v, wv = (sb(n, MR) for n in ("t", "y1", "v", "wv"))
            y2, o = sb("y2", R), sb("o", R)
            ps_t, ps_h, ps_o, ps_v = (self.ps(ctx, pre + n, [128, G, 128]) for n in ("ps_t", "ps_h", "ps_o", "ps_v"))
            ps_f = [self.ps(ctx, pre + f"ps_f{k}", [128, G, P]) for k in range(F)]
            loaded, tr, ev, mm, side, tsum = (self.sem(pre + n) for n in ("loaded", "tr", "ev", "mm", "side", "tsum"))
            hg, hb, trh, evh, f1, relu, f2, side2, vsum, g2d, side3, wsum, go = (self.sem(pre + n) for n in (
                "hg", "hb", "trh", "evh", "f1", "relu", "f2", "side2", "vsum", "g2d", "side3", "wsum", "go"))
            ln1 = LayerNorm(self, ctx, pre + "ln1", on_vector=True)
            ln2, ln3 = LayerNorm(self, ctx, pre + "ln2"), LayerNorm(self, ctx, pre + "ln3")
            vecs = ("bo", "ln1_g", "ln1_b", "b2", "ln2_g", "ln2_b")
            consts = [(wo[:], a["L2_gnn_Wo"]), (w1[:], a["L2_gnn_W1"]), (w2[:], a["L2_gnn_W2"].rearrange("(f i) o -> i f o", f=F))]
            consts += [(rows[:, k, :], rows_of(a["L2_gnn_" + n], P)) for k, n in enumerate(vecs)]
            n_const = 16 * (len(consts) + 1)
            row = lambda n: over_tiles(rows[:, vecs.index(n), :])
            block = ctx.enter_context(nc.Block())

            @block.sync
            def _(sp):
                pipeline(sp, NSTEPS, R, [(0, lambda st: load(sp, st, [(tr, 1), (side, 1), (side3, 1)])),
                                         (19, lambda st: store(sp, st, o, ln3))])
                finish(sp)

            @block.tensor
            def _(pe):
                def turn(bank, tiles, done):
                    for k in range(G):
                        i = nc.tensor.transpose(bank[:, k, 0:P], tiles[:, k, :], self.ident[0:P, 0:P])
                    i.then_inc(done, 1)

                def turn_sums(st):
                    st.pair_arrived(pe, got)
                    st.freed(pe, ev, 1)
                    turn(ps_t, s[0:P, st.slot(R)], tr)

                def out_product(st):
                    if st.peeled and st.j == 0:
                        pe.wait_ge(loaded, n_const)
                    st.ready(pe, ev)
                    st.freed(pe, tsum, 1)
                    for k in range(G):
                        i = nc.tensor.matmul(ps_o[0:P, k, :], aT[:, st.slot(2), k, :], wo[:], start=True, stop=True, skip_group_check=True)
                    i.then_inc(mm, 1)

                def turn_h(st):
                    st.ready(pe, hb)
                    st.freed(pe, evh, 1)
                    turn(ps_h, h[:, st.slot(2)], trh)

                def up(st):
                    st.ready(pe, evh)
                    for f in range(F):
                        if st.has(1):
                            pe.wait_ge(relu, st.j * F - (F - 1 - f))
                        nc.tensor.matmul(ps_f[f][:], w1[:, f * D:f * D + D], hT[:, st.slot(2)], start=True, stop=True).then_inc(f1, 1)

                def down(st):
                    st.ready(pe, relu, F)
                    st.freed(pe, vsum, 1)
                    for k in range(G):
                        for f in range(F):
                            i = nc.tensor.matmul(ps_v[0:P, k, :], hid[:, st.slot(2), f, k, :], w2[:, f, :],
                                                 start=(f == 0), stop=(f == F - 1), skip_group_check=True)
                    i.then_inc(f2, 1)

                pipeline(pe, NSTEPS, R, [(0, turn_sums), (7, turn_h), (9, down), (1, out_product), (8, up)])

            @block.scalar
            def _(act):
                def evac(st):
                    st.ready(act, tr)
                    st.freed(act, mm, 2)
                    nc.scalar.copy(aT[:, st.slot(2)], ps_t[:, :, 0:P]).then_inc(ev, 1)

                self.load_consts(act, loaded, consts)
                with nc.allow_non_contiguous_dma(reason="512 biases, one a partition and chunk"):
                    act.dma_start(b1[:], a["L2_gnn_b1"].rearrange("(f i) -> i f", f=F)).then_inc(loaded, 16)

                def evac_h(st):
                    st.ready(act, trh)
                    st.freed(act, f1, 2, F)
                    nc.scalar.copy(hT[:, st.slot(2)], ps_h[:, :, 0:P]).then_inc(evh, 1)

                def relus(st):
                    st.freed(act, f2, 2)
                    for f in range(F):
                        act.wait_ge(f1, st.j * F + f + 1)
                        nc.scalar.activation(hid[:, st.slot(2), f], ps_f[f][:], ACT.Relu, bias=b1[:, f:f + 1]).then_inc(relu, 1)

                def scale2(st):
                    st.freed(act, g2d, 2)
                    ln2.scale(act, st, v[:, st.slot(MR)], n2[:, st.slot(2)])

                def scale3(st):
                    st.pair_sent(act, put)
                    ln3.scale(act, st, wv[:, st.slot(MR)], o[:, st.slot(R)])

                pipeline(act, NSTEPS, R, [(3, lambda st: ln1.root(act, st)), (11, lambda st: ln2.root(act, st)),
                                          (15, lambda st: ln3.root(act, st)), (0, evac), (7, evac_h),
                                          (12, scale2), (16, scale3), (8, relus)])

            @block.gpsimd
            def _(pool):
                tt = nc.gpsimd.tensor_tensor

                def x_bo(st):
                    wait_pool(pool, go, lambda: st.pair_arrived(pool, got))
                    if st.has(2):
                        wait_pool(pool, go, lambda: st.freed(pool, tsum, 2))
                    tt(y0[:, st.slot(2)], x[0:P, st.slot(R)], row("bo"), ALU.add).then_inc(side, 1)

                def x_ln2_b(st):
                    if st.has(R):
                        wait_pool(pool, go, lambda: st.freed(pool, wsum, R))
                    tt(y2[:, st.slot(R)], x[0:P, st.slot(R)], row("ln2_b"), ALU.add).then_inc(side3, 1)

                def h_gain(st):
                    wait_pool(pool, go, lambda: st.ready(pool, ln1.scaled))
                    if st.has(2):
                        wait_pool(pool, go, lambda: st.freed(pool, hb, 2))
                    tt(h0[:, st.slot(2)], n1[:, st.slot(2)], row("ln1_g"), ALU.mult).then_inc(hg, 1)

                def h_bias(st):
                    wait_pool(pool, go, lambda: st.ready(pool, hg))
                    if st.has(2):
                        wait_pool(pool, go, lambda: st.freed(pool, trh, 2))
                        wait_pool(pool, go, lambda: st.freed(pool, side2, 2))
                    tt(h[:, st.slot(2)], h0[:, st.slot(2)], row("ln1_b"), ALU.add).then_inc(hb, 1)

                def h_b2(st):
                    wait_pool(pool, go, lambda: st.ready(pool, hb))
                    if st.has(MR):
                        wait_pool(pool, go, lambda: st.freed(pool, vsum, MR))
                    tt(y1[:, st.slot(MR)], h[:, st.slot(2)], row("b2"), ALU.add).then_inc(side2, 1)

                def n2_gain(st):
                    wait_pool(pool, go, lambda: st.ready(pool, ln2.scaled))
                    if st.has(2):
                        wait_pool(pool, go, lambda: st.freed(pool, wsum, 2))
                    tt(g2[:, st.slot(2)], n2[:, st.slot(2)], row("ln2_g"), ALU.mult).then_inc(g2d, 1)

                wait_pool(pool, go, lambda: pool.wait_ge(loaded, n_const))
                pipeline(pool, NSTEPS, R, [(6, h_bias), (5, h_gain), (1, x_bo), (7, h_b2), (6, x_ln2_b), (13, n2_gain)])

            @block.vector
            def _(dve):
                add = nc.vector.tensor_tensor

                def first(st):
                    st.ready(dve, mm)
                    st.ready(dve, side)
                    st.freed(dve, ln1.scaled, MR)
                    add(t[:, st.slot(MR)], ps_o[0:P], y0[:, st.slot(2)], ALU.add).then_inc(tsum, 1)

                def ffn(st):
                    st.ready(dve, f2)
                    st.ready(dve, side2)
                    st.freed(dve, ln2.scaled, MR)
                    add(v[:, st.slot(MR)], ps_v[0:P], y1[:, st.slot(MR)], ALU.add).then_inc(vsum, 1)

                def third(st):
                    st.ready(dve, g2d)
                    st.ready(dve, side3)
                    st.freed(dve, ln3.scaled, MR)
                    add(wv[:, st.slot(MR)], g2[:, st.slot(2)], y2[:, st.slot(R)], ALU.add).then_inc(wsum, 1)

                def stats(ln, summed, of):
                    def fn(st):
                        st.ready(dve, summed)
                        ln.stats(dve, st, of[:, st.slot(MR)])
                    return fn

                def scale1(st):
                    st.freed(dve, hg, 2)
                    ln1.scale(dve, st, t[:, st.slot(MR)], n1[:, st.slot(2)])

                pipeline(dve, NSTEPS, R, [
                    (2, first), (14, third), (10, ffn), (2, stats(ln1, tsum, t)), (14, stats(ln3, wsum, wv)), (10, stats(ln2, vsum, v)),
                    (3, lambda st: ln1.inverse(dve, st)), (11, lambda st: ln2.inverse(dve, st)), (15, lambda st: ln3.inverse(dve, st)),
                    (4, scale1), (11, lambda st: ln2.negated(dve, st)), (15, lambda st: ln3.negated(dve, st)),
                    (2, lambda st: ln1.aggregate(dve, st)), (14, lambda st: ln3.aggregate(dve, st)), (10, lambda st: ln2.aggregate(dve, st))])

    def nodes_relational(self):
        nc, a, pre, l, R = self.nc, self.a, "n3_", 3, NR
        with ExitStack() as ctx:
            sb = lambda name, shape: self.sb(ctx, pre + name, shape)
            x, s, got, put, load, store, finish = self.node_io(ctx, pre, l, self.agg3, W3)
            b3, bias = sb("b3", [P, 3, D]), sb("bias", [P, 2, D])
            xT, m = sb("xT", [128, 2, G, P]), sb("m", [P, 2, G, 3, D])
            r01, r2s, r3 = (sb(n, [P, 2, G, D]) for n in ("r01", "r2s", "r3"))
            u, o = sb("u", [P, MR, G, D]), sb("o", [P, R, G, D])
            ps_t, ps_y = ([self.ps(ctx, pre + f"{n}{k}", [128, G, 128]) for k in range(2)] for n in ("ps_t", "ps_y"))
            ps_o = [self.ps(ctx, pre + f"ps_o{k}", [128, 512]) for k in range(G)]
            loaded, own, biased, tr, ev, mm, added, weighted, part, summed, usum, go = (self.sem(pre + n) for n in (
                "loaded", "own", "biased", "tr", "ev", "mm", "added", "weighted", "part", "summed", "usum", "go"))
            ln = LayerNorm(self, ctx, pre + "ln")
            block = ctx.enter_context(nc.Block())

            @block.sync
            def _(sp):
                pipeline(sp, NSTEPS, R, [(0, lambda st: load(sp, st, [(weighted, G), (added, 1), (part, 1)])),
                                         (11, lambda st: store(sp, st, o, ln))])
                finish(sp)

            @block.tensor
            def _(pe):
                def transposes(st):
                    st.pair_arrived(pe, got)
                    st.freed(pe, ev, 2)
                    for k in range(G):
                        i = nc.tensor.transpose(ps_t[st.slot(2)][:, k, 0:P], x[0:P, st.slot(R), k, :], self.ident[0:P, 0:P])
                    i.then_inc(tr, 1)

                def products(st):
                    st.ready(pe, ev)
                    for k in range(G):
                        if st.has(1):
                            pe.wait_ge(weighted, st.j * G - (G - 1 - k))
                        nc.tensor.matmul(ps_o[k][0:P, 0:3 * D], xT[:, st.slot(2), k, :], self.w3s[:],
                                         start=True, stop=True).then_inc(mm, 1)

                def adds(st):
                    if st.peeled and st.j == 0:
                        pe.wait_ge(loaded, 64)
                    st.freed(pe, usum, 2)
                    nc.tensor.matmul(ps_y[st.slot(2)][0:P], self.ident_b[:], x[:, st.slot(R)], start=True, stop=True).then_inc(added, 1)

                pipeline(pe, NSTEPS, R, [(0, transposes), (3, adds), (1, products)])

            @block.scalar
            def _(act):
                def evac(st):
                    st.ready(act, tr)
                    st.freed(act, mm, 2, G)
                    nc.scalar.copy(xT[:, st.slot(2)], ps_t[st.slot(2)][:, :, 0:P]).then_inc(ev, 1)

                self.load_consts(act, loaded, [(b3[:, r, :], rows_of(a["L3_gnn_bias"][r, :], P)) for r in range(3)])
                act.wait_ge(biased, 1)
                act.dma_start(x[P:P + 1].rearrange("p r g d -> p (r g) d"), over_tiles(bias[0:1, 0, :], R * G)).then_inc(loaded, 16)

                def scale(st):
                    st.pair_sent(act, put)
                    ln.scale(act, st, u[:, st.slot(MR)], o[:, st.slot(R)])

                pipeline(act, NSTEPS, R, [(6, lambda st: ln.root(act, st)), (0, evac), (7, scale)])

            @block.gpsimd
            def _(pool):
                def relations(st):
                    slot, tt = st.slot(2), nc.gpsimd.tensor_tensor
                    wait_pool(pool, go, lambda: st.ready(pool, weighted, G))
                    if st.has(2):
                        wait_pool(pool, go, lambda: st.freed(pool, usum, 2))
                        wait_pool(pool, go, lambda: st.freed(pool, summed, 2))
                    tt(r01[:, slot], m[:, slot, :, 0, :], m[:, slot, :, 1, :], ALU.add)
                    tt(r2s[:, slot], m[:, slot, :, 2, :], s[0:P, st.slot(R), :, 0:D], ALU.add).then_inc(part, 1)
                    wait_pool(pool, go, lambda: st.ready(pool, part))
                    tt(r3[:, slot], r01[:, slot], r2s[:, slot], ALU.add).then_inc(summed, 1)

                pipeline(pool, NSTEPS, R, [(3, relations)])

            @block.vector
            def _(dve):
                V, ch, rw = nc.vector, Chain(dve, own), self.rel_w
                dve.wait_ge(loaded, 48)
                ch(V.tensor_scalar(bias[:, 1, :], b3[:, 0, :], rw[0:P, 0:1], None, ALU.mult))
                ch(V.scalar_tensor_tensor(out=bias[:, 0, :], in0=b3[:, 1, :], scalar=rw[0:P, 1:2], in1=bias[:, 1, :], op0=ALU.mult, op1=ALU.add))
                ch(V.scalar_tensor_tensor(out=bias[:, 1, :], in0=b3[:, 2, :], scalar=rw[0:P, 2:3], in1=bias[:, 0, :], op0=ALU.mult, op1=ALU.add))
                V.tensor_copy(bias[:, 0, :], bias[:, 1, :]).then_inc(biased, 1)

                def weigh(st):
                    st.pair_arrived(dve, got)
                    st.freed(dve, summed, 2)
                    for k in range(G):
                        dve.wait_ge(mm, st.j * G + k + 1)
                        V.tensor_tensor(m[:, st.slot(2), k].rearrange("p r (h c) -> p (r h) c", h=4),
                                        ps_o[k][0:P, 0:3 * D].rearrange("p (q c) -> p q c", c=32),
                                        s[0:P, st.slot(R), k, D:W3].unsqueeze(2).to_broadcast([P, 12, 32]), ALU.mult).then_inc(weighted, 1)

                def total(st):
                    st.ready(dve, added)
                    st.ready(dve, summed)
                    st.freed(dve, ln.scaled, MR)
                    V.tensor_tensor(u[:, st.slot(MR)], ps_y[st.slot(2)][0:P], r3[:, st.slot(2)], ALU.add).then_inc(usum, 1)

                def stats(st):
                    st.ready(dve, usum)
                    ln.stats(dve, st, u[:, st.slot(MR)])

                pipeline(dve, NSTEPS, R, [(2, weigh), (5, lambda st: ln.aggregate(dve, st)), (4, total), (6, lambda st: ln.inverse(dve, st)),
                                          (4, stats), (6, lambda st: ln.negated(dve, st))])

    def run(self, layers=(0, 1, 2, 3)):
        self.order_edges()
        self.graph()
        if 0 in layers:
            self.attention_layer(0)
            self.nodes_simple(0)
            self.recycle()
        if 1 in layers:
            self.edge_pass(1)
            self.nodes_simple(1)
            self.recycle()
        if 2 in layers:
            self.attention_layer(2)
            self.nodes_transformer()
            self.recycle()
        if 3 in layers:
            with ExitStack() as ctx:
                self.w3s = self.sb(ctx, "w3s", [D, 3 * D])
                self.rel_w = self.sb(ctx, "rel_w", [D, 3])
                self.attention_layer(3)
                self.nodes_relational()


def wait_pool(pool, go, wait):
    wait()
    pool.sem_inc(go, 1)


class LayerNorm:

    def __init__(self, b, ctx, name, on_vector=False, shared=0):
        self.b, self.on_vector, self.shared = b, on_vector, shared
        sb = lambda n, shape: b.sb(ctx, name + n, shape)
        self.bn, self.mv = sb("bn", [P, LR, G, 6]), sb("mv", [P, LR, G, 2])
        self.sd, self.rs, self.nb = (sb(n, [P, LR, G]) for n in ("sd", "rs", "nb"))
        self.parts, self.aggr, self.rooted, self.inverted, self.offset, self.scaled, self.go = (
            b.sem(name + n) for n in ("parts", "aggr", "rooted", "inverted", "offset", "scaled", "go"))
        self.scaled_too = b.sem(name + "scaled_too") if shared else None

    def output_ready(self, eng, st):
        st.ready(eng, self.scaled)
        if self.shared:
            st.ready(eng, self.scaled_too)

    def output_read_from(self, eng, st, ring):
        st.freed(eng, self.scaled, ring)
        if self.shared:
            st.freed(eng, self.scaled_too, ring)

    def scale_shared(self, st, x, out):
        slot = st.slot(LR)
        for k in range(G - self.shared, G):
            i = self.b.nc.gpsimd.tensor_scalar(out[:, k, :], x[:, k, :], self.rs[:, slot, k:k + 1], self.nb[:, slot, k:k + 1],
                                               ALU.mult, ALU.add)
        i.then_inc(self.scaled_too, 1)

    def stats(self, dve, st, x):
        st.freed(dve, self.aggr, LR)
        for k in range(G):
            i = self.b.nc.vector.bn_stats(self.bn[:, st.slot(LR), k, :], x[:, k, :])
        i.then_inc(self.parts, 1)

    def aggregate(self, dve, st):
        st.ready(dve, self.parts)
        dve.sem_inc(self.go, 1)
        if st.has(LR):
            st.freed(dve, self.scaled if self.on_vector else self.offset, LR)
            dve.sem_inc(self.go, 1)
            if self.shared:
                st.freed(dve, self.scaled_too, LR)
                dve.sem_inc(self.go, 1)
        for k in range(G):
            i = self.b.nc.vector.bn_aggr(self.mv[:, st.slot(LR), k, :], self.bn[:, st.slot(LR), k, :])
        i.then_inc(self.aggr, 1)

    def root(self, act, st):
        slot = st.slot(LR)
        st.ready(act, self.aggr)
        st.freed(act, self.inverted, LR)
        self.b.nc.scalar.activation(self.sd[:, slot], self.mv[:, slot, :, 1], ACT.Sqrt, bias=self.b.eps[0:P]).then_inc(self.rooted, 1)

    def inverse(self, dve, st):
        st.ready(dve, self.rooted)
        self.output_read_from(dve, st, LR)
        self.b.nc.vector.reciprocal(self.rs[:, st.slot(LR)], self.sd[:, st.slot(LR)]).then_inc(self.inverted, 1)

    def negated(self, dve, st):
        slot = st.slot(LR)
        st.ready(dve, self.inverted)
        self.b.nc.vector.scalar_tensor_tensor(out=self.nb[:, slot], in0=self.mv[:, slot, :, 0], scalar=-1.0, in1=self.rs[:, slot],
                                              op0=ALU.mult, op1=ALU.mult).then_inc(self.offset, 1)

    def scale(self, eng, st, x, out):
        slot = st.slot(LR)
        st.ready(eng, self.inverted if self.on_vector else self.offset)
        for k in range(G - self.shared):
            if self.on_vector:
                i = self.b.nc.vector.tensor_scalar(out[:, k, :], x[:, k, :], self.mv[:, slot, k, 0:1], self.rs[:, slot, k:k + 1],
                                                   ALU.subtract, ALU.mult)
            else:
                i = self.b.nc.scalar.activation(out[:, k, :], x[:, k, :], ACT.Identity, bias=self.nb[:, slot, k:k + 1],
                                                scale=self.rs[:, slot, k:k + 1])
        i.then_inc(self.scaled, 1)


def build(nc, args, out):
    with ExitStack() as top:
        Builder(nc, args, out, top).run()


_INS = ["x", "src", "dst", "edge_attr_128", "edge_type_3", "L0_gnn_W_src", "L0_gnn_W_dst", "L0_gnn_attn", "L0_gnn_W_out",
        "L0_gnn_b_out", "L0_gnn_gamma", "L0_gnn_beta", "L1_gnn_WA", "L1_gnn_bA", "L1_gnn_WB", "L1_gnn_bB", "L1_gnn_WC",
        "L1_gnn_bC", "L1_gnn_WE", "L1_gnn_bE", "L1_gnn_Wres", "L1_gnn_bres", "L2_gnn_Wq", "L2_gnn_bq", "L2_gnn_Wk",
        "L2_gnn_bk", "L2_gnn_Wv", "L2_gnn_bv", "L2_gnn_Wo", "L2_gnn_bo", "L2_gnn_ln1_g", "L2_gnn_ln1_b", "L2_gnn_W1",
        "L2_gnn_b1", "L2_gnn_W2", "L2_gnn_b2", "L2_gnn_ln2_g", "L2_gnn_ln2_b", "L3_gnn_W", "L3_gnn_att_src",
        "L3_gnn_att_dst", "L3_gnn_bias", "L3_gnn_rel_w"]


def kernel(**inputs):
    import concourse.bacc as bacc
    from concourse.bass_utils import run_bass_kernel_spmd

    nc = bacc.Bacc("TRN2", target_bir_lowering=False, num_devices=1)
    arrays, args = {}, {}
    for name in _INS:
        arr = np.ascontiguousarray(inputs[name])
        arrays[f"in_{name}"] = arr
        args[name] = nc.dram_tensor(f"in_{name}", arr.shape, mybir.dt.from_np(arr.dtype), kind="ExternalInput").ap()
    out = nc.dram_tensor("out_x", (N_NODES, D), F32, kind="ExternalOutput").ap()
    build(nc, args, out)
    r = run_bass_kernel_spmd(nc, [arrays], core_ids=[0])
    return r.results[0]["out_x"]
```
